# Optimizing a Trainium2 kernel written in Bass

```python
import numpy as np
import jax
import jax.numpy as jnp

def _softmax(x, axis=-1):
    return jax.nn.softmax(x, axis=axis)

def _gelu(x):
    return jax.nn.gelu(x, approximate=True)

def _silu(x):
    return jax.nn.silu(x)

def _sigmoid(x):
    return jax.nn.sigmoid(x)

def _layernorm(x, axis=-1, eps=1e-05):
    m = jnp.mean(x, axis=axis, keepdims=True)
    v = jnp.var(x, axis=axis, keepdims=True)
    return (x - m) / jnp.sqrt(v + eps)

def _scatter_add(tgt, idx, src, axis=0):
    return tgt.at[idx].add(src)

def _segment_sum(src, seg, n):
    return jax.ops.segment_sum(src, seg, n)
kernel_name = 'mk_early_fusion_d1_tok_img1024_r4_d3165b'

def setup_inputs(seed: int=0):
    np.random.seed(seed)
    _w = jnp.asarray

    def _rec_inputs():
        import jax
        import jax.numpy as jnp
        _rk = jax.random.key(seed)
        x = -0.000125008 + 0.999885 * jax.random.normal(jax.random.fold_in(_rk, 1), (8, 512, 256, 4), jnp.float32)
        txt = -8.03667e-05 + 0.656214 * jax.random.normal(jax.random.fold_in(_rk, 2), (8, 128, 256), jnp.float32)
        return (x, txt)
    x, txt = _rec_inputs()

    def _L0_tok_setup():
        import jax, jax.numpy as jnp
        import numpy as np
        key = jax.random.key(seed)
        k1, k2, k3 = jax.random.split(key, 3)
        B, H, I, O, Dp1 = (4, 512, 256, 256, 4)
        x = jax.random.normal(k1, (B, H, I, Dp1), dtype=jnp.float32)
        weight = 0.1 * jax.random.normal(k2, (O, Dp1), dtype=jnp.float32)
        weighted_sum = 0.1 * jax.random.normal(k3, (O, I), dtype=jnp.float32)
        return {'x': x, 'weight': weight, 'weighted_sum': weighted_sum}
    _L0_tok_all = _L0_tok_setup()
    _L0_tok_in = {k: v for k, v in _L0_tok_all.items() if k in ('weight', 'weighted_sum')}
    del _L0_tok_all

    def _L0_attn_setup():
        import jax, jax.numpy as jnp
        import numpy as np
        B, T, D = (4, 512, 256)
        H, Dh = (16, 64)
        key = jax.random.key(seed)
        ks = jax.random.split(key, 5)
        std_qkv = float(np.sqrt(2.0 / (Dh * D)))
        std_o = float(np.sqrt(2.0 / (D * Dh)))
        return {'x': jax.random.normal(ks[0], (B, T, D), dtype=jnp.float32), 'W_Q': jax.random.normal(ks[1], (H, Dh, D), dtype=jnp.float32) * std_qkv, 'b_Q': jnp.zeros((H, Dh), dtype=jnp.float32), 'W_K': jax.random.normal(ks[2], (H, Dh, D), dtype=jnp.float32) * std_qkv, 'b_K': jnp.zeros((H, Dh), dtype=jnp.float32), 'W_V': jax.random.normal(ks[3], (H, Dh, D), dtype=jnp.float32) * std_qkv, 'b_V': jnp.zeros((H, Dh), dtype=jnp.float32), 'W_O': jax.random.normal(ks[4], (H, D, Dh), dtype=jnp.float32) * std_o, 'b_O': jnp.zeros((D,), dtype=jnp.float32)}
    _L0_attn_all = _L0_attn_setup()
    _L0_attn_in = {k: v for k, v in _L0_attn_all.items() if k in ('W_Q', 'b_Q', 'W_K', 'b_K', 'W_V', 'b_V', 'W_O', 'b_O')}
    del _L0_attn_all

    def _L0_ffn_setup():
        import jax, jax.numpy as jnp
        import numpy as np
        BLOCK = 32
        W_BITS = 4
        ACT_BITS = 16

        def act_qdq(x):
            qmax = 2.0 ** (ACT_BITS - 1) - 1.0
            scale = jnp.maximum(jnp.max(jnp.abs(x)) / qmax, 1e-12)
            return jnp.clip(jnp.round(x / scale), -qmax - 1.0, qmax) * scale

        def fixed_qdq_u16(x):
            scale = 1.0 / 65536.0
            return jnp.clip(jnp.round(x / scale), 0.0, 65535.0) * scale

        def lpbq_dequant(w):
            O, I = w.shape
            qmax = 2.0 ** (W_BITS - 1) - 1.0
            wb = w.reshape(O, I // BLOCK, BLOCK)
            s = jnp.maximum(jnp.max(jnp.abs(wb), axis=-1, keepdims=True) / qmax, 1e-12)
            wq = jnp.clip(jnp.round(wb / s), -qmax - 1.0, qmax) * s
            return wq.reshape(O, I)
        key = jax.random.key(seed)
        k1, k2, k3, k4 = jax.random.split(key, 4)
        B, S, H, I = (2, 1024, 256, 768)
        x = jax.random.normal(k1, (B, S, H), jnp.float32)
        w_gate = jax.random.normal(k2, (I, H), jnp.float32) * 0.02
        w_up = jax.random.normal(k3, (I, H), jnp.float32) * 0.02
        w_down = jax.random.normal(k4, (H, I), jnp.float32) * 0.02
        return {'x': x, 'w_gate': w_gate, 'w_up': w_up, 'w_down': w_down}
    _L0_ffn_all = _L0_ffn_setup()
    _L0_ffn_in = {k: v for k, v in _L0_ffn_all.items() if k in ('w_gate', 'w_up', 'w_down')}
    del _L0_ffn_all
    return {'x': x, 'txt': txt, 'L0_tok_weight': _L0_tok_in['weight'], 'L0_tok_weighted_sum': _L0_tok_in['weighted_sum'], 'L0_attn_W_Q': _L0_attn_in['W_Q'], 'L0_attn_b_Q': _L0_attn_in['b_Q'], 'L0_attn_W_K': _L0_attn_in['W_K'], 'L0_attn_b_K': _L0_attn_in['b_K'], 'L0_attn_W_V': _L0_attn_in['W_V'], 'L0_attn_b_V': _L0_attn_in['b_V'], 'L0_attn_W_O': _L0_attn_in['W_O'], 'L0_attn_b_O': _L0_attn_in['b_O'], 'L0_ffn_w_gate': _L0_ffn_in['w_gate'], 'L0_ffn_w_up': _L0_ffn_in['w_up'], 'L0_ffn_w_down': _L0_ffn_in['w_down']}

def reference(x, txt, L0_tok_weight, L0_tok_weighted_sum, L0_attn_W_Q, L0_attn_b_Q, L0_attn_W_K, L0_attn_b_K, L0_attn_W_V, L0_attn_b_V, L0_attn_W_O, L0_attn_b_O, L0_ffn_w_gate, L0_ffn_w_up, L0_ffn_w_down):
    import jax
    import jax.numpy as jnp

    def _L0_tok_ref(x, weight, weighted_sum):
        import jax, jax.numpy as jnp
        import numpy as np
        return jnp.einsum('bhid,oi,od->bho', x, weighted_sum, weight)

    def _L0_attn_ref(x, W_Q, b_Q, W_K, b_K, W_V, b_V, W_O, b_O):
        import jax, jax.numpy as jnp
        import numpy as np
        B, T, D = (4, 512, 256)
        H, Dh = (16, 64)
        Q = jnp.einsum('btd,hkd->bthk', x, W_Q) + b_Q
        K = jnp.einsum('btd,hkd->bthk', x, W_K) + b_K
        V = jnp.einsum('btd,hkd->bthk', x, W_V) + b_V
        d_head = W_Q.shape[1]
        scores = jnp.einsum('bqhk,bshk->bhqs', Q, K) / jnp.sqrt(jnp.asarray(d_head, x.dtype))
        attn = jax.nn.softmax(scores, axis=-1)
        out_h = jnp.einsum('bhqs,bshk->bqhk', attn, V)
        return jnp.einsum('bqhk,hdk->bqd', out_h, W_O) + b_O

    def _L0_ffn_ref(x, w_gate, w_up, w_down):
        import jax, jax.numpy as jnp
        import numpy as np
        BLOCK = 32
        W_BITS = 4
        ACT_BITS = 16

        def act_qdq(x):
            qmax = 2.0 ** (ACT_BITS - 1) - 1.0
            scale = jnp.maximum(jnp.max(jnp.abs(x)) / qmax, 1e-12)
            return jnp.clip(jnp.round(x / scale), -qmax - 1.0, qmax) * scale

        def fixed_qdq_u16(x):
            scale = 1.0 / 65536.0
            return jnp.clip(jnp.round(x / scale), 0.0, 65535.0) * scale

        def lpbq_dequant(w):
            O, I = w.shape
            qmax = 2.0 ** (W_BITS - 1) - 1.0
            wb = w.reshape(O, I // BLOCK, BLOCK)
            s = jnp.maximum(jnp.max(jnp.abs(wb), axis=-1, keepdims=True) / qmax, 1e-12)
            wq = jnp.clip(jnp.round(wb / s), -qmax - 1.0, qmax) * s
            return wq.reshape(O, I)
        x = act_qdq(x)
        up = act_qdq(x @ lpbq_dequant(w_up).T)
        gate = act_qdq(x @ lpbq_dequant(w_gate).T)
        sig = fixed_qdq_u16(jax.nn.sigmoid(gate))
        gate = act_qdq(gate * sig)
        o = act_qdq(gate * up)
        return o @ lpbq_dequant(w_down).T
    h = _L0_tok_ref(x, L0_tok_weight, L0_tok_weighted_sum)
    h = jnp.concatenate([h, txt], axis=1)
    h = h + _L0_attn_ref(_layernorm(h, axis=-1), L0_attn_W_Q, L0_attn_b_Q, L0_attn_W_K, L0_attn_b_K, L0_attn_W_V, L0_attn_b_V, L0_attn_W_O, L0_attn_b_O)
    h = h + _L0_ffn_ref(_layernorm(h, axis=-1), L0_ffn_w_gate, L0_ffn_w_up, L0_ffn_w_down)
    return h

_drawn_inputs = setup_inputs


def setup_inputs(seed=0):
    import zlib

    import numpy as np

    out = dict(_drawn_inputs(seed))
    spreads = {'L0_attn_b_Q': (0.0, 0.8),
     'L0_attn_b_K': (0.0, 0.8),
     'L0_attn_b_V': (0.0, 0.1),
     'L0_attn_b_O': (0.0, 0.1)}
    factors = {'L0_attn_W_Q': 8.0, 'L0_attn_W_K': 8.0, 'L0_attn_W_V': 8.0}
    for name, (base, spread) in spreads.items():
        noise = np.random.default_rng([zlib.crc32(name.encode()), seed]).standard_normal(out[name].shape)
        drawn = base * np.exp(spread * noise) if base else spread * noise
        out[name] = jnp.asarray(drawn.astype(out[name].dtype))
    for name, factor in factors.items():
        out[name] = (out[name] * factor).astype(out[name].dtype)
    return out
```

```python
import concourse.bass as bass
from concourse import mybir
from contextlib import ExitStack

F32, F16, I16, U16 = mybir.dt.float32, mybir.dt.float16, mybir.dt.int16, mybir.dt.uint16
I32, U32 = mybir.dt.int32, mybir.dt.uint32
ALU = mybir.AluOpType
ACT = mybir.ActivationFunctionType
AX = mybir.AxisListType
RMAX = bass.bass_isa.ReduceOp.max

B = 8
T_IMG, T_TXT = 512, 128
T = T_IMG + T_TXT
TT = T // 128
HT = T // 2
D = 256
KT = D // 128
DC = 4
HEADS, DH = 16, 64
HD = HEADS * DH
PAIRS = HEADS // 2
F = 768
FT = F // 128
BLK = 32
NBLK = FT * D // BLK
LN_EPS = 1e-5
QMAX16, QMAX4 = 32767.0, 7.0
W_SCALE = 8.0
M_UNIT = 32768.0
RING = 4
LEAD = 3
GC = 1024
NG = FT * B * T // GC
DT = 4
ND = B * TT // DT


class Ready:

    def __init__(self, eng, sem, base=0):
        self.eng, self.sem, self.base, self.n = eng, sem, base, 0

    def __call__(self, ins, wait=True):
        self.n += 1
        ins.then_inc(self.sem, 1)
        if wait:
            self.eng.wait_ge(self.sem, self.base + self.n)


def build(nc, xT, txt, ws, wb, wq, wk, wv, wo, bq, bk, bv, bo, w_up, w_gate, w_down, out):
    ctx = ExitStack()
    with ctx:
        sem = lambda name: ctx.enter_context(nc.semaphore(name))

        start = 16512
        end = 229344
        at = [start]

        def place(name, shape, dt, where=None):
            where = at if where is None else where
            n = mybir.dt.size(dt)
            for k in shape[1:]:
                n *= k
            t = nc.alloc_sbuf_tensor_at(name, shape, dt, offset=where[0])
            where[0] += -(-n // 32) * 32
            assert where[0] <= end, (name, where[0])
            return t

        ident = place("ident", [128, 128], F32)
        ident16 = place("ident16", [128, 128], F16)
        ones = place("ones", [128, DH], F32)
        bo_row = place("bo_row", [128, D], F32)
        b_raw = place("b_raw", [128, 3, PAIRS], F32)
        b_scaled = place("b_scaled", [128, 3, PAIRS], F32)
        amax = place("amax", [128, 8], F32)
        bmax = place("bmax", [128, 3], F32)
        amax_all = place("amax_all", [128, 8], F32)
        pow2 = place("pow2", [128, 8], F32)
        wmul = place("wmul", [128, 8], F32)
        sc = place("sc", [128, 32], F32)
        blk_max = place("blk_max", [128, 3, NBLK], F32)
        blk_s = place("blk_s", [128, 3, NBLK], F32)
        blk_r = place("blk_r", [128, 3, NBLK], F32)
        bn6 = place("bn6", [128, TT, 6], F32)
        bn2 = place("bn2", [128, TT, 2], F32)
        rs = place("rs", [128, 4, TT], F32)
        nmax = place("nmax", [128, 2 * TT], F32)
        nmax16 = place("nmax16", [128, 2 * TT], F16)
        xmax = place("xmax", [128, B], F32)
        umax = place("umax", [128, B * FT], F32)
        gmax = place("gmax", [128, B * FT], F32)
        pmax = place("pmax", [128, NG], F32)
        omax = place("omax", [128, NG], F32)
        ffn_hi = [place(f"{n}_hi", [128, KT * F], F16) for n in ("up", "gate", "down")]
        ffn_lo = [place(f"{n}_lo", [128, KT * F], F16) for n in ("up", "gate", "down")]
        XB = 2 * KT * T
        x_at = at[0]
        X = place("X", [128, B * XB], F16)
        X32 = nc.alloc_sbuf_tensor_at("X32", [128, B * XB // 2], F32, offset=x_at)
        stage_at = at[0]
        w_hi = [place(f"w{n}_hi", [128, KT, HD], F16) for n in "qkv"]
        w_lo = [place(f"w{n}_lo", [128, KT, HD], F16) for n in "qkv"]
        wo_hi = place("wo_hi", [128, PAIRS, D], F16)
        wo_lo = place("wo_lo", [128, PAIRS, D], F16)
        ab_at = at[0]

        a = [ab_at]
        h_all = place("h_all", [128, B * TT, D], F32, a)
        xbuf = [place(f"xbuf{i}", [128, KT, DC, 128], F32, a) for i in range(4)]
        xn = place("xn", [128, TT, D], F32, a)
        w2 = place("w2", [128, KT, DC, D], F32, a)
        w_raw = [place(f"w{n}_raw", [128, KT * HD], F32, a) for n in "qkv"]
        ffn_q = place("ffn_q", [128, KT * F], I16, a)
        late = [x_at + 4 * 2 * XB]
        ffn_raw = [place(f"{n}_raw", [128, KT * F], F32, late) for n in ("up", "gate", "down")]
        late = [x_at + 2 * 2 * XB]
        w_raw.append(place("wo_raw", [128, PAIRS * D], F32, late))
        ws_sb = place("ws_sb", [128, KT, D], F32, a)
        wb_sb = place("wb_sb", [128, DC, D], F32, a)

        a = [ab_at]
        v_all = place("v_all", [128, TT, HD], F32, a)
        qA = [place(f"qA{i}", [128, 2, T], F16, a) for i in range(2)]
        qB = [place(f"qB{i}", [128, 2, T], F16, a) for i in range(2)]
        kA = [place(f"kA{i}", [128, 2, T], F16, a) for i in range(2)]
        kB = [place(f"kB{i}", [128, 2, T], F16, a) for i in range(2)]
        v_pair = [place(f"v_pair{i}", [128, TT, 128], F32, a) for i in range(2)]
        probs = place("probs", [128, RING, 2, HT], F32, a)
        psum_p = place("psum_p", [128, 2, T], F32, a)
        o_raw = place("o_raw", [128, 2, HT], F32, a)
        inv = place("inv", [128, 2, HT], F32, a)
        o_norm = place("o_norm", [128, T], F32, a)
        o_hi = place("o_hi", [128, PAIRS, T], F16, a)
        o_lo = place("o_lo", [128, PAIRS, T], F16, a)
        h2 = place("h2", [128, TT, D], F32, a)
        xn2 = place("xn2", [128, TT, D], F32, a)

        a = [stage_at]
        G = place("G", [128, FT, B * T], F32, a)
        Gf = G[:, :, :].rearrange("p f t -> p (f t)")
        ubuf = [place(f"ubuf{i}", [128, T], F32, a) for i in range(4)]
        xq = place("xq", [128, KT * T], I16, a)
        xh = [place(f"xh{i}", [128, KT, T], F16, a) for i in range(2)]
        xl = [place(f"xl{i}", [128, KT, T], F16, a) for i in range(2)]
        a = [x_at]
        gq = [place(f"gq{i}", [128, GC], I16, a) for i in range(2)]
        sg = [place(f"sg{i}", [128, GC], F32, a) for i in range(2)]
        sq = [place(f"sq{i}", [128, GC], U16, a) for i in range(2)]
        uin = [place(f"uin{i}", [128, GC], F32, a) for i in range(2)]
        uq = [place(f"uq{i}", [128, GC], I16, a) for i in range(2)]
        tq = [place(f"tq{i}", [128, GC], I16, a) for i in range(2)]
        assert a[0] <= stage_at
        a = [x_at]
        oq = place("oq", [128, FT, DT * 128], I16, a)
        oh = [place(f"oh{i}", [128, FT, DT * 128], F16, a) for i in range(2)]
        ol = [place(f"ol{i}", [128, FT, DT * 128], F16, a) for i in range(2)]
        assert a[0] <= stage_at
        a = [stage_at + FT * B * T * 4]
        hin = [place(f"hin{i}", [128, DT, D], F32, a) for i in range(2)]
        yout = [place(f"yout{i}", [128, DT, D], F32, a) for i in range(2)]

        ps = ctx.enter_context(nc.psum_tensor("ps", [128, 8, 512], F32))
        work = [ps[:, 0:2, :], ps[:, 2:4, :]]
        score = [ps[:, 4, 0:HT], ps[:, 5, 0:HT]]
        av = ps[:, 6:8, 0:HT]

        h_dram = nc.dram_tensor("h_scratch", [B, TT, 128, D], F32, kind="Internal").ap()
        u_dram = nc.dram_tensor("u_scratch", [128, FT * B * T], F32, kind="Internal").ap()

        S_SCORE, S_OUT, S_X, S_XI, S_U, S_UM, S_G, S_GM, S_T, S_TM, S_O, S_OM, S_Y, S_TMP, S_RED, S_ALL = (
            sc[:, i:i + 1] for i in range(16))

        ws_loaded, wb_loaded, attn_w_loaded, wo_loaded = sem("ws_loaded"), sem("wb_loaded"), sem("attn_w_loaded"), sem("wo_loaded")
        bias_loaded, ffn_w_loaded, txt_loaded = sem("bias_loaded"), sem("ffn_w_loaded"), sem("txt_loaded")
        x_loaded = [sem(f"x_loaded{i}") for i in range(4)]
        const_ready, ident_ready = sem("const_ready"), sem("ident_ready")
        w2_ready, tok_done, h_copied, xn_ready = sem("w2_ready"), sem("tok_done"), sem("h_copied"), sem("xn_ready")
        xt_done, x_hi_ready, x_lo_ready = sem("xt_done"), sem("x_hi_ready"), sem("x_lo_ready")
        bo_added, h_stored = sem("bo_added"), sem("h_stored")
        amax_ready, amax_reduced, wmul_ready = sem("amax_ready"), sem("amax_reduced"), sem("wmul_ready")
        w_hi_ready, w_lo_ready = sem("w_hi_ready"), sem("w_lo_ready")
        ffn_deq, ffn_t_done, ffn_hi_ready, ffn_lo_ready = sem("ffn_deq"), sem("ffn_t_done"), sem("ffn_hi_ready"), sem("ffn_lo_ready")
        vec_chain = sem("vec_chain")
        norm_chain = sem("norm_chain")
        work_full = [sem("work0_full"), sem("work1_full")]
        work_free = [sem("work0_free"), sem("work1_free")]
        score_ready, prob_ready, av_done, av_saved = sem("score_ready"), sem("prob_ready"), sem("av_done"), sem("av_saved")
        sum_done, q_hi_ready, k_hi_ready = sem("sum_done"), sem("q_hi_ready"), sem("k_hi_ready")
        prep_chain, qk_ready, nmax_ready, row_chain = sem("prep_chain"), sem("qk_ready"), sem("nmax_ready"), sem("row_chain")
        unit_ready, v_staged = sem("unit_ready"), sem("v_staged")
        o_normed, o_hi_ready, o_lo_ready = sem("o_normed"), sem("o_hi_ready"), sem("o_lo_ready")
        h_loaded, h2_stored, xn2_ready, x2_max = sem("h_loaded"), sem("h2_stored"), sem("xn2_ready"), sem("x2_max")
        red_ready, red_done, scales_ready, scale_chain = sem("red_ready"), sem("red_done"), sem("scales_ready"), sem("scale_chain")
        xh_ready, xl_ready, xq_chain = sem("xh_ready"), sem("xl_ready"), sem("xq_chain")
        unit_done, unit_copied, unit_max, u_stored = sem("unit_done"), sem("unit_copied"), sem("unit_max"), [sem(f"u_stored{i}") for i in range(4)]
        gq_ready, sg_ready, sq_ready, p_ready, p_max = sem("gq_ready"), sem("sg_ready"), sem("sq_ready"), sem("p_ready"), sem("p_max")
        u_loaded = [sem("u_loaded0"), sem("u_loaded1")]
        uq_ready, tq_ready, t_ready, t_max = sem("uq_ready"), sem("tq_ready"), sem("t_ready"), sem("t_max")
        oq_ready, oh_ready, ol_ready, y_done, y_ready = sem("oq_ready"), sem("oh_ready"), sem("ol_ready"), sem("y_done"), sem("y_ready")
        hin_loaded = [sem("hin_loaded0"), sem("hin_loaded1")]
        out_stored = [sem("out_stored0"), sem("out_stored1")]

        def n_prob(S, u, h):
            return 20 * (S + 1) + 2 * u + h + 1

        def n_av(S, u):
            return 10 * (S + 1) + u + 1

        def n_sum(S, u, h=1):
            half, j = divmod(u, TT)
            return 16 * (S + 1) + half * 8 + (max(j, 1) - 1) * 2 + h + 1

        def back(S, u, n):
            return (S, u - n) if u >= n else (S - 1, u - n + 10)

        TAIL = [("V", 0, 1), ("V", 1, 0), ("O", 0, 1), ("O", 1, 0), ("O", 2, 1), ("O", 3, 0), ("O", 4, 1),
                ("V", 2, 0), ("V", 3, 1), ("V", 4, 0), ("L", 0, 1), ("L", 1, 0), ("L", 2, 1), ("L", 3, 0), ("L", 4, 1)]
        TAIL_LAST = [("O", 0, 1), ("O", 1, 0), ("O", 2, 1), ("O", 3, 0), ("O", 4, 1),
                     ("L", 0, 0), ("L", 1, 1), ("L", 2, 0), ("L", 3, 1), ("L", 4, 0)]

        def slot_base(x, b, s, last=False):
            skipped = (0 if s < 7 else (1 if s == 7 else (7 if x == 0 else 8))) if last else 0
            return 10 + (63 if x == 0 else 64) * b + 7 * s - skipped

        def n_work(b, s, use, i=0, last=False):
            if use == "sum":
                return 0, slot_base(0, b, s, last)
            if use == "max":
                x = (1 + i) % 2
                return x, slot_base(x, b, s, last) + ((i + 1) // 2 if x == 0 else i // 2 + 1)
            if use == "row":
                return 1, slot_base(1, b, s, last) + 6
            if use == "Q":
                return 0, slot_base(0, b, s, last) + 6
            return 1, slot_base(1, b, s, last) + 7

        def n_tail(b, last, use, i):
            n = [0, 0]
            for name, k, x in (TAIL_LAST if last else TAIL):
                n[x] += 1
                if (name, k) == (use, i):
                    return x, slot_base(x, b, 8, last) + n[x]

        def n_start(use, i=0):
            order = [("Q", 0, 0), ("K", 0, 1)] + [("V", j, j % 2) for j in range(TT)]
            order += [("max", k, (1 + k) % 2) for k in range(10)] + [("row", 0, 1), ("Q", 1, 0), ("K", 1, 1)]
            n = [0, 0]
            for name, k, x in order:
                n[x] += 1
                if (name, k) == (use, i):
                    return x, n[x]

        def slots(body, b, last):
            eng = body.eng
            body(b, 0, 0, False)
            with eng.Fori(0, 2) as g:
                body(b, 1 + 2 * g, 1, False)
                body(b, 2 + 2 * g, 0, False)
            body(b, 5, 1, last)
            body(b, 6, 0, last)
            body(b, 7, 1, last)

        block = ctx.enter_context(nc.Block())

        @block.sync
        def _(sp):
            sp.dma_start(ws_sb[:, :, :], ws.rearrange("(k p) o -> p k o", p=128)).then_inc(ws_loaded, 16)
            sp.dma_start(wb_sb[:, :, :], wb.rearrange("d o -> (d o)").unsqueeze(0).to_broadcast([128, DC * D]).rearrange("p (d o) -> p d o", d=DC)
                         ).then_inc(wb_loaded, 16)
            for i in range(4):
                sp.dma_start(xbuf[i][:, :, :, :], xT[0, i]).then_inc(x_loaded[i], 16)
            with sp.Fori(1, B) as b:
                for i in range(4):
                    sp.wait_ge(tok_done, 4 * (b - 1) + i + 1)
                    sp.dma_start(xbuf[i][:, :, :, :], xT[bass.ds(b, 1), i].rearrange("a p k d t -> (a p) k d t")
                                 ).then_inc(x_loaded[i], 16)
            sp.wait_ge(h_stored, 16 * B)
            sp.wait_ge(work_full[0], 1)
            with sp.Fori(0, B) as b:
                sp.wait_ge(h2_stored, 16 * b)
                sp.dma_start(h2[:, :, :], h_dram[bass.ds(b, 1)].rearrange("a j p d -> p (a j) d")).then_inc(h_loaded, 16)
                sp.wait_ge(xn2_ready, TT * (b + 1))
                sp.dma_start(h_dram[bass.ds(b, 1)].rearrange("a j p d -> p (a j) d"), h2[:, :, :]).then_inc(h2_stored, 16)
            with sp.Fori(0, B) as b:
                for f in range(FT):
                    sp.wait_ge(unit_copied, 12 * b + 2 * f + 1)
                    sp.dma_start(u_dram[:, bass.ds(b * T + f * B * T, T)], ubuf[f % 4][:, :]
                                 ).then_inc(u_stored[f % 4], 16)
            for k in range(4):
                sp.wait_ge(u_stored[k], 16 * (B * (2 if k < 2 else 1)))
            sp.wait_ge(xl_ready, B)
            for k in range(2):
                sp.dma_start(uin[k][:, :], u_dram[:, k * GC:(k + 1) * GC]).then_inc(u_loaded[k], 16)
            with sp.Fori(1, NG // 2) as c:
                for k in range(2):
                    sp.wait_ge(uq_ready, 2 * (c - 1) + k + 1)
                    sp.dma_start(uin[k][:, :], u_dram[:, bass.ds(c * 2 * GC + k * GC, GC)]).then_inc(u_loaded[k], 16)
            hd = h_dram.rearrange("b j p d -> (b j) p d")
            sp.wait_ge(scales_ready, 2)
            sp.wait_ge(h2_stored, 16 * B)
            with sp.Fori(0, ND // 2) as c:
                for k in range(2):
                    sp.wait_ge(y_ready, DT * (2 * c + k))
                    sp.dma_start(hin[k][:, :, :], hd[bass.ds(c * 2 * DT + k * DT, DT)].rearrange("j p d -> p j d")
                                 ).then_inc(hin_loaded[k], 16)

        @block.gpsimd
        def _(pool):
            pool.memset(ident[:, :], 0.0).then_inc(const_ready, 1)
            pool.memset(ident16[:, :], 0.0).then_inc(const_ready, 1)
            pool.wait_ge(const_ready, 2)
            for m in (ident, ident16):
                pool.affine_select(out=m[:, :], in_=m[:, :], compare_op=ALU.not_equal, fill=1.0, base=0,
                                   pattern=[[-1, 128]], channel_multiplier=1).then_inc(ident_ready, 1)
            pool.wait_ge(amax_ready, 1)
            pool.partition_all_reduce(amax_all[:, 0:7], amax[:, 0:7], 128, RMAX).then_inc(amax_reduced, 1)
            bo_b = bo_row[:, :].unsqueeze(1).to_broadcast([128, TT, D])
            pool.wait_ge(bias_loaded, 64)
            with pool.Fori(0, B) as b:
                pool.wait_ge(xn_ready, TT * (b + 1))
                hb = h_all[:, bass.ds(b * TT, TT), :]
                pool.tensor_tensor(hb, hb, bo_b, ALU.add).then_inc(bo_added, 1)
                pool.wait_ge(bo_added, b + 1)
                pool.dma_start(h_dram[bass.ds(b, 1)].rearrange("a j p d -> p (a j) d"), hb).then_inc(h_stored, 16)
            pool.wait_ge(h_stored, 16 * B)
            pool.wait_ge(work_full[0], 1)
            pool.sem_inc(sum_done, 16)

            def pool_slot(b, s, par, last):
                S = 8 * b + s
                for half in range(2):
                    for j in range(1, TT):
                        for h in range(2):
                            u = half * TT + j
                            dst = psum_p[:, h, half * HT:(half + 1) * HT]
                            pool.wait_ge(prob_ready, n_prob(S, u, h))
                            if j == 1:
                                if half == 0 and h == 0:
                                    sb = b - 1 if (isinstance(s, int) and s == 0) else b
                                    ss = 8 if (isinstance(s, int) and s == 0) else s
                                    x, n = n_work(sb, ss, "sum", last=last and ss != 8)
                                    pool.wait_ge(work_full[0], n)
                                src = probs[:, (10 * par + u - 1) % RING, h, :]
                            else:
                                pool.wait_ge(sum_done, n_sum(S, u - 1, h))
                                src = dst
                            pool.tensor_tensor(dst, src, probs[:, (10 * par + u) % RING, h, :], ALU.add).then_inc(sum_done, 1)
            pool_slot.eng = pool
            with pool.Fori(0, B - 1) as b:
                slots(pool_slot, b, False)
            slots(pool_slot, B - 1, True)
            for k in range(4):
                pool.wait_ge(red_ready, k + 1)
                width = 2 if k == 1 else 1
                pool.partition_all_reduce(sc[:, 18 + 2 * k:18 + 2 * k + width], sc[:, 26:26 + width], 128, RMAX).then_inc(red_done, 1)

        @block.tensor
        def _(pe):
            mm = nc.tensor.matmul

            def tok(b, i):
                pe.wait_ge(x_loaded[i], 16 * (b + 1))
                pe.wait_ge(h_copied, 4 * b + i + 1)
                for n in range(KT * DC):
                    k, d = divmod(n, DC)
                    last = mm(ps[:, i, 0:D], xbuf[i][:, k, d, :], w2[:, k, d, :], start=n == 0, stop=n == KT * DC - 1)
                last.then_inc(tok_done, 1)

            def xn_transposes(b):
                for i in range(TT):
                    pe.wait_ge(xn_ready, TT * b + i + 1)
                    pe.wait_ge(x_lo_ready, TT * b + (1 if i == 4 else 0))
                    for k in range(KT):
                        last = nc.tensor.transpose(ps[:, 4 + i % 4, k * 128:(k + 1) * 128], xn[:, i, k * 128:(k + 1) * 128], ident[:, :])
                    last.then_inc(xt_done, 1)

            pe.wait_ge(w2_ready, KT)
            pe.wait_ge(ident_ready, 2)
            with pe.Fori(0, LEAD) as b:
                for i in range(4):
                    tok(b, i)
            for w in range(3):
                pe.wait_ge(ffn_deq, w + 1)
                for g in range(2):
                    n = 2 * w + g
                    bank = 4 + 2 * (n % 2)
                    if n >= 2:
                        pe.wait_ge(ffn_lo_ready, 2 * (n - 1))
                    for m in range(6):
                        if w < 2:
                            src = ffn_raw[w][:, m * D + g * 128:m * D + (g + 1) * 128]
                            dst = ps[:, bank + m // 3, (m % 3) * 128:(m % 3 + 1) * 128]
                        else:
                            dt_, f = divmod(m, 3)
                            src = ffn_raw[w][:, dt_ * F + (3 * g + f) * 128:dt_ * F + (3 * g + f + 1) * 128]
                            dst = ps[:, bank + dt_, f * 128:(f + 1) * 128]
                        last = nc.tensor.transpose(dst, src, ident[:, :])
                    last.then_inc(ffn_t_done, 1)
            pe.wait_ge(ffn_lo_ready, 12)
            with pe.Fori(0, B - LEAD) as b:
                for i in range(4):
                    tok(b + LEAD, i)
                xn_transposes(b)
            with pe.Fori(B - LEAD, B) as b:
                xn_transposes(b)

            def use(where, fill):
                x, n = where
                pe.wait_ge(work_free[x], n - 1)
                fill(work[x]).then_inc(work_full[x], 1)

            def project(wi, bb, pair):
                def fill(w):
                    n = 0
                    for k in range(KT):
                        for wt, xs in ((w_hi[wi], (0, 1)), (w_lo[wi], (0,))):
                            lhsT = wt[:, k, bass.ds(pair * 128, 128)]
                            for xp in xs:
                                for half in range(2):
                                    last = mm(w[:, half, 0:HT], lhsT, X[:, bass.ds(bb * XB + (xp * KT + k) * T + half * HT, HT)],
                                              start=n < 2, stop=n >= 10)
                                    n += 1
                    return last
                return fill

            def project_v(bb, j):
                def fill(w):
                    n = 0
                    for k in range(KT):
                        for xp, wt in ((0, w_hi[2]), (0, w_lo[2]), (1, w_hi[2])):
                            lhsT = X[:, bass.ds(bb * XB + (xp * KT + k) * T + j * 128, 128)]
                            for c in range(2):
                                last = mm(w[:, c, :], lhsT, wt[:, k, c * 512:(c + 1) * 512], start=n < 2, stop=n >= 10)
                                n += 1
                    return last
                return fill

            def max_tile(par, i):
                def fill(w):
                    t, h = divmod(i, 2)
                    for half in range(2):
                        last = mm(w[:, half, 0:HT], qA[par][:, h, t * 128:(t + 1) * 128], kA[par][:, h, half * HT:(half + 1) * HT],
                                  start=True, stop=True)
                    return last
                return fill

            def max_row(w):
                flat = w.rearrange("p a n -> p (a n)")
                for h in range(2):
                    for t in range(TT):
                        last = mm(flat[64 + 32 * h:65 + 32 * h, t * 128:(t + 1) * 128], nmax16[:, 2 * t + h:2 * t + h + 1], ident16[:, :],
                                  start=True, stop=True)
                return last

            def sum_rows(w):
                for half in range(2):
                    for h in range(2):
                        last = mm(w[64 * h:64 * h + 64, half, 0:HT], ones[:, :], psum_p[:, h, half * HT:(half + 1) * HT], start=True, stop=True)
                return last

            def out_tile(j):
                def fill(w):
                    n = 0
                    for p in range(PAIRS):
                        for ot, wt in ((o_hi, wo_hi), (o_hi, wo_lo), (o_lo, wo_hi)):
                            last = mm(w[:, 0, 0:D], ot[:, p, j * 128:(j + 1) * 128], wt[:, p, :], start=n == 0, stop=n == 3 * PAIRS - 1)
                            n += 1
                    return last
                return fill

            def xn2_tile(j):
                def fill(w):
                    for k in range(KT):
                        last = nc.tensor.transpose(w[:, 0, k * 128:(k + 1) * 128], xn2[:, j, k * 128:(k + 1) * 128], ident[:, :])
                    return last
                return fill

            def pe_slot(b, s, par, last):
                S = 8 * b + s
                nxt = not (last and isinstance(s, int) and s == 7)
                ahead = nxt and not (last and isinstance(s, int) and s == 6)
                finish = not (isinstance(s, int) and s == 0)
                other = 1 - par
                at_unit = {2: [0, 1], 3: [2], 4: [3, 4], 5: [5], 6: [6, 7], 7: [8], 8: [9]}
                if finish:
                    pe.wait_ge(work_free[1], n_work(b, s - 1, "row", last=last)[1])

                def attend(u):
                    half, j = divmod(u, TT)
                    if u == 0:
                        pe.wait_ge(v_staged, S + 1)
                        pe.wait_ge(av_saved, S)
                    pe.wait_ge(prob_ready, n_prob(S, u, 1))
                    for h in range(2):
                        last = mm(av[64 * h:64 * h + 64, half, :], v_pair[par][:, j, 64 * h:64 * h + 64],
                                  probs[:, (10 * par + u) % RING, h, :], start=j == 0, stop=j == TT - 1)
                    last.then_inc(av_done, 1)

                for u in range(10):
                    half, j = divmod(u, TT)
                    for h in range(2):
                        pe.wait_ge(prob_ready, n_prob(*back(S, u, 1), h))
                        mm(score[h], kA[par][:, h, j * 128:(j + 1) * 128], qA[par][:, h, half * HT:(half + 1) * HT], start=True, stop=False)
                        mm(score[h], kB[par][0:65, h, j * 128:(j + 1) * 128], qB[par][0:65, h, half * HT:(half + 1) * HT],
                           start=False, stop=True).then_inc(score_ready, 1)
                    if u == 0 and finish:
                        pe.wait_ge(sum_done, 16 * (S + 1))
                        use(n_work(b, s, "sum", last=last), sum_rows)
                    if nxt:
                        if u == 2:
                            pe.wait_ge(qk_ready, S + 2)
                        for i in at_unit.get(u, []):
                            use(n_work(b, s, "max", i, last), max_tile(other, i))
                        if u == 9:
                            pe.wait_ge(nmax_ready, S + 2)
                            use(n_work(b, s, "row", last=last), max_row)
                    if u:
                        attend(u - 1)
                if ahead:
                    use(n_work(b, s, "Q", last=last), project(0, b + (s + 2) // 8, (s + 2) % 8))
                attend(9)
                if ahead:
                    use(n_work(b, s, "K", last=last), project(1, b + (s + 2) // 8, (s + 2) % 8))
            pe_slot.eng = pe

            def pe_tail(b, last):
                pe.wait_ge(sum_done, 16 * (8 * b + 9))
                use(n_work(b, 8, "sum", last=last), sum_rows)
                for name, i, x in (TAIL_LAST if last else TAIL):
                    if name == "O" and i == 0:
                        pe.wait_ge(o_lo_ready, 8 * (b + 1))
                    if name == "L":
                        pe.wait_ge(xn2_ready, TT * (b + 1))
                    fill = {"V": lambda: project_v(b + 1, i), "O": lambda: out_tile(i), "L": lambda: xn2_tile(i)}[name]()
                    use(n_tail(b, last, name, i), fill)

            pe.wait_ge(x_lo_ready, TT * B)
            pe.wait_ge(x_hi_ready, TT * B)
            pe.wait_ge(w_lo_ready, 4)
            pe.sem_inc(av_done, 10)
            pe.wait_ge(unit_ready, 2)
            use(n_start("Q", 0), project(0, 0, 0))
            use(n_start("K", 0), project(1, 0, 0))
            for j in range(TT):
                use(n_start("V", j), project_v(0, j))
            pe.wait_ge(qk_ready, 1)
            for i in range(10):
                use(n_start("max", i), max_tile(0, i))
            pe.wait_ge(nmax_ready, 1)
            use(n_start("row"), max_row)
            use(n_start("Q", 1), project(0, 0, 1))
            use(n_start("K", 1), project(1, 0, 1))
            with pe.Fori(0, B - 1) as b:
                slots(pe_slot, b, False)
                pe_tail(b, False)
            slots(pe_slot, B - 1, True)
            pe_tail(B - 1, True)

            pe.sem_inc(unit_done, 2 * FT)
            pe.sem_inc(y_done, DT)
            pe.wait_ge(work_free[0], n_tail(B - 1, True, "L", 4)[1])
            pe.wait_ge(work_free[1], n_tail(B - 1, True, "L", 3)[1])
            with pe.Fori(0, B // 2) as bb:
                for par in range(2):
                    b = 2 * bb + par
                    pe.wait_ge(xh_ready, b + 1)
                    pe.wait_ge(xl_ready, b + 1)
                    for n in range(2 * FT):
                        f, w = divmod(n, 2)
                        if n < 4 and par == 0:
                            pe.wait_ge(unit_copied, 12 * b)
                        else:
                            pe.wait_ge(unit_copied, 12 * b + n - 3)
                        u = ps[:, 2 * (n % 4):2 * (n % 4) + 2, :]
                        m = 0
                        for k in range(KT):
                            for wt, xs in ((ffn_hi[w], (xh, xl)), (ffn_lo[w], (xh,))):
                                for xp in xs:
                                    for half in range(2):
                                        last = mm(u[:, half, 0:HT], wt[:, k * F + f * 128:k * F + (f + 1) * 128],
                                                  xp[par][:, k, half * HT:(half + 1) * HT], start=m < 2, stop=m >= 10)
                                        m += 1
                        last.then_inc(unit_done, 1)
            with pe.Fori(0, ND // 2) as c:
                for k in range(2):
                    n = 2 * c + k
                    pe.wait_ge(ol_ready, n + 1)
                    for j in range(DT):
                        pe.wait_ge(y_ready, DT * n)
                        m = 0
                        for f in range(FT):
                            for ot, wt in ((oh, ffn_hi[2]), (oh, ffn_lo[2]), (ol, ffn_hi[2])):
                                last = mm(ps[:, 4 * k + j, 0:D], ot[k][:, f, j * 128:(j + 1) * 128], wt[:, f * D:(f + 1) * D],
                                          start=m == 0, stop=m == 3 * FT - 1)
                                m += 1
                        last.then_inc(y_done, 1)

        @block.scalar
        def _(act):
            fn = nc.scalar.activation
            for i, w in enumerate((wq, wk, wv)):
                act.dma_start(w_raw[i][:, :].rearrange("p (k n) -> p k n", k=KT), w.rearrange("(k p) n -> p k n", p=128)).then_inc(attn_w_loaded, 16)
            act.dma_start(w_raw[3][:, :].rearrange("p (k n) -> p k n", k=PAIRS), wo.rearrange("(k p) n -> p k n", p=128)).then_inc(wo_loaded, 16)
            for i, bias in enumerate((bq, bk, bv)):
                act.dma_start(b_raw[:, i, :], bias).then_inc(bias_loaded, 16)
            act.dma_start(bo_row[:, :], bo.unsqueeze(0).to_broadcast([128, D])).then_inc(bias_loaded, 16)
            for i, w in enumerate((w_up, w_gate, w_down)):
                act.dma_start(ffn_raw[i][:, :].rearrange("p (k n) -> p k n", k=(FT, FT, KT)[i]), w.rearrange("(k p) n -> p k n", p=128)).then_inc(ffn_w_loaded, 16)
            for b in range(B):
                act.dma_start(h_all[:, b * TT + TT - 1, :], txt[b]).then_inc(txt_loaded, 16)

            def copy_h(b):
                for i in range(4):
                    act.wait_ge(tok_done, 4 * b + i + 1)
                    fn(h_all[:, bass.ds(b * TT + i, 1), :].rearrange("p a d -> p (a d)"), ps[:, i, 0:D], ACT.Copy).then_inc(h_copied, 1)

            def split_x(b):
                for i in range(TT):
                    act.wait_ge(xt_done, TT * b + i + 1)
                    dst = X[:, bass.ds(b * XB, KT * T)].rearrange("p (k t) -> p k t", k=KT)[:, :, i * 128:(i + 1) * 128]
                    fn(dst, ps[:, 4 + i % 4, 0:D].rearrange("p (k t) -> p k t", k=KT), ACT.Copy).then_inc(x_hi_ready, 1)

            act.sem_inc(h_copied, 4)
            with act.Fori(0, LEAD) as b:
                copy_h(b)
            act.wait_ge(wmul_ready, 1)
            for i in range(4):
                dst = w_hi[i][:, :, :].rearrange("p k n -> p (k n)") if i < 3 else wo_hi[:, :, :].rearrange("p k n -> p (k n)")
                fn(dst, w_raw[i][:, :], ACT.Copy, scale=wmul[:, i:i + 1]).then_inc(w_hi_ready, 1)
            for w in range(3):
                for g in range(2):
                    n = 2 * w + g
                    bank = 4 + 2 * (n % 2)
                    act.wait_ge(ffn_t_done, n + 1)
                    for m in range(2):
                        if w < 2:
                            dst = ffn_hi[w][:, g * F + m * 384:g * F + (m + 1) * 384]
                            src = ps[:, bank + m, 0:384]
                        else:
                            dst = ffn_hi[w][:, :].rearrange("p (f n) -> p f n", n=D)[:, 3 * g:3 * g + 3, m * 128:(m + 1) * 128]
                            src = ps[:, bank + m, 0:384].rearrange("p (f n) -> p f n", n=128)
                        fn(dst, src, ACT.Copy, scale=wmul[:, 4 + w:5 + w]).then_inc(ffn_hi_ready, 1)
            act.wait_ge(w_lo_ready, 4)
            with act.Fori(0, B - LEAD) as b:
                copy_h(b + LEAD)
                split_x(b)
            with act.Fori(B - LEAD, B) as b:
                split_x(b)

            act.wait_ge(x_lo_ready, TT * B)
            act.wait_ge(h_stored, 16 * B)
            act.sem_inc(prob_ready, 20)

            def hi_part(dst, wi, sem_hi, where, P, pair, par):
                x, n = where
                act.wait_ge(work_full[x], n)
                for h in range(2):
                    fn(dst[par][0:64, h, :].rearrange("p (a n) -> p a n", a=2), work[x][64 * h:64 * h + 64, :, 0:HT], ACT.Identity,
                       bias=b_scaled[64 * h:64 * h + 64, wi, bass.ds(pair, 1)]).then_inc(sem_hi, 1)

            def move_rows(where, par):
                x, n = where
                act.wait_ge(work_full[x], n)
                for h in range(2):
                    flat = work[x].rearrange("p a n -> p (a n)")
                    ins = fn(qB[par][64:65, h, :], flat[64 + 32 * h:65 + 32 * h, 0:T], ACT.Copy)
                    ins.then_inc(work_free[x] if h else row_chain, 1)

            def copy_v(where, j):
                x, n = where
                act.wait_ge(work_full[x], n)
                fn(v_all[:, j, :], work[x].rearrange("p a n -> p (a n)"), ACT.Copy).then_inc(work_free[x], 1)

            def o_high(b, s):
                act.wait_ge(o_normed, 8 * b + s)
                act.wait_ge(work_full[1], slot_base(1, b, 0) - 4)
                fn(o_hi[:, bass.ds(s - 1, 1), :].rearrange("p a t -> p (a t)"), o_norm[:, :], ACT.Identity,
                   bias=b_scaled[:, 2, bass.ds(s - 1, 1)]).then_inc(o_hi_ready, 1)

            def act_slot(b, s, par, last):
                S = 8 * b + s
                nxt = not (last and isinstance(s, int) and s == 7)
                ahead = nxt and not (last and isinstance(s, int) and s == 6)
                finish = not (isinstance(s, int) and s == 0)
                other = 1 - par
                for u in range(10):
                    act.wait_ge(av_done, n_av(*back(S, u, RING)))
                    act.wait_ge(sum_done, n_sum(*back(S, u, RING)))
                    for h in range(2):
                        act.wait_ge(score_ready, 20 * S + 2 * u + h + 1)
                        fn(probs[:, (10 * par + u) % RING, h, :], score[h], ACT.Exp, scale=S_SCORE).then_inc(prob_ready, 1)
                    if u == 0 and nxt and finish:
                        hi_part(kA, 1, k_hi_ready, n_work(b, s - 1, "K"), S + 1, (s + 1) % 8, other)
                    if u == 2 and finish:
                        o_high(b, s)
                if nxt:
                    move_rows(n_work(b, s, "row", last=last), other)
                if ahead:
                    hi_part(qA, 0, q_hi_ready, n_work(b, s, "Q", last=last), S + 2, (s + 2) % 8, par)
                act.wait_ge(av_done, n_av(S, 9))
                act.wait_ge(o_normed, S)
                fn(o_raw[:, :, :], av, ACT.Copy).then_inc(av_saved, 1)
            act_slot.eng = act

            def act_tail(b, last):
                if not last:
                    hi_part(kA, 1, k_hi_ready, n_work(b, 7, "K"), 8 * b + 9, 1, 1)
                    act.wait_ge(v_staged, 8 * (b + 1))
                else:
                    o_high(b, 8)
                for name, i, _x in (TAIL_LAST if last else TAIL):
                    if name == "V":
                        copy_v(n_tail(b, last, name, i), i)
                        if i == 0:
                            o_high(b, 8)
                    if name == "L":
                        x, n = n_tail(b, last, name, i)
                        act.wait_ge(work_full[x], n)
                        dst = X32[:, bass.ds(b * (XB // 2), KT * T)].rearrange("p (k t) -> p k t", k=KT)[:, :, i * 128:(i + 1) * 128]
                        fn(dst, work[x][:, 0, 0:D].rearrange("p (k t) -> p k t", k=KT), ACT.Copy).then_inc(work_free[x], 1)

            hi_part(qA, 0, q_hi_ready, n_start("Q", 0), 0, 0, 0)
            hi_part(kA, 1, k_hi_ready, n_start("K", 0), 0, 0, 0)
            for j in range(TT):
                copy_v(n_start("V", j), j)
            move_rows(n_start("row"), 0)
            hi_part(qA, 0, q_hi_ready, n_start("Q", 1), 1, 1, 1)
            hi_part(kA, 1, k_hi_ready, n_start("K", 1), 1, 1, 1)
            with act.Fori(0, B - 1) as b:
                slots(act_slot, b, False)
                act_tail(b, False)
            slots(act_slot, B - 1, True)
            act_tail(B - 1, True)

            act.wait_ge(h2_stored, 16 * B)
            with act.Fori(0, B) as b:
                for n in range(2 * FT):
                    f, w = divmod(n, 2)
                    act.wait_ge(unit_done, 2 * FT * (b + 1) + n + 1)
                    src = ps[:, 2 * (n % 4):2 * (n % 4) + 2, 0:HT]
                    if w == 0:
                        act.wait_ge(u_stored[f % 4], 16 * (b * (2 if f % 4 < 2 else 1) + f // 4))
                        act.wait_ge(unit_max, 12 * b + (n - 7 if n >= 8 else 0))
                        dst = ubuf[f % 4][:, :]
                    else:
                        dst = G[:, f, bass.ds(b * T, T)]
                    fn(dst.rearrange("p (a n) -> p a n", a=2), src, ACT.Copy).then_inc(unit_copied, 1)
            act.wait_ge(scales_ready, 2)
            with act.Fori(0, NG // 2) as c:
                for k in range(2):
                    n = 2 * c + k
                    act.wait_ge(p_ready, n + 1)
                    fn(gq[k][:, :], Gf[:, bass.ds(n * GC, GC)], ACT.Copy, scale=S_GM).then_inc(gq_ready, 1)
                    act.wait_ge(gq_ready, n + 1)
                    fn(sg[k][:, :], gq[k][:, :], ACT.Sigmoid, scale=S_G).then_inc(sg_ready, 1)
            act.wait_ge(scales_ready, 3)
            with act.Fori(0, NG // 2) as c:
                for k in range(2):
                    n = 2 * c + k
                    act.wait_ge(t_ready, n + 1)
                    fn(tq[k][:, :], Gf[:, bass.ds(n * GC, GC)], ACT.Copy, scale=S_TM).then_inc(tq_ready, 1)
                    act.wait_ge(u_loaded[k], 16 * (c + 1))
                    fn(uq[k][:, :], uin[k][:, :], ACT.Copy, scale=S_UM).then_inc(uq_ready, 1)
            od = out.rearrange("b (j p) d -> (b j) p d", p=128)
            with act.Fori(0, ND // 2) as c:
                for k in range(2):
                    act.wait_ge(y_ready, DT * (2 * c + k + 2))
                    act.dma_start(od[bass.ds(c * 2 * DT + k * DT, DT)].rearrange("j p d -> p j d"), yout[k][:, :, :]).then_inc(out_stored[k], 16)
            for k in range(2):
                act.wait_ge(out_stored[k], 16 * (ND // 2))

        @block.vector
        def _(dve):
            v = nc.vector
            step = Ready(dve, vec_chain)

            dve.wait_ge(ws_loaded, 16)
            dve.wait_ge(wb_loaded, 16)
            for k in range(KT):
                v.tensor_tensor(w2[:, k, :, :], ws_sb[:, k, :].unsqueeze(1).to_broadcast([128, DC, D]), wb_sb[:, :, :], ALU.mult).then_inc(w2_ready, 1)
            step(v.memset(ones[:, :], 1.0), wait=False)
            dve.wait_ge(attn_w_loaded, 48)
            for i in range(3):
                step(v.tensor_reduce(amax[:, i:i + 1], w_raw[i][:, :], op=ALU.max, axis=AX.X, apply_absolute_value=True), wait=False)
            dve.wait_ge(wo_loaded, 16)
            step(v.tensor_reduce(amax[:, 3:4], w_raw[3][:, :], op=ALU.max, axis=AX.X, apply_absolute_value=True), wait=False)
            dve.wait_ge(bias_loaded, 64)
            step(v.tensor_reduce(bmax[:, :], b_raw[:, :, :], op=ALU.max, axis=AX.X, apply_absolute_value=True), wait=False)
            dve.wait_ge(ffn_w_loaded, 48)
            for i in range(3):
                step(v.tensor_reduce(blk_max[:, i, :], ffn_raw[i][:, :].rearrange("p (n c) -> p n c", c=BLK), op=ALU.max, axis=AX.X,
                                     apply_absolute_value=True), wait=i == 2)
            step(v.tensor_reduce(amax[:, 4:7], blk_max[:, :, :], op=ALU.max, axis=AX.X))
            v.scalar_tensor_tensor(amax[:, 0:3], bmax[:, :], 1.0 / 16, amax[:, 0:3], ALU.mult, ALU.max).then_inc(amax_ready, 1)
            dve.wait_ge(amax_reduced, 1)
            step(v.tensor_scalar(amax_all[:, 0:7], amax_all[:, 0:7], 1e-30, None, ALU.max))
            step(v.tensor_scalar(pow2[:, 0:7].bitcast(U32), amax_all[:, 0:7].bitcast(U32), 0x7F800000, None, ALU.bitwise_and))
            step(v.reciprocal(wmul[:, 0:7], pow2[:, 0:7]))
            v.tensor_scalar(wmul[:, 0:7], wmul[:, 0:7], W_SCALE, None, ALU.mult).then_inc(wmul_ready, 1)
            dve.wait_ge(wmul_ready, 1)
            for i in range(3):
                step(v.tensor_scalar(b_scaled[:, i, :], b_raw[:, i, :], wmul[:, i:i + 1], None, ALU.mult), wait=False)
            step(v.scalar_tensor_tensor(S_SCORE, pow2[:, 0:1], 1.0 / (W_SCALE * W_SCALE * DH ** 0.5), pow2[:, 1:2], ALU.mult, ALU.mult), wait=False)
            step(v.scalar_tensor_tensor(S_OUT, pow2[:, 2:3], 1.0 / (W_SCALE * W_SCALE), pow2[:, 3:4], ALU.mult, ALU.mult))
            step(v.tensor_scalar(blk_s[:, :, :], blk_max[:, :, :], 1.0 / QMAX4, 1e-12, ALU.mult, ALU.max))
            step(v.reciprocal(blk_r[:, :, :], blk_s[:, :, :]))
            for i in range(3):
                w3 = ffn_raw[i][:, :].rearrange("p (n c) -> p n c", c=BLK)
                q3 = ffn_q[:, :].rearrange("p (n c) -> p n c", c=BLK)
                step(v.tensor_tensor(w3, w3, blk_r[:, i, :].unsqueeze(2).to_broadcast([128, NBLK, BLK]), ALU.mult))
                step(v.tensor_scalar(ffn_q[:, :], ffn_raw[i][:, :], QMAX4, -QMAX4 - 1, ALU.min, ALU.max))
                v.tensor_tensor(w3, q3, blk_s[:, i, :].unsqueeze(2).to_broadcast([128, NBLK, BLK]), ALU.mult).then_inc(ffn_deq, 1)
                dve.wait_ge(ffn_deq, i + 1)
            for i in range(4):
                dve.wait_ge(w_hi_ready, i + 1)
                hi = w_hi[i][:, :, :].rearrange("p k n -> p (k n)") if i < 3 else wo_hi[:, :, :].rearrange("p k n -> p (k n)")
                lo = w_lo[i][:, :, :].rearrange("p k n -> p (k n)") if i < 3 else wo_lo[:, :, :].rearrange("p k n -> p (k n)")
                v.scalar_tensor_tensor(lo, w_raw[i][:, :], wmul[:, i:i + 1], hi, ALU.mult, ALU.subtract).then_inc(w_lo_ready, 1)
            for w in range(3):
                for g in range(2):
                    n = 2 * w + g
                    bank = 4 + 2 * (n % 2)
                    for m in range(2):
                        dve.wait_ge(ffn_hi_ready, 2 * n + m + 1)
                        if w < 2:
                            view = lambda t: t[:, g * F + m * 384:g * F + (m + 1) * 384]
                            src = ps[:, bank + m, 0:384]
                        else:
                            view = lambda t: t[:, :].rearrange("p (f n) -> p f n", n=D)[:, 3 * g:3 * g + 3, m * 128:(m + 1) * 128]
                            src = ps[:, bank + m, 0:384].rearrange("p (f n) -> p f n", n=128)
                        v.scalar_tensor_tensor(view(ffn_lo[w]), src, wmul[:, 4 + w:5 + w], view(ffn_hi[w]), ALU.mult, ALU.subtract).then_inc(ffn_lo_ready, 1)

            NORM = 2 + 3 + 12

            def row_stats(n, tile):
                link = Ready(dve, norm_chain, NORM * n)
                for j in range(TT):
                    ins = v.bn_stats(bn6[:, j, :], tile(j))
                link(ins)
                v.memset(rs[:, 2, :], 0.0)
                for j in range(TT):
                    ins = v.bn_aggr(bn2[:, j, :], bn6[:, j, :])
                link(ins)
                y, vh, t, u = (rs[:, i, :] for i in range(4))
                var = bn2[:, :, 1]
                link(v.tensor_scalar(u, var, LN_EPS, None, ALU.add))
                link(v.tensor_scalar(t.bitcast(U32), u.bitcast(U32), 1, None, ALU.logical_shift_right))
                v.tensor_scalar(vh, u, 0.5, None, ALU.mult)
                link(v.tensor_scalar(y.bitcast(I32), t.bitcast(I32), -1.0, 1597463007.0, ALU.mult, ALU.add))
                for _ in range(3):
                    link(v.tensor_tensor(t, y, y, ALU.mult))
                    link(v.tensor_tensor(t, t, vh, ALU.mult))
                    link(v.tensor_scalar(t, t, -1.0, 1.5, ALU.mult, ALU.add))
                    link(v.tensor_tensor(y, y, t, ALU.mult))
                assert link.n == NORM

            def normalise(dst, src, ready):
                for j in range(TT):
                    v.tensor_scalar(dst[:, j, :], src(j), bn2[:, j, 0:1], rs[:, 0, j:j + 1], ALU.subtract, ALU.mult).then_inc(ready, 1)

            def norm1(b):
                dve.wait_ge(h_copied, 4 * (b + 2))
                dve.wait_ge(txt_loaded, 16 * B)
                dve.wait_ge(xn_ready, TT * b)
                tile = lambda j: h_all[:, bass.ds(b * TT + j, 1), :].rearrange("p a d -> p (a d)")
                row_stats(b, tile)
                dve.wait_ge(xt_done, TT * b)
                normalise(xn, tile, xn_ready)
                for j in range(TT):
                    dve.wait_ge(x_hi_ready, TT * b + j + 1)
                    part = lambda hl: X[:, bass.ds(b * XB + hl * KT * T, KT * T)].rearrange("p (k t) -> p k t", k=KT)[:, :, j * 128:(j + 1) * 128]
                    v.tensor_tensor(part(1), ps[:, 4 + j % 4, 0:D].rearrange("p (k t) -> p k t", k=KT), part(0), ALU.subtract).then_inc(x_lo_ready, 1)
            with dve.Fori(0, B) as b:
                norm1(b)

            dve.wait_ge(x_lo_ready, TT * B)
            dve.wait_ge(xn_ready, TT * B)
            dve.wait_ge(h_stored, 16 * B)
            for par in range(2):
                v.memset(kB[par][64:65, :, :], M_UNIT).then_inc(unit_ready, 1)

            def low_parts(Pq, where_q, where_k, par, pair):
                for dst, hi, wi, sem_hi, (x, n) in ((qA, qA, 0, q_hi_ready, where_q), (kB, kA, 1, k_hi_ready, where_k)):
                    for h in range(2):
                        rows = slice(64, 128) if wi == 0 else slice(0, 64)
                        dve.wait_ge(sem_hi, 2 * Pq + h + 1)
                        ins = v.scalar_tensor_tensor(dst[par][rows, h, :].rearrange("p (a n) -> p a n", a=2), work[x][64 * h:64 * h + 64, :, 0:HT],
                                                     b_scaled[64 * h:64 * h + 64, wi, bass.ds(pair, 1)],
                                                     hi[par][0:64, h, :].rearrange("p (a n) -> p a n", a=2), ALU.add, ALU.subtract)
                        ins.then_inc(work_free[x] if h else prep_chain, 1)
                v.tensor_copy(qB[par][0:64, :, :], qA[par][0:64, :, :]).then_inc(prep_chain, 1)
                v.tensor_copy(kA[par][64:128, :, :], kA[par][0:64, :, :]).then_inc(qk_ready, 1)

            def maximum(where, i):
                x, n = where
                dve.wait_ge(work_full[x], n)
                v.tensor_reduce(nmax[:, i:i + 1], work[x][:, :, 0:HT], op=ALU.max, axis=AX.XY, negate=True).then_inc(work_free[x], 1)

            def to_unit(last_where):
                x, n = last_where
                dve.wait_ge(work_free[x], n)
                v.tensor_scalar(nmax16[:, :], nmax[:, :], 1.0 / M_UNIT, None, ALU.mult).then_inc(nmax_ready, 1)

            def scale_output(b, s, where):
                x, n = where
                dve.wait_ge(work_full[x], n)
                v.reciprocal(inv[:, :, :], work[x][:, :, 0:HT]).then_inc(work_free[x], 1)
                dve.wait_ge(work_free[x], n)
                dve.wait_ge(av_saved, 8 * b + s)
                dve.wait_ge(o_lo_ready, 8 * b + s - 1)
                v.tensor_tensor(o_norm[:, :], o_raw[:, :, :].rearrange("p a n -> p (a n)"), inv[:, :, :].rearrange("p a n -> p (a n)"), ALU.mult).then_inc(o_normed, 1)

            def o_low(b, s):
                dve.wait_ge(o_hi_ready, 8 * b + s)
                one = lambda t: t[:, bass.ds(s - 1, 1), :].rearrange("p a t -> p (a t)")
                v.scalar_tensor_tensor(one(o_lo), o_norm[:, :], b_scaled[:, 2, bass.ds(s - 1, 1)], one(o_hi), ALU.add, ALU.subtract).then_inc(o_lo_ready, 1)

            def dve_slot(b, s, par, last):
                S = 8 * b + s
                nxt = not (last and isinstance(s, int) and s == 7)
                zero = isinstance(s, int) and s == 0
                other = 1 - par
                dve.wait_ge(av_done, 10 * S)
                if zero:
                    x, n = v_where(b)
                    dve.wait_ge(work_free[x], n)
                v.tensor_copy(v_pair[par][:, :, :], v_all[:, :, bass.ds(s * 128, 128)]).then_inc(v_staged, 1)
                if nxt and not zero:
                    low_parts(S + 1, n_work(b, s - 1, "Q"), n_work(b, s - 1, "K"), other, (s + 1) % 8)
                if not zero:
                    scale_output(b, s, n_work(b, s, "sum", last=last))
                if nxt:
                    for i in range(10):
                        maximum(n_work(b, s, "max", i, last), i)
                        if i == 1 and not zero:
                            o_low(b, s)
                    to_unit(n_work(b, s, "max", 9, last))
                elif not zero:
                    o_low(b, s)
            dve_slot.eng = dve

            def v_where(b):
                x, n = n_tail(b - 1, False, "V", 4)
                return x, n

            def dve_tail(b, last):
                if not last:
                    low_parts(8 * b + 9, n_work(b, 7, "Q"), n_work(b, 7, "K"), 1, 1)
                scale_output(b, 8, n_work(b, 8, "sum", last=last))
                o_low(b, 8)
                dve.wait_ge(h_loaded, 16 * (b + 1))
                for i in range(TT):
                    x, n = n_tail(b, last, "O", i)
                    dve.wait_ge(work_full[x], n)
                    v.scalar_tensor_tensor(h2[:, i, :], work[x][:, 0, 0:D], S_OUT, h2[:, i, :], ALU.mult, ALU.add).then_inc(work_free[x], 1)
                x, n = n_tail(b, last, "O", TT - 1)
                dve.wait_ge(work_free[x], n)
                row_stats(B + b, lambda j: h2[:, j, :])
                dve.wait_ge(work_full[1], slot_base(1, b, 0))
                normalise(xn2, lambda j: h2[:, j, :], xn2_ready)
                dve.wait_ge(xn2_ready, TT * (b + 1))
                v.tensor_reduce(xmax[:, bass.ds(b, 1)], xn2[:, :, :], op=ALU.max, axis=AX.XY, apply_absolute_value=True).then_inc(x2_max, 1)

            low_parts(0, n_start("Q", 0), n_start("K", 0), 0, 0)
            for i in range(10):
                maximum(n_start("max", i), i)
            to_unit(n_start("max", 9))
            low_parts(1, n_start("Q", 1), n_start("K", 1), 1, 1)
            with dve.Fori(0, B - 1) as b:
                slots(dve_slot, b, False)
                dve_tail(b, False)
            slots(dve_slot, B - 1, True)
            dve_tail(B - 1, True)

            scale_link = Ready(dve, scale_chain)

            def tensor_max(k, parts):
                for n, p in enumerate(parts):
                    ins = v.tensor_reduce(sc[:, 26 + n:27 + n], p, op=ALU.max, axis=AX.X)
                    if n < len(parts) - 1:
                        scale_link(ins, wait=False)
                ins.then_inc(red_ready, 1)
                dve.wait_ge(red_done, k + 1)
                return [sc[:, 18 + 2 * k + n:19 + 2 * k + n] for n in range(len(parts))]

            def quant_scale(top, unit, scale, mult):
                scale_link(v.tensor_scalar(S_TMP, top, unit, 1.0 / QMAX16, ALU.mult, ALU.mult))
                scale_link(v.tensor_scalar(scale, S_TMP, 1e-12, None, ALU.max))
                scale_link(v.reciprocal(S_ALL, scale))
                ins = v.tensor_scalar(mult, S_ALL, unit, None, ALU.mult)
                return ins

            dve.wait_ge(x2_max, B)
            top, = tensor_max(0, [xmax[:, :]])
            scale_link(v.tensor_scalar(S_X, top, 1.0 / QMAX16, 1e-12, ALU.mult, ALU.max))
            v.reciprocal(S_XI, S_X).then_inc(scales_ready, 1)
            dve.wait_ge(scales_ready, 1)
            for x, k in ((0, 4), (1, 3)):
                dve.wait_ge(work_free[x], n_tail(B - 1, True, "L", k)[1])

            def quantise_x(b, par):
                dve.wait_ge(xl_ready, b)
                dve.wait_ge(unit_done, 2 * FT * b)
                v.tensor_scalar(xq[:, :], X32[:, bass.ds(b * (XB // 2), KT * T)], S_XI, None, ALU.mult).then_inc(xq_chain, 1)
                dve.wait_ge(xq_chain, b + 1)
                flat = lambda t: t[par][:, :, :].rearrange("p k t -> p (k t)")
                v.tensor_copy(flat(xh), xq[:, :]).then_inc(xh_ready, 1)
                dve.wait_ge(xh_ready, b + 1)
                v.tensor_tensor(flat(xl), xq[:, :], flat(xh), ALU.subtract).then_inc(xl_ready, 1)

            def unit_maxima(b, ns):
                for n in ns:
                    f, w = divmod(n, 2)
                    dve.wait_ge(unit_copied, 2 * FT * b + n + 1)
                    src, dst = (ubuf[f % 4][:, :], umax) if w == 0 else (G[:, f, bass.ds(b * T, T)], gmax)
                    v.tensor_reduce(dst[:, bass.ds(b * FT + f, 1)], src, op=ALU.max, axis=AX.X, apply_absolute_value=True).then_inc(unit_max, 1)

            quantise_x(0, 0)
            with dve.Fori(0, B // 2 - 1) as bb:
                for par in range(2):
                    unit_maxima(2 * bb + par, range(FT))
                    quantise_x(2 * bb + par + 1, 1 - par)
                    unit_maxima(2 * bb + par, range(FT, 2 * FT))
            unit_maxima(B - 2, range(FT))
            quantise_x(B - 1, 1)
            unit_maxima(B - 2, range(FT, 2 * FT))
            unit_maxima(B - 1, range(2 * FT))

            dve.wait_ge(unit_max, 2 * FT * B)
            u_top, g_top = tensor_max(1, [umax[:, :], gmax[:, :]])
            for top, col, scale, mult in ((u_top, 4, S_U, S_UM), (g_top, 5, S_G, S_GM)):
                scale_link(v.scalar_tensor_tensor(S_RED, pow2[:, col:col + 1], 1.0 / W_SCALE, S_X, ALU.mult, ALU.mult))
                ins = quant_scale(top, S_RED, scale, mult)
                if col == 4:
                    scale_link(ins)
            ins.then_inc(scales_ready, 1)

            dve.sem_inc(p_ready, 2)
            with dve.Fori(0, NG // 2) as c:
                for k in range(2):
                    n = 2 * c + k
                    dve.wait_ge(sg_ready, n + 1)
                    dve.wait_ge(p_ready, n + 1)
                    v.tensor_scalar(sq[k][:, :], sg[k][:, :], 65536.0, None, ALU.mult).then_inc(sq_ready, 1)
                    dve.wait_ge(sq_ready, n + 1)
                    g = Gf[:, bass.ds(n * GC, GC)]
                    v.tensor_tensor(g, gq[k][:, :], sq[k][:, :], ALU.mult).then_inc(p_ready, 1)
                    dve.wait_ge(p_ready, n + 3)
                    v.tensor_reduce(pmax[:, bass.ds(n, 1)], g, op=ALU.max, axis=AX.X, apply_absolute_value=True).then_inc(p_max, 1)
            dve.wait_ge(p_max, NG)
            top, = tensor_max(2, [pmax[:, :]])
            scale_link(v.tensor_scalar(S_RED, S_G, 1.0 / 65536, None, ALU.mult))
            quant_scale(top, S_RED, S_T, S_TM).then_inc(scales_ready, 1)

            dve.sem_inc(t_ready, 2)
            with dve.Fori(0, NG // 2) as c:
                for k in range(2):
                    n = 2 * c + k
                    dve.wait_ge(tq_ready, n + 1)
                    dve.wait_ge(uq_ready, n + 1)
                    g = Gf[:, bass.ds(n * GC, GC)]
                    v.tensor_tensor(g, tq[k][:, :], uq[k][:, :], ALU.mult).then_inc(t_ready, 1)
                    dve.wait_ge(t_ready, n + 3)
                    v.tensor_reduce(omax[:, bass.ds(n, 1)], g, op=ALU.max, axis=AX.X, apply_absolute_value=True).then_inc(t_max, 1)
            dve.wait_ge(t_max, NG)
            top, = tensor_max(3, [omax[:, :]])
            scale_link(v.tensor_scalar(S_RED, S_T, S_U, None, ALU.mult))
            scale_link(quant_scale(top, S_RED, S_O, S_OM))
            v.scalar_tensor_tensor(S_Y, pow2[:, 6:7], 1.0 / W_SCALE, S_O, ALU.mult, ALU.mult).then_inc(scales_ready, 1)
            dve.wait_ge(scales_ready, 4)

            def quantise_o(n, k):
                dve.wait_ge(ol_ready, n)
                dve.wait_ge(y_done, DT * n)
                v.tensor_scalar(oq[:, :, :], G[:, :, bass.ds(n * DT * 128, DT * 128)], S_OM, None, ALU.mult).then_inc(oq_ready, 1)
                dve.wait_ge(oq_ready, n + 1)
                v.tensor_copy(oh[k][:, :, :], oq[:, :, :]).then_inc(oh_ready, 1)
                dve.wait_ge(oh_ready, n + 1)
                v.tensor_tensor(ol[k][:, :, :], oq[:, :, :], oh[k][:, :, :], ALU.subtract).then_inc(ol_ready, 1)

            def results(n, c, k):
                dve.wait_ge(hin_loaded[k], 16 * (c + 1))
                dve.wait_ge(out_stored[k], 16 * c)
                for j in range(DT):
                    dve.wait_ge(y_done, DT * (n + 1) + j + 1)
                    v.scalar_tensor_tensor(yout[k][:, j, :], ps[:, 4 * k + j, 0:D], S_Y, hin[k][:, j, :], ALU.mult, ALU.add).then_inc(y_ready, 1)

            dve.sem_inc(y_ready, DT)
            quantise_o(0, 0)
            with dve.Fori(0, ND // 2 - 1) as c:
                for k in range(2):
                    quantise_o(2 * c + k + 1, 1 - k)
                    results(2 * c + k, c, k)
            quantise_o(ND - 1, 1)
            results(ND - 2, ND // 2 - 1, 0)
            results(ND - 1, ND // 2 - 1, 1)


def kernel(**inputs):
    import numpy as np
    import concourse.bacc as bacc
    from concourse.bass_utils import run_bass_kernel_spmd

    n = {k: np.asarray(v) for k, v in inputs.items()}
    pairs = lambda b: b.reshape(PAIRS, 128).T
    arrays = {
        "x_t": n["x"].reshape(B, T_IMG // 128, 128, KT, 128, DC).transpose(0, 1, 4, 3, 5, 2),
        "txt": n["txt"],
        "tok_ws_t": n["L0_tok_weighted_sum"].T,
        "tok_w_t": n["L0_tok_weight"].T,
        "wq_t": n["L0_attn_W_Q"].reshape(HD, D).T,
        "wk_t": n["L0_attn_W_K"].reshape(HD, D).T,
        "wv_t": n["L0_attn_W_V"].reshape(HD, D).T,
        "wo_t": n["L0_attn_W_O"].transpose(0, 2, 1).reshape(HD, D),
        "bq": pairs(n["L0_attn_b_Q"]),
        "bk": pairs(n["L0_attn_b_K"]),
        "bv": pairs(n["L0_attn_b_V"]),
        "bo": n["L0_attn_b_O"],
        "w_up": n["L0_ffn_w_up"],
        "w_gate": n["L0_ffn_w_gate"],
        "w_down": n["L0_ffn_w_down"],
    }
    arrays = {k: np.ascontiguousarray(v) for k, v in arrays.items()}
    nc = bacc.Bacc("TRN2", target_bir_lowering=False, num_devices=1)
    args = [nc.dram_tensor(k, v.shape, mybir.dt.from_np(v.dtype), kind="ExternalInput").ap() for k, v in arrays.items()]
    out = nc.dram_tensor("out", (B, T, D), F32, kind="ExternalOutput").ap()
    build(nc, *args, out)
    r = run_bass_kernel_spmd(nc, [arrays], core_ids=[0])
    return r.results[0]["out"]
```

```python
import concourse.bass as bass
from concourse import mybir
from contextlib import ExitStack

F32, F16, I16, U16 = mybir.dt.float32, mybir.dt.float16, mybir.dt.int16, mybir.dt.uint16
I32, U32 = mybir.dt.int32, mybir.dt.uint32
ALU = mybir.AluOpType
ACT = mybir.ActivationFunctionType
AX = mybir.AxisListType
RMAX = bass.bass_isa.ReduceOp.max

B = 8
T_IMG, T_TXT = 512, 128
T = T_IMG + T_TXT
TT = T // 128
HT = T // 2
D = 256
KT = D // 128
DC = 4
HEADS, DH = 16, 64
HD = HEADS * DH
PAIRS = HEADS // 2
F = 768
FT = F // 128
BLK = 32
NBLK = FT * D // BLK
LN_EPS = 1e-5
QMAX16, QMAX4 = 32767.0, 7.0
W_SCALE = 8.0
M_UNIT = 32768.0
RING = 4
LEAD = 3
GC = 1024
NG = FT * B * T // GC
DT = 4
ND = B * TT // DT


class Ready:

    def __init__(self, eng, sem, base=0):
        self.eng, self.sem, self.base, self.n = eng, sem, base, 0

    def __call__(self, ins, wait=True):
        self.n += 1
        ins.then_inc(self.sem, 1)
        if wait:
            self.eng.wait_ge(self.sem, self.base + self.n)


def build(nc, xT, txt, ws, wb, wq, wk, wv, wo, bq, bk, bv, bo, w_up, w_gate, w_down, out):
    ctx = ExitStack()
    with ctx:
        sem = lambda name: ctx.enter_context(nc.semaphore(name))

        start = 16512
        end = 229344
        at = [start]

        def place(name, shape, dt, where=None):
            where = at if where is None else where
            n = mybir.dt.size(dt)
            for k in shape[1:]:
                n *= k
            t = nc.alloc_sbuf_tensor_at(name, shape, dt, offset=where[0])
            where[0] += -(-n // 32) * 32
            assert where[0] <= end, (name, where[0])
            return t

        ident = place("ident", [128, 128], F32)
        ident16 = place("ident16", [128, 128], F16)
        ones = place("ones", [128, 32], F32)
        bo_row = place("bo_row", [128, D], F32)
        b_raw = place("b_raw", [128, 3, PAIRS], F32)
        b_scaled = place("b_scaled", [128, 3, PAIRS], F32)
        b_second = place("b_second", [64, 2, PAIRS], F32)
        amax = place("amax", [128, 8], F32)
        bmax = place("bmax", [128, 3], F32)
        amax_all = place("amax_all", [128, 8], F32)
        pow2 = place("pow2", [128, 8], F32)
        wmul = place("wmul", [128, 8], F32)
        warm = place("warm", [128, 1], F32)
        sc = place("sc", [128, 32], F32)
        blk_max = place("blk_max", [128, 3, NBLK], F32)
        blk_s = place("blk_s", [128, 3, NBLK], F32)
        blk_r = place("blk_r", [128, 3, NBLK], F32)
        bn6 = place("bn6", [128, TT, 6], F32)
        bn2 = place("bn2", [128, TT, 2], F32)
        rs = place("rs", [128, 4, TT], F32)
        nmax = place("nmax", [128, 2 * TT], F32)
        nmax16 = place("nmax16", [128, 2 * TT], F16)
        xmax = place("xmax", [128, B], F32)
        umax = place("umax", [128, B * FT], F32)
        gmax = place("gmax", [128, B * FT], F32)
        pmax = place("pmax", [128, NG], F32)
        omax = place("omax", [128, NG], F32)
        ffn_hi = [place(f"{n}_hi", [128, KT * F], F16) for n in ("up", "gate", "down")]
        ffn_lo = [place(f"{n}_lo", [128, KT * F], F16) for n in ("up", "gate", "down")]
        XB = 2 * KT * T
        x_at = at[0]
        X = place("X", [128, B * XB], F16)
        X32 = nc.alloc_sbuf_tensor_at("X32", [128, B * XB // 2], F32, offset=x_at)
        stage_at = at[0]
        w_hi = [place(f"w{n}_hi", [128, KT, HD], F16) for n in "qkv"]
        w_lo = [place(f"w{n}_lo", [128, KT, HD], F16) for n in "qkv"]
        wo_hi = place("wo_hi", [128, PAIRS, D], F16)
        wo_lo = place("wo_lo", [128, PAIRS, D], F16)
        ab_at = at[0]

        a = [ab_at]
        h_all = place("h_all", [128, B * TT, D], F32, a)
        xbuf = [place(f"xbuf{i}", [128, KT, DC, 128], F32, a) for i in range(4)]
        xn = place("xn", [128, TT, D], F32, a)
        w2 = place("w2", [128, KT, DC, D], F32, a)
        w_raw = [place(f"w{n}_raw", [128, KT * HD], F32, a) for n in "qkv"]
        ffn_q = place("ffn_q", [128, KT * F], I16, a)
        late = [x_at + 4 * 2 * XB]
        ffn_raw = [place(f"{n}_raw", [128, KT * F], F32, late) for n in ("up", "gate", "down")]
        late = [x_at + 2 * 2 * XB]
        w_raw.append(place("wo_raw", [128, PAIRS * D], F32, late))
        ws_sb = place("ws_sb", [128, KT, D], F32, a)
        wb_sb = place("wb_sb", [128, DC, D], F32, a)

        a = [ab_at]
        v_all = place("v_all", [128, TT, HD], F32, a)
        qA = [place(f"qA{i}", [128, 2, T], F16, a) for i in range(2)]
        qB = [place(f"qB{i}", [128, 2, T], F16, a) for i in range(2)]
        kA = [place(f"kA{i}", [128, 2, T], F16, a) for i in range(2)]
        kB = [place(f"kB{i}", [128, 2, T], F16, a) for i in range(2)]
        v_pair = [place(f"v_pair{i}", [128, TT, 128], F32, a) for i in range(2)]
        probs = place("probs", [128, RING, 2, HT], F32, a)
        psum_p = place("psum_p", [128, 2, T], F32, a)
        o_raw = [place(f"o_raw{i}", [128, T], F32, a) for i in range(2)]
        sums = place("sums", [128, HT], F32, a)
        inv = place("inv", [128, HT], F32, a)
        o_norm = place("o_norm", [128, T], F32, a)
        o_hi = place("o_hi", [128, PAIRS, T], F16, a)
        o_lo = place("o_lo", [128, PAIRS, T], F16, a)
        h2 = place("h2", [128, TT, D], F32, a)
        xn2 = place("xn2", [128, TT, D], F32, a)

        a = [stage_at]
        G = place("G", [128, FT, B * T], F32, a)
        Gf = G[:, :, :].rearrange("p f t -> p (f t)")
        ubuf = [place(f"ubuf{i}", [128, T], F32, a) for i in range(4)]
        xq = place("xq", [128, KT * T], I16, a)
        xh = [place(f"xh{i}", [128, KT, T], F16, a) for i in range(2)]
        xl = [place(f"xl{i}", [128, KT, T], F16, a) for i in range(2)]
        a = [x_at]
        gq = [place(f"gq{i}", [128, GC], I16, a) for i in range(2)]
        sg = [place(f"sg{i}", [128, GC], F32, a) for i in range(2)]
        sq = [place(f"sq{i}", [128, GC], U16, a) for i in range(2)]
        uin = [place(f"uin{i}", [128, GC], F32, a) for i in range(2)]
        uq = [place(f"uq{i}", [128, GC], I16, a) for i in range(2)]
        tq = [place(f"tq{i}", [128, GC], I16, a) for i in range(2)]
        assert a[0] <= stage_at
        a = [x_at]
        oq = place("oq", [128, FT, DT * 128], I16, a)
        oh = [place(f"oh{i}", [128, FT, DT * 128], F16, a) for i in range(2)]
        ol = [place(f"ol{i}", [128, FT, DT * 128], F16, a) for i in range(2)]
        assert a[0] <= stage_at
        a = [stage_at + FT * B * T * 4]
        hin = [place(f"hin{i}", [128, DT, D], F32, a) for i in range(2)]
        yout = [place(f"yout{i}", [128, DT, D], F32, a) for i in range(2)]

        ps = ctx.enter_context(nc.psum_tensor("ps", [128, 8, 512], F32))
        work = [ps[:, 0:2, :], ps[:, 2:4, :]]
        score = [ps[:, 4, 0:HT], ps[:, 5, 0:HT]]
        av = ps[:, 6:8, 0:HT]
        v_bank = [ps[:, 4:6, :], ps[:, 6:8, :]]

        h_dram = nc.dram_tensor("h_scratch", [B, TT, 128, D], F32, kind="Internal").ap()
        u_dram = nc.dram_tensor("u_scratch", [128, FT * B * T], F32, kind="Internal").ap()

        S_SCORE, S_OUT, S_X, S_XI, S_U, S_UM, S_G, S_GM, S_T, S_TM, S_O, S_OM, S_Y, S_TMP, S_RED, S_ALL = (
            sc[:, i:i + 1] for i in range(16))

        ws_loaded, wb_loaded, attn_w_loaded, wo_loaded = sem("ws_loaded"), sem("wb_loaded"), sem("attn_w_loaded"), sem("wo_loaded")
        bias_loaded, ffn_w_loaded, txt_loaded = sem("bias_loaded"), sem("ffn_w_loaded"), sem("txt_loaded")
        x_loaded = [sem(f"x_loaded{i}") for i in range(4)]
        const_ready, ident_ready = sem("const_ready"), sem("ident_ready")
        w2_ready, tok_done, h_copied, xn_ready = sem("w2_ready"), sem("tok_done"), sem("h_copied"), sem("xn_ready")
        xt_done, x_hi_ready, x_lo_ready = sem("xt_done"), sem("x_hi_ready"), sem("x_lo_ready")
        bo_added, h_stored = sem("bo_added"), sem("h_stored")
        amax_ready, amax_reduced, wmul_ready = sem("amax_ready"), sem("amax_reduced"), sem("wmul_ready")
        w_hi_ready, w_lo_ready = sem("w_hi_ready"), sem("w_lo_ready")
        ffn_deq, ffn_t_done, ffn_hi_ready, ffn_lo_ready = sem("ffn_deq"), sem("ffn_t_done"), sem("ffn_hi_ready"), sem("ffn_lo_ready")
        vec_chain = sem("vec_chain")
        norm_chain = sem("norm_chain")
        work_full = [sem("work0_full"), sem("work1_full")]
        work_free = [sem("work0_free"), sem("work1_free")]
        score_ready, prob_ready, av_done, av_saved = sem("score_ready"), sem("prob_ready"), sem("av_done"), sem("av_saved")
        sum_done, q_hi_ready, k_hi_ready = sem("sum_done"), sem("q_hi_ready"), sem("k_hi_ready")
        prep_chain, qk_ready, nmax_ready, row_chain = sem("prep_chain"), sem("qk_ready"), sem("nmax_ready"), sem("row_chain")
        unit_ready, v_staged = sem("unit_ready"), sem("v_staged")
        v_projected, v_copied = sem("v_projected"), sem("v_copied")
        inverted, o_hi_ready, o_lo_ready = sem("inverted"), sem("o_hi_ready"), sem("o_lo_ready")
        h_loaded, h2_stored, xn2_ready, x2_max = sem("h_loaded"), sem("h2_stored"), sem("xn2_ready"), sem("x2_max")
        red_ready, red_done, scales_ready, scale_chain = sem("red_ready"), sem("red_done"), sem("scales_ready"), sem("scale_chain")
        xh_ready, xl_ready, xq_chain = sem("xh_ready"), sem("xl_ready"), sem("xq_chain")
        unit_done, unit_copied, unit_max, u_stored = sem("unit_done"), sem("unit_copied"), sem("unit_max"), [sem(f"u_stored{i}") for i in range(4)]
        gq_ready, sg_ready, sq_ready, p_ready, p_max = sem("gq_ready"), sem("sg_ready"), sem("sq_ready"), sem("p_ready"), sem("p_max")
        u_loaded = [sem("u_loaded0"), sem("u_loaded1")]
        uq_ready, tq_ready, t_ready, t_max = sem("uq_ready"), sem("tq_ready"), sem("t_ready"), sem("t_max")
        oq_ready, oh_ready, ol_ready, y_done, y_ready = sem("oq_ready"), sem("oh_ready"), sem("ol_ready"), sem("y_done"), sem("y_ready")
        hin_loaded = [sem("hin_loaded0"), sem("hin_loaded1")]
        out_stored = [sem("out_stored0"), sem("out_stored1")]

        def n_prob(S, u, h):
            return 20 * (S + 1) + 2 * u + h + 1

        def n_av(S, u):
            return 10 * (S + 1) + u + 1

        def n_sum(S, u, h=1):
            half, j = divmod(u, TT)
            return 16 * (S + 1) + half * 8 + (max(j, 1) - 1) * 2 + h + 1

        def back(S, u, n):
            return (S, u - n) if u >= n else (S - 1, u - n + 10)

        START = [("Q", 0, 0), ("K", 0, 1)] + [("max", k, (1 + k) % 2) for k in range(10)] + [("row", 0, 1), ("Q", 1, 0)]
        TAIL = [("inv", 0, 1), ("sum", 0, 0), ("inv", 1, 0), ("O", 0, 1), ("O", 1, 0), ("O", 2, 1), ("O", 3, 0), ("O", 4, 1),
                ("L", 0, 0), ("L", 1, 1), ("L", 2, 0), ("L", 3, 1), ("L", 4, 0)]

        def counted(order, x, upto=None):
            n = 0
            for name, k, y in order:
                n += x == y
                if (name, k) == upto:
                    break
            return n

        def finishing(s):
            return min(s, 2) if isinstance(s, int) else 2

        def slot_base(x, b, s, last=False):
            per_slot = 8 if x == 0 else 7
            short = (3 if x == 0 else 0)
            per_batch = 8 * per_slot - short + counted(TAIL, x)
            skipped = (0 if s < 7 else (1 - x if s == 7 else 7)) if last else 0
            before = (0, 6)[s] if x == 0 and isinstance(s, int) and s < 2 else per_slot * s - short
            return counted(START, x) + per_batch * b + before - skipped

        def n_work(b, s, use, i=0, last=False):
            x0, x1 = slot_base(0, b, s, last), slot_base(1, b, s, last)
            if use == "sum":
                return 0, x0 + 1
            if use == "inv":
                return 0, x0 + 2
            if use == "max":
                return (0, x0 + finishing(s) + (i + 1) // 2) if i % 2 else (1, x1 + i // 2 + 2)
            if use == "row":
                return 1, x1 + 7
            if use == "Q":
                return 0, x0 + finishing(s) + 6
            return 1, x1 + 1

        def n_tail(b, last, use, i):
            x = {(name, k): y for name, k, y in TAIL}[use, i]
            return x, slot_base(x, b, 8, last) + counted(TAIL, x, (use, i))

        def n_start(use, i=0):
            x = {(name, k): y for name, k, y in START}[use, i]
            return x, counted(START, x, (use, i))

        TAIL_AFTER_SUM = counted(TAIL, 0) - counted(TAIL, 0, ("sum", 0))

        def slots(body, b, last):
            eng = body.eng
            body(b, 0, 0, False)
            body(b, 1, 1, False)
            with eng.Fori(0, 2) as g:
                body(b, 2 + 2 * g, 0, False)
                body(b, 3 + 2 * g, 1, False)
            body(b, 6, 0, last)
            body(b, 7, 1, last)

        block = ctx.enter_context(nc.Block())

        @block.sync
        def _(sp):
            sp.dma_start(ws_sb[:, :, :], ws.rearrange("(k p) o -> p k o", p=128)).then_inc(ws_loaded, 16)
            sp.dma_start(wb_sb[:, :, :], wb.rearrange("d o -> (d o)").unsqueeze(0).to_broadcast([128, DC * D]).rearrange("p (d o) -> p d o", d=DC)
                         ).then_inc(wb_loaded, 16)
            for i in range(4):
                sp.dma_start(xbuf[i][:, :, :, :], xT[0, i]).then_inc(x_loaded[i], 16)
            with sp.Fori(1, B) as b:
                for i in range(4):
                    sp.wait_ge(tok_done, 4 * (b - 1) + i + 1)
                    sp.dma_start(xbuf[i][:, :, :, :], xT[bass.ds(b, 1), i].rearrange("a p k d t -> (a p) k d t")
                                 ).then_inc(x_loaded[i], 16)
            sp.wait_ge(h_stored, 16 * B)
            sp.wait_ge(work_full[0], 1)
            with sp.Fori(0, B) as b:
                sp.wait_ge(h2_stored, 16 * b)
                sp.dma_start(h2[:, :, :], h_dram[bass.ds(b, 1)].rearrange("a j p d -> p (a j) d")).then_inc(h_loaded, 16)
                sp.wait_ge(xn2_ready, TT * (b + 1))
                sp.dma_start(h_dram[bass.ds(b, 1)].rearrange("a j p d -> p (a j) d"), h2[:, :, :]).then_inc(h2_stored, 16)
            with sp.Fori(0, B) as b:
                for f in range(FT):
                    sp.wait_ge(unit_copied, 12 * b + 2 * f + 1)
                    sp.dma_start(u_dram[:, bass.ds(b * T + f * B * T, T)], ubuf[f % 4][:, :]
                                 ).then_inc(u_stored[f % 4], 16)
            for k in range(4):
                sp.wait_ge(u_stored[k], 16 * (B * (2 if k < 2 else 1)))
            sp.wait_ge(xl_ready, B)
            for k in range(2):
                sp.dma_start(uin[k][:, :], u_dram[:, k * GC:(k + 1) * GC]).then_inc(u_loaded[k], 16)
            with sp.Fori(1, NG // 2) as c:
                for k in range(2):
                    sp.wait_ge(uq_ready, 2 * (c - 1) + k + 1)
                    sp.dma_start(uin[k][:, :], u_dram[:, bass.ds(c * 2 * GC + k * GC, GC)]).then_inc(u_loaded[k], 16)
            hd = h_dram.rearrange("b j p d -> (b j) p d")
            sp.wait_ge(scales_ready, 2)
            sp.wait_ge(h2_stored, 16 * B)
            with sp.Fori(0, ND // 2) as c:
                for k in range(2):
                    sp.wait_ge(y_ready, DT * (2 * c + k))
                    sp.dma_start(hin[k][:, :, :], hd[bass.ds(c * 2 * DT + k * DT, DT)].rearrange("j p d -> p j d")
                                 ).then_inc(hin_loaded[k], 16)

        @block.gpsimd
        def _(pool):
            pool.memset(ident[:, :], 0.0).then_inc(const_ready, 1)
            pool.memset(ident16[:, :], 0.0).then_inc(const_ready, 1)
            pool.wait_ge(const_ready, 2)
            for m in (ident, ident16):
                pool.affine_select(out=m[:, :], in_=m[:, :], compare_op=ALU.not_equal, fill=1.0, base=0,
                                   pattern=[[-1, 128]], channel_multiplier=1).then_inc(ident_ready, 1)
            pool.wait_ge(amax_ready, 1)
            pool.partition_all_reduce(amax_all[:, 0:7], amax[:, 0:7], 128, RMAX).then_inc(amax_reduced, 1)
            bo_b = bo_row[:, :].unsqueeze(1).to_broadcast([128, TT, D])
            pool.wait_ge(bias_loaded, 96)
            with pool.Fori(0, B) as b:
                pool.wait_ge(xn_ready, TT * (b + 1))
                hb = h_all[:, bass.ds(b * TT, TT), :]
                pool.tensor_tensor(hb, hb, bo_b, ALU.add).then_inc(bo_added, 1)
                pool.wait_ge(bo_added, b + 1)
                pool.dma_start(h_dram[bass.ds(b, 1)].rearrange("a j p d -> p (a j) d"), hb).then_inc(h_stored, 16)
            pool.wait_ge(h_stored, 16 * B)
            pool.wait_ge(work_full[0], 1)
            pool.sem_inc(sum_done, 16)

            def pool_slot(b, s, par, last):
                S = 8 * b + s
                for half in range(2):
                    for j in range(1, TT):
                        for h in range(2):
                            u = half * TT + j
                            dst = psum_p[:, h, half * HT:(half + 1) * HT]
                            pool.wait_ge(prob_ready, n_prob(S, u, h))
                            if j == 1:
                                if half == 0 and h == 0:
                                    if isinstance(s, int) and s == 0:
                                        pool.wait_ge(work_full[0], slot_base(0, b, 0) - TAIL_AFTER_SUM)
                                    else:
                                        pool.wait_ge(work_full[0], n_work(b, s, "sum", last=last)[1])
                                src = probs[:, (10 * par + u - 1) % RING, h, :]
                            else:
                                pool.wait_ge(sum_done, n_sum(S, u - 1, h))
                                src = dst
                            pool.tensor_tensor(dst, src, probs[:, (10 * par + u) % RING, h, :], ALU.add).then_inc(sum_done, 1)
            pool_slot.eng = pool
            with pool.Fori(0, B - 1) as b:
                slots(pool_slot, b, False)
            slots(pool_slot, B - 1, True)
            for k in range(4):
                pool.wait_ge(red_ready, k + 1)
                width = 2 if k == 1 else 1
                pool.partition_all_reduce(sc[:, 18 + 2 * k:18 + 2 * k + width], sc[:, 26:26 + width], 128, RMAX).then_inc(red_done, 1)

        @block.tensor
        def _(pe):
            mm = nc.tensor.matmul

            def tok(b, i):
                pe.wait_ge(x_loaded[i], 16 * (b + 1))
                pe.wait_ge(h_copied, 4 * b + i + 1)
                for n in range(KT * DC):
                    k, d = divmod(n, DC)
                    last = mm(ps[:, i, 0:D], xbuf[i][:, k, d, :], w2[:, k, d, :], start=n == 0, stop=n == KT * DC - 1)
                last.then_inc(tok_done, 1)

            def xn_transposes(b):
                for i in range(TT):
                    pe.wait_ge(xn_ready, TT * b + i + 1)
                    pe.wait_ge(x_lo_ready, TT * b + (1 if i == 4 else 0))
                    for k in range(KT):
                        last = nc.tensor.transpose(ps[:, 4 + i % 4, k * 128:(k + 1) * 128], xn[:, i, k * 128:(k + 1) * 128], ident[:, :])
                    last.then_inc(xt_done, 1)

            pe.wait_ge(w2_ready, KT)
            pe.wait_ge(ident_ready, 2)
            with pe.Fori(0, LEAD) as b:
                for i in range(4):
                    tok(b, i)
            for w in range(3):
                pe.wait_ge(ffn_deq, w + 1)
                for g in range(2):
                    n = 2 * w + g
                    bank = 4 + 2 * (n % 2)
                    if n >= 2:
                        pe.wait_ge(ffn_lo_ready, 2 * (n - 1))
                    for m in range(6):
                        if w < 2:
                            src = ffn_raw[w][:, m * D + g * 128:m * D + (g + 1) * 128]
                            dst = ps[:, bank + m // 3, (m % 3) * 128:(m % 3 + 1) * 128]
                        else:
                            dt_, f = divmod(m, 3)
                            src = ffn_raw[w][:, dt_ * F + (3 * g + f) * 128:dt_ * F + (3 * g + f + 1) * 128]
                            dst = ps[:, bank + dt_, f * 128:(f + 1) * 128]
                        last = nc.tensor.transpose(dst, src, ident[:, :])
                    last.then_inc(ffn_t_done, 1)
            pe.wait_ge(ffn_lo_ready, 12)
            with pe.Fori(0, B - LEAD) as b:
                for i in range(4):
                    tok(b + LEAD, i)
                xn_transposes(b)
            with pe.Fori(B - LEAD, B) as b:
                xn_transposes(b)

            def use(where, fill):
                x, n = where
                pe.wait_ge(work_free[x], n - 1)
                fill(work[x]).then_inc(work_full[x], 1)

            def project(wi, bb, pair):
                def fill(w):
                    n = 0
                    for k in range(KT):
                        for wt, xs in ((w_hi[wi], (0, 1)), (w_lo[wi], (0,))):
                            lhsT = wt[:, k, bass.ds(pair * 128, 128)]
                            for xp in xs:
                                for half in range(2):
                                    last = mm(w[:, half, 0:HT], lhsT, X[:, bass.ds(bb * XB + (xp * KT + k) * T + half * HT, HT)],
                                              start=n < 2, stop=n >= 10)
                                    n += 1
                    return last
                return fill

            def project_v(bb, j):
                if j > 1:
                    pe.wait_ge(v_copied, TT * bb + j - 1)
                n = 0
                for k in range(KT):
                    for xp, wt in ((0, w_hi[2]), (0, w_lo[2]), (1, w_hi[2])):
                        lhsT = X[:, bass.ds(bb * XB + (xp * KT + k) * T + j * 128, 128)]
                        for c in range(2):
                            last = mm(v_bank[j % 2][:, c, :], lhsT, wt[:, k, c * 512:(c + 1) * 512], start=n < 2, stop=n >= 10)
                            n += 1
                last.then_inc(v_projected, 1)

            def max_tile(par, i):
                def fill(w):
                    t, h = divmod(i, 2)
                    for half in range(2):
                        last = mm(w[:, half, 0:HT], qA[par][:, h, t * 128:(t + 1) * 128], kA[par][:, h, half * HT:(half + 1) * HT],
                                  start=True, stop=True)
                    return last
                return fill

            def max_row(w):
                flat = w.rearrange("p a n -> p (a n)")
                for h in range(2):
                    for t in range(TT):
                        last = mm(flat[64 + 32 * h:65 + 32 * h, t * 128:(t + 1) * 128], nmax16[:, 2 * t + h:2 * t + h + 1], ident16[:, :],
                                  start=True, stop=True)
                return last

            def sum_rows(w):
                for i in range(4):
                    h, half = divmod(i, 2)
                    last = mm(w[32 * i:32 * i + 32, 0, 0:HT], ones[:, :], psum_p[:, h, half * HT:(half + 1) * HT], start=True, stop=True)
                return last

            def spread_inv(w):
                for half in range(2):
                    for h in range(2):
                        row = 32 * (2 * h + half)
                        last = mm(w[64 * h:64 * h + 64, half, 0:HT], ident[:, row:row + 1].to_broadcast([128, DH]), inv[:, :], start=True, stop=True)
                return last

            def out_tile(j):
                def fill(w):
                    n = 0
                    for p in range(PAIRS):
                        for ot, wt in ((o_hi, wo_hi), (o_hi, wo_lo), (o_lo, wo_hi)):
                            last = mm(w[:, 0, 0:D], ot[:, p, j * 128:(j + 1) * 128], wt[:, p, :], start=n == 0, stop=n == 3 * PAIRS - 1)
                            n += 1
                    return last
                return fill

            def xn2_tile(j):
                def fill(w):
                    for k in range(KT):
                        last = nc.tensor.transpose(w[:, 0, k * 128:(k + 1) * 128], xn2[:, j, k * 128:(k + 1) * 128], ident[:, :])
                    return last
                return fill

            def attend(S, par, u):
                half, j = divmod(u, TT)
                if u == 0:
                    pe.wait_ge(v_staged, S + 1)
                    pe.wait_ge(av_saved, S)
                pe.wait_ge(prob_ready, n_prob(S, u, 1))
                for h in range(2):
                    last = mm(av[64 * h:64 * h + 64, half, :], v_pair[par][:, j, 64 * h:64 * h + 64],
                              probs[:, (10 * par + u) % RING, h, :], start=j == 0, stop=j == TT - 1)
                last.then_inc(av_done, 1)

            def pe_slot(b, s, par, last):
                S = 8 * b + s
                nxt = not (last and isinstance(s, int) and s == 7)
                ahead = nxt and not (last and isinstance(s, int) and s == 6)
                finish = not (isinstance(s, int) and s == 0)
                other = 1 - par

                def maximum_of(i):
                    if nxt and 0 <= i < 10:
                        use(n_work(b, s, "max", i, last), max_tile(other, i))

                if finish:
                    pe.wait_ge(work_free[1], n_work(b, s - 1, "row", last=last)[1])
                else:
                    pe.wait_ge(v_copied, TT * (b + 1))
                for u in range(10):
                    half, j = divmod(u, TT)
                    for h in range(2):
                        pe.wait_ge(prob_ready, n_prob(*back(S, u, 1), h))
                        mm(score[h], kA[par][:, h, j * 128:(j + 1) * 128], qA[par][:, h, half * HT:(half + 1) * HT], start=True, stop=False)
                        mm(score[h], kB[par][0:65, h, j * 128:(j + 1) * 128], qB[par][0:65, h, half * HT:(half + 1) * HT],
                           start=False, stop=True).then_inc(score_ready, 1)
                    if u == 0 and nxt:
                        use(n_work(b, s, "K", last=last), project(1, b + (s + 1) // 8, (s + 1) % 8))
                    if u == 1 and finish:
                        pe.wait_ge(sum_done, 16 * (S + 1))
                        use(n_work(b, s, "sum", last=last), sum_rows)
                    if u == 2 and finishing(s) == 2:
                        pe.wait_ge(inverted, S - 1)
                        use(n_work(b, s, "inv", last=last), spread_inv)
                    if u == 3 and nxt:
                        pe.wait_ge(qk_ready, S + 2)
                    maximum_of(2 * (u - 3))
                    if u >= 2:
                        attend(S, par, u - 2)
                    elif finish:
                        attend(S - 1, other, 8 + u)
                    maximum_of(2 * (u - 3) + 1)
                    if u == 8 and nxt:
                        pe.wait_ge(nmax_ready, S + 2)
                        use(n_work(b, s, "row", last=last), max_row)
                if ahead:
                    use(n_work(b, s, "Q", last=last), project(0, b + (s + 2) // 8, (s + 2) % 8))
            pe_slot.eng = pe

            def pe_tail(b, last):
                attend(8 * b + 7, 1, 8)
                attend(8 * b + 7, 1, 9)
                pe.wait_ge(inverted, 8 * b + 7)
                use(n_tail(b, last, "inv", 0), spread_inv)
                if not last:
                    project_v(b + 1, 0)
                pe.wait_ge(sum_done, 16 * (8 * b + 9))
                use(n_tail(b, last, "sum", 0), sum_rows)
                if not last:
                    pe.wait_ge(av_saved, 8 * (b + 1))
                    project_v(b + 1, 1)
                pe.wait_ge(inverted, 8 * b + 8)
                use(n_tail(b, last, "inv", 1), spread_inv)
                if not last:
                    project_v(b + 1, 2)
                pe.wait_ge(o_lo_ready, 8 * (b + 1))
                for i in range(TT):
                    use(n_tail(b, last, "O", i), out_tile(i))
                if not last:
                    project_v(b + 1, 3)
                    project_v(b + 1, 4)
                for i in range(TT):
                    pe.wait_ge(xn2_ready, TT * b + i + 1)
                    use(n_tail(b, last, "L", i), xn2_tile(i))

            pe.wait_ge(x_lo_ready, TT * B)
            pe.wait_ge(x_hi_ready, TT * B)
            pe.wait_ge(w_lo_ready, 4)
            pe.sem_inc(av_done, 10)
            pe.wait_ge(unit_ready, 2)
            use(n_start("Q", 0), project(0, 0, 0))
            use(n_start("K", 0), project(1, 0, 0))
            for j in range(TT):
                project_v(0, j)
            pe.wait_ge(qk_ready, 1)
            for i in range(10):
                use(n_start("max", i), max_tile(0, i))
            pe.wait_ge(nmax_ready, 1)
            use(n_start("row"), max_row)
            use(n_start("Q", 1), project(0, 0, 1))
            pe.wait_ge(work_free[1], n_start("row")[1])
            with pe.Fori(0, B - 1) as b:
                slots(pe_slot, b, False)
                pe_tail(b, False)
            slots(pe_slot, B - 1, True)
            pe_tail(B - 1, True)

            pe.sem_inc(unit_done, 2 * FT)
            pe.sem_inc(y_done, DT)
            pe.wait_ge(work_free[0], n_tail(B - 1, True, "L", 4)[1])
            pe.wait_ge(work_free[1], n_tail(B - 1, True, "L", 3)[1])
            with pe.Fori(0, B // 2) as bb:
                for par in range(2):
                    b = 2 * bb + par
                    pe.wait_ge(xh_ready, b + 1)
                    pe.wait_ge(xl_ready, b + 1)
                    for n in range(2 * FT):
                        f, w = divmod(n, 2)
                        if n < 4 and par == 0:
                            pe.wait_ge(unit_copied, 12 * b)
                        else:
                            pe.wait_ge(unit_copied, 12 * b + n - 3)
                        u = ps[:, 2 * (n % 4):2 * (n % 4) + 2, :]
                        m = 0
                        for k in range(KT):
                            for wt, xs in ((ffn_hi[w], (xh, xl)), (ffn_lo[w], (xh,))):
                                for xp in xs:
                                    for half in range(2):
                                        last = mm(u[:, half, 0:HT], wt[:, k * F + f * 128:k * F + (f + 1) * 128],
                                                  xp[par][:, k, half * HT:(half + 1) * HT], start=m < 2, stop=m >= 10)
                                        m += 1
                        last.then_inc(unit_done, 1)
            with pe.Fori(0, ND // 2) as c:
                for k in range(2):
                    n = 2 * c + k
                    pe.wait_ge(ol_ready, n + 1)
                    for j in range(DT):
                        pe.wait_ge(y_ready, DT * n)
                        m = 0
                        for f in range(FT):
                            for ot, wt in ((oh, ffn_hi[2]), (oh, ffn_lo[2]), (ol, ffn_hi[2])):
                                last = mm(ps[:, 4 * k + j, 0:D], ot[k][:, f, j * 128:(j + 1) * 128], wt[:, f * D:(f + 1) * D],
                                          start=m == 0, stop=m == 3 * FT - 1)
                                m += 1
                        last.then_inc(y_done, 1)

        @block.scalar
        def _(act):
            fn = nc.scalar.activation
            for i, w in enumerate((wq, wk, wv)):
                act.dma_start(w_raw[i][:, :].rearrange("p (k n) -> p k n", k=KT), w.rearrange("(k p) n -> p k n", p=128)).then_inc(attn_w_loaded, 16)
            act.dma_start(w_raw[3][:, :].rearrange("p (k n) -> p k n", k=PAIRS), wo.rearrange("(k p) n -> p k n", p=128)).then_inc(wo_loaded, 16)
            for i, bias in enumerate((bq, bk, bv)):
                act.dma_start(b_raw[:, i, :], bias).then_inc(bias_loaded, 16)
                if i < 2:
                    act.dma_start(b_second[:, i, :], bias[64:128, :]).then_inc(bias_loaded, 16)
            act.dma_start(bo_row[:, :], bo.unsqueeze(0).to_broadcast([128, D])).then_inc(bias_loaded, 16)
            for i, w in enumerate((w_up, w_gate, w_down)):
                act.dma_start(ffn_raw[i][:, :].rearrange("p (k n) -> p k n", k=(FT, FT, KT)[i]), w.rearrange("(k p) n -> p k n", p=128)).then_inc(ffn_w_loaded, 16)
            for b in range(B):
                act.dma_start(h_all[:, b * TT + TT - 1, :], txt[b]).then_inc(txt_loaded, 16)

            def copy_h(b):
                for i in range(4):
                    act.wait_ge(tok_done, 4 * b + i + 1)
                    fn(h_all[:, bass.ds(b * TT + i, 1), :].rearrange("p a d -> p (a d)"), ps[:, i, 0:D], ACT.Copy).then_inc(h_copied, 1)

            def split_x(b):
                for i in range(TT):
                    act.wait_ge(xt_done, TT * b + i + 1)
                    dst = X[:, bass.ds(b * XB, KT * T)].rearrange("p (k t) -> p k t", k=KT)[:, :, i * 128:(i + 1) * 128]
                    fn(dst, ps[:, 4 + i % 4, 0:D].rearrange("p (k t) -> p k t", k=KT), ACT.Copy).then_inc(x_hi_ready, 1)

            act.sem_inc(h_copied, 4)
            with act.Fori(0, LEAD) as b:
                copy_h(b)
            act.wait_ge(wmul_ready, 1)
            for i in range(4):
                dst = w_hi[i][:, :, :].rearrange("p k n -> p (k n)") if i < 3 else wo_hi[:, :, :].rearrange("p k n -> p (k n)")
                fn(dst, w_raw[i][:, :], ACT.Copy, scale=wmul[:, i:i + 1]).then_inc(w_hi_ready, 1)
            for w in range(3):
                for g in range(2):
                    n = 2 * w + g
                    bank = 4 + 2 * (n % 2)
                    act.wait_ge(ffn_t_done, n + 1)
                    for m in range(2):
                        if w < 2:
                            dst = ffn_hi[w][:, g * F + m * 384:g * F + (m + 1) * 384]
                            src = ps[:, bank + m, 0:384]
                        else:
                            dst = ffn_hi[w][:, :].rearrange("p (f n) -> p f n", n=D)[:, 3 * g:3 * g + 3, m * 128:(m + 1) * 128]
                            src = ps[:, bank + m, 0:384].rearrange("p (f n) -> p f n", n=128)
                        fn(dst, src, ACT.Copy, scale=wmul[:, 4 + w:5 + w]).then_inc(ffn_hi_ready, 1)
            act.wait_ge(w_lo_ready, 4)
            with act.Fori(0, B - LEAD) as b:
                copy_h(b + LEAD)
                split_x(b)
            with act.Fori(B - LEAD, B) as b:
                split_x(b)

            act.wait_ge(x_lo_ready, TT * B)
            act.wait_ge(h_stored, 16 * B)
            act.sem_inc(prob_ready, 20)

            def hi_part(dst, wi, sem_hi, where, P, pair, par):
                x, n = where
                act.wait_ge(work_full[x], n)
                for h in range(2):
                    fn(dst[par][0:64, h, :].rearrange("p (a n) -> p a n", a=2), work[x][64 * h:64 * h + 64, :, 0:HT], ACT.Identity,
                       bias=b_scaled[64 * h:64 * h + 64, wi, bass.ds(pair, 1)]).then_inc(sem_hi, 1)

            def move_rows(where, par):
                x, n = where
                act.wait_ge(work_full[x], n)
                for h in range(2):
                    flat = work[x].rearrange("p a n -> p (a n)")
                    ins = fn(qB[par][64:65, h, :], flat[64 + 32 * h:65 + 32 * h, 0:T], ACT.Copy)
                    ins.then_inc(work_free[x] if h else row_chain, 1)

            def copy_v(bb, j):
                act.wait_ge(v_projected, TT * bb + j + 1)
                fn(v_all[:, j, :], v_bank[j % 2].rearrange("p a n -> p (a n)"), ACT.Copy).then_inc(v_copied, 1)

            def o_high(b, pair, where):
                x, n = where
                act.wait_ge(work_free[x], n)
                act.wait_ge(work_full[1], slot_base(1, b, 0) - 2)
                fn(o_hi[:, bass.ds(pair, 1), :].rearrange("p a t -> p (a t)"), o_norm[:, :], ACT.Identity,
                   bias=b_scaled[:, 2, bass.ds(pair, 1)]).then_inc(o_hi_ready, 1)

            def copy_sums(S, where):
                x, n = where
                act.wait_ge(inverted, S)
                act.wait_ge(work_full[x], n)
                fn(sums[:, :], work[x][:, 0, 0:HT], ACT.Copy).then_inc(work_free[x], 1)

            def save_output(S, par):
                act.wait_ge(av_done, n_av(S, 9))
                fn(o_raw[par][:, :].rearrange("p (a n) -> p a n", a=2), av, ACT.Copy).then_inc(av_saved, 1)

            def stage_v(S, pair, par):
                act.wait_ge(av_done, 10 * S)
                act.wait_ge(v_copied, TT * (S // 8 + 1))
                fn(v_pair[par][:, :, :], v_all[:, :, bass.ds(pair * 128, 128)], ACT.Copy).then_inc(v_staged, 1)

            def act_slot(b, s, par, last):
                S = 8 * b + s
                nxt = not (last and isinstance(s, int) and s == 7)
                ahead = nxt and not (last and isinstance(s, int) and s == 6)
                finish = not (isinstance(s, int) and s == 0)
                other = 1 - par
                for u in range(10):
                    act.wait_ge(av_done, n_av(*back(S, u, RING)))
                    act.wait_ge(sum_done, n_sum(*back(S, u, RING)))
                    for h in range(2):
                        act.wait_ge(score_ready, 20 * S + 2 * u + h + 1)
                        fn(probs[:, (10 * par + u) % RING, h, :], score[h], ACT.Exp, scale=S_SCORE).then_inc(prob_ready, 1)
                    if u == 0 and nxt:
                        hi_part(kA, 1, k_hi_ready, n_work(b, s, "K", last=last), S + 1, (s + 1) % 8, other)
                    if u == 1 and finish:
                        copy_sums(S - 1, n_work(b, s, "sum", last=last))
                        save_output(S - 1, other)
                    if u == 5 and not (isinstance(s, int) and s == 7):
                        stage_v(S + 1, s + 1, other)
                    if u == 4 and finishing(s) == 2:
                        o_high(b, s - 2, n_work(b, s, "inv", last=last))
                    if u == 8 and nxt:
                        move_rows(n_work(b, s, "row", last=last), other)
                if ahead:
                    hi_part(qA, 0, q_hi_ready, n_work(b, s, "Q", last=last), S + 2, (s + 2) % 8, par)
            act_slot.eng = act

            def act_tail(b, last):
                save_output(8 * b + 7, 1)
                o_high(b, 6, n_tail(b, last, "inv", 0))
                if not last:
                    act.wait_ge(v_staged, 8 * (b + 1))
                    copy_v(b + 1, 0)
                copy_sums(8 * b + 7, n_tail(b, last, "sum", 0))
                if not last:
                    copy_v(b + 1, 1)
                o_high(b, 7, n_tail(b, last, "inv", 1))
                if not last:
                    for j in range(2, TT):
                        copy_v(b + 1, j)
                    stage_v(8 * (b + 1), 0, 0)
                for i in range(TT):
                    x, n = n_tail(b, last, "L", i)
                    act.wait_ge(work_full[x], n)
                    dst = X32[:, bass.ds(b * (XB // 2), KT * T)].rearrange("p (k t) -> p k t", k=KT)[:, :, i * 128:(i + 1) * 128]
                    fn(dst, work[x][:, 0, 0:D].rearrange("p (k t) -> p k t", k=KT), ACT.Copy).then_inc(work_free[x], 1)

            hi_part(qA, 0, q_hi_ready, n_start("Q", 0), 0, 0, 0)
            hi_part(kA, 1, k_hi_ready, n_start("K", 0), 0, 0, 0)
            for j in range(TT):
                copy_v(0, j)
            stage_v(0, 0, 0)
            move_rows(n_start("row"), 0)
            hi_part(qA, 0, q_hi_ready, n_start("Q", 1), 1, 1, 1)
            with act.Fori(0, B - 1) as b:
                slots(act_slot, b, False)
                act_tail(b, False)
            slots(act_slot, B - 1, True)
            act_tail(B - 1, True)

            act.wait_ge(h2_stored, 16 * B)
            with act.Fori(0, B) as b:
                for n in range(2 * FT):
                    f, w = divmod(n, 2)
                    act.wait_ge(unit_done, 2 * FT * (b + 1) + n + 1)
                    src = ps[:, 2 * (n % 4):2 * (n % 4) + 2, 0:HT]
                    if w == 0:
                        act.wait_ge(u_stored[f % 4], 16 * (b * (2 if f % 4 < 2 else 1) + f // 4))
                        act.wait_ge(unit_max, 12 * b + (n - 7 if n >= 8 else 0))
                        dst = ubuf[f % 4][:, :]
                    else:
                        dst = G[:, f, bass.ds(b * T, T)]
                    fn(dst.rearrange("p (a n) -> p a n", a=2), src, ACT.Copy).then_inc(unit_copied, 1)
            act.wait_ge(scales_ready, 2)
            fn(warm[:, :], ones[:, 0:1], ACT.Sigmoid)
            with act.Fori(0, NG // 2) as c:
                for k in range(2):
                    n = 2 * c + k
                    act.wait_ge(p_ready, n + 1)
                    fn(gq[k][:, :], Gf[:, bass.ds(n * GC, GC)], ACT.Copy, scale=S_GM).then_inc(gq_ready, 1)
                    act.wait_ge(gq_ready, n + 1)
                    fn(sg[k][:, :], gq[k][:, :], ACT.Sigmoid, scale=S_G).then_inc(sg_ready, 1)
            act.wait_ge(scales_ready, 3)
            with act.Fori(0, NG // 2) as c:
                for k in range(2):
                    n = 2 * c + k
                    act.wait_ge(t_ready, n + 1)
                    fn(tq[k][:, :], Gf[:, bass.ds(n * GC, GC)], ACT.Copy, scale=S_TM).then_inc(tq_ready, 1)
                    act.wait_ge(u_loaded[k], 16 * (c + 1))
                    fn(uq[k][:, :], uin[k][:, :], ACT.Copy, scale=S_UM).then_inc(uq_ready, 1)
            od = out.rearrange("b (j p) d -> (b j) p d", p=128)
            with act.Fori(0, ND // 2) as c:
                for k in range(2):
                    act.wait_ge(y_ready, DT * (2 * c + k + 2))
                    act.dma_start(od[bass.ds(c * 2 * DT + k * DT, DT)].rearrange("j p d -> p j d"), yout[k][:, :, :]).then_inc(out_stored[k], 16)
            for k in range(2):
                act.wait_ge(out_stored[k], 16 * (ND // 2))

        @block.vector
        def _(dve):
            v = nc.vector
            step = Ready(dve, vec_chain)

            dve.wait_ge(ws_loaded, 16)
            dve.wait_ge(wb_loaded, 16)
            for k in range(KT):
                v.tensor_tensor(w2[:, k, :, :], ws_sb[:, k, :].unsqueeze(1).to_broadcast([128, DC, D]), wb_sb[:, :, :], ALU.mult).then_inc(w2_ready, 1)
            step(v.memset(ones[:, :], 1.0), wait=False)
            dve.wait_ge(attn_w_loaded, 48)
            for i in range(3):
                step(v.tensor_reduce(amax[:, i:i + 1], w_raw[i][:, :], op=ALU.max, axis=AX.X, apply_absolute_value=True), wait=False)
            dve.wait_ge(wo_loaded, 16)
            step(v.tensor_reduce(amax[:, 3:4], w_raw[3][:, :], op=ALU.max, axis=AX.X, apply_absolute_value=True), wait=False)
            dve.wait_ge(bias_loaded, 96)
            step(v.tensor_reduce(bmax[:, :], b_raw[:, :, :], op=ALU.max, axis=AX.X, apply_absolute_value=True), wait=False)
            dve.wait_ge(ffn_w_loaded, 48)
            for i in range(3):
                step(v.tensor_reduce(blk_max[:, i, :], ffn_raw[i][:, :].rearrange("p (n c) -> p n c", c=BLK), op=ALU.max, axis=AX.X,
                                     apply_absolute_value=True), wait=i == 2)
            step(v.tensor_reduce(amax[:, 4:7], blk_max[:, :, :], op=ALU.max, axis=AX.X))
            v.scalar_tensor_tensor(amax[:, 0:3], bmax[:, :], 1.0 / 16, amax[:, 0:3], ALU.mult, ALU.max).then_inc(amax_ready, 1)
            dve.wait_ge(amax_reduced, 1)
            step(v.tensor_scalar(amax_all[:, 0:7], amax_all[:, 0:7], 1e-30, None, ALU.max))
            step(v.tensor_scalar(pow2[:, 0:7].bitcast(U32), amax_all[:, 0:7].bitcast(U32), 0x7F800000, None, ALU.bitwise_and))
            step(v.reciprocal(wmul[:, 0:7], pow2[:, 0:7]))
            v.tensor_scalar(wmul[:, 0:7], wmul[:, 0:7], W_SCALE, None, ALU.mult).then_inc(wmul_ready, 1)
            dve.wait_ge(wmul_ready, 1)
            for i in range(3):
                step(v.tensor_scalar(b_scaled[:, i, :], b_raw[:, i, :], wmul[:, i:i + 1], None, ALU.mult), wait=False)
            for i in range(2):
                step(v.tensor_scalar(b_second[:, i, :], b_second[:, i, :], wmul[0:64, i:i + 1], None, ALU.mult), wait=False)
            step(v.scalar_tensor_tensor(S_SCORE, pow2[:, 0:1], 1.0 / (W_SCALE * W_SCALE * DH ** 0.5), pow2[:, 1:2], ALU.mult, ALU.mult), wait=False)
            step(v.scalar_tensor_tensor(S_OUT, pow2[:, 2:3], 1.0 / (W_SCALE * W_SCALE), pow2[:, 3:4], ALU.mult, ALU.mult))
            step(v.tensor_scalar(blk_s[:, :, :], blk_max[:, :, :], 1.0 / QMAX4, 1e-12, ALU.mult, ALU.max))
            step(v.reciprocal(blk_r[:, :, :], blk_s[:, :, :]))
            for i in range(3):
                w3 = ffn_raw[i][:, :].rearrange("p (n c) -> p n c", c=BLK)
                q3 = ffn_q[:, :].rearrange("p (n c) -> p n c", c=BLK)
                step(v.tensor_tensor(w3, w3, blk_r[:, i, :].unsqueeze(2).to_broadcast([128, NBLK, BLK]), ALU.mult))
                step(v.tensor_scalar(ffn_q[:, :], ffn_raw[i][:, :], QMAX4, -QMAX4 - 1, ALU.min, ALU.max))
                v.tensor_tensor(w3, q3, blk_s[:, i, :].unsqueeze(2).to_broadcast([128, NBLK, BLK]), ALU.mult).then_inc(ffn_deq, 1)
                dve.wait_ge(ffn_deq, i + 1)
            for i in range(4):
                dve.wait_ge(w_hi_ready, i + 1)
                hi = w_hi[i][:, :, :].rearrange("p k n -> p (k n)") if i < 3 else wo_hi[:, :, :].rearrange("p k n -> p (k n)")
                lo = w_lo[i][:, :, :].rearrange("p k n -> p (k n)") if i < 3 else wo_lo[:, :, :].rearrange("p k n -> p (k n)")
                v.scalar_tensor_tensor(lo, w_raw[i][:, :], wmul[:, i:i + 1], hi, ALU.mult, ALU.subtract).then_inc(w_lo_ready, 1)
            for w in range(3):
                for g in range(2):
                    n = 2 * w + g
                    bank = 4 + 2 * (n % 2)
                    for m in range(2):
                        dve.wait_ge(ffn_hi_ready, 2 * n + m + 1)
                        if w < 2:
                            view = lambda t: t[:, g * F + m * 384:g * F + (m + 1) * 384]
                            src = ps[:, bank + m, 0:384]
                        else:
                            view = lambda t: t[:, :].rearrange("p (f n) -> p f n", n=D)[:, 3 * g:3 * g + 3, m * 128:(m + 1) * 128]
                            src = ps[:, bank + m, 0:384].rearrange("p (f n) -> p f n", n=128)
                        v.scalar_tensor_tensor(view(ffn_lo[w]), src, wmul[:, 4 + w:5 + w], view(ffn_hi[w]), ALU.mult, ALU.subtract).then_inc(ffn_lo_ready, 1)

            NORM = 2 + 3 + 12

            def row_stats(n, tile):
                link = Ready(dve, norm_chain, NORM * n)
                for j in range(TT):
                    ins = v.bn_stats(bn6[:, j, :], tile(j))
                link(ins)
                v.memset(rs[:, 2, :], 0.0)
                for j in range(TT):
                    ins = v.bn_aggr(bn2[:, j, :], bn6[:, j, :])
                link(ins)
                y, vh, t, u = (rs[:, i, :] for i in range(4))
                var = bn2[:, :, 1]
                link(v.tensor_scalar(u, var, LN_EPS, None, ALU.add))
                link(v.tensor_scalar(t.bitcast(U32), u.bitcast(U32), 1, None, ALU.logical_shift_right))
                v.tensor_scalar(vh, u, 0.5, None, ALU.mult)
                link(v.tensor_scalar(y.bitcast(I32), t.bitcast(I32), -1.0, 1597463007.0, ALU.mult, ALU.add))
                for _ in range(3):
                    link(v.tensor_tensor(t, y, y, ALU.mult))
                    link(v.tensor_tensor(t, t, vh, ALU.mult))
                    link(v.tensor_scalar(t, t, -1.0, 1.5, ALU.mult, ALU.add))
                    link(v.tensor_tensor(y, y, t, ALU.mult))
                assert link.n == NORM

            def normalise(dst, src, ready):
                for j in range(TT):
                    v.tensor_scalar(dst[:, j, :], src(j), bn2[:, j, 0:1], rs[:, 0, j:j + 1], ALU.subtract, ALU.mult).then_inc(ready, 1)

            def norm1(b):
                dve.wait_ge(h_copied, 4 * (b + 2))
                dve.wait_ge(txt_loaded, 16 * B)
                dve.wait_ge(xn_ready, TT * b)
                tile = lambda j: h_all[:, bass.ds(b * TT + j, 1), :].rearrange("p a d -> p (a d)")
                row_stats(b, tile)
                dve.wait_ge(xt_done, TT * b)
                normalise(xn, tile, xn_ready)
                for j in range(TT):
                    dve.wait_ge(x_hi_ready, TT * b + j + 1)
                    part = lambda hl: X[:, bass.ds(b * XB + hl * KT * T, KT * T)].rearrange("p (k t) -> p k t", k=KT)[:, :, j * 128:(j + 1) * 128]
                    v.tensor_tensor(part(1), ps[:, 4 + j % 4, 0:D].rearrange("p (k t) -> p k t", k=KT), part(0), ALU.subtract).then_inc(x_lo_ready, 1)
            with dve.Fori(0, B) as b:
                norm1(b)

            dve.wait_ge(x_lo_ready, TT * B)
            dve.wait_ge(xn_ready, TT * B)
            dve.wait_ge(h_stored, 16 * B)
            for par in range(2):
                v.memset(kB[par][64:65, :, :], M_UNIT).then_inc(unit_ready, 1)

            def low_part(Pq, where, wi, par, pair):
                x, n = where
                hi, sem_hi = ((qA, q_hi_ready), (kA, k_hi_ready))[wi]
                dst, rows = ((qA, slice(64, 128)), (kB, slice(0, 64)))[wi]
                for h in range(2):
                    bias = b_second if h else b_scaled
                    dve.wait_ge(sem_hi, 2 * Pq + h + 1)
                    ins = v.scalar_tensor_tensor(dst[par][rows, h, :].rearrange("p (a n) -> p a n", a=2), work[x][64 * h:64 * h + 64, :, 0:HT],
                                                 bias[0:64, wi, bass.ds(pair, 1)],
                                                 hi[par][0:64, h, :].rearrange("p (a n) -> p a n", a=2), ALU.add, ALU.subtract)
                    ins.then_inc(work_free[x] if h else prep_chain, 1)
                if wi == 0:
                    v.tensor_copy(qB[par][0:64, :, :], qA[par][0:64, :, :]).then_inc(prep_chain, 1)
                else:
                    v.tensor_copy(kA[par][64:128, :, :], kA[par][0:64, :, :]).then_inc(qk_ready, 1)

            def low_parts(Pq, where_q, where_k, par, pair):
                low_part(Pq, where_q, 0, par, pair)
                low_part(Pq, where_k, 1, par, pair)

            def maximum(where, i):
                x, n = where
                dve.wait_ge(work_full[x], n)
                v.tensor_reduce(nmax[:, i:i + 1], work[x][:, :, 0:HT], op=ALU.max, axis=AX.XY, negate=True).then_inc(work_free[x], 1)

            def to_unit(last_where):
                x, n = last_where
                dve.wait_ge(work_free[x], n)
                v.tensor_scalar(nmax16[:, :], nmax[:, :], 1.0 / M_UNIT, None, ALU.mult).then_inc(nmax_ready, 1)

            def invert_sums(where):
                x, n = where
                dve.wait_ge(work_free[x], n)
                v.reciprocal(inv[:, :], sums[:, :]).then_inc(inverted, 1)

            def scale_output(b, pair, par, where):
                x, n = where
                dve.wait_ge(work_full[x], n)
                dve.wait_ge(av_saved, 8 * b + pair + 1)
                dve.wait_ge(o_lo_ready, 8 * b + pair)
                two = lambda t: t.rearrange("p (a n) -> p a n", a=2)
                v.tensor_tensor(two(o_norm[:, :]), two(o_raw[par][:, :]), work[x][:, :, 0:HT], ALU.mult).then_inc(work_free[x], 1)

            def o_low(b, pair):
                dve.wait_ge(o_hi_ready, 8 * b + pair + 1)
                one = lambda t: t[:, bass.ds(pair, 1), :].rearrange("p a t -> p (a t)")
                v.scalar_tensor_tensor(one(o_lo), o_norm[:, :], b_scaled[:, 2, bass.ds(pair, 1)], one(o_hi), ALU.add, ALU.subtract).then_inc(o_lo_ready, 1)

            def dve_slot(b, s, par, last):
                S = 8 * b + s
                nxt = not (last and isinstance(s, int) and s == 7)
                zero = isinstance(s, int) and s == 0
                other = 1 - par
                if nxt and not zero:
                    low_part(S + 1, n_work(b, s - 1, "Q"), 0, other, (s + 1) % 8)
                if nxt:
                    low_part(S + 1, n_work(b, s, "K", last=last), 1, other, (s + 1) % 8)
                if finishing(s) == 2:
                    scale_output(b, s - 2, par, n_work(b, s, "inv", last=last))
                if nxt:
                    for i in range(10):
                        maximum(n_work(b, s, "max", i, last), i)
                        if i == 4 and finishing(s) == 2:
                            o_low(b, s - 2)
                    to_unit(n_work(b, s, "max", 9, last))
                else:
                    o_low(b, s - 2)
                if not zero:
                    invert_sums(n_work(b, s, "sum", last=last))
            dve_slot.eng = dve

            def dve_tail(b, last):
                if not last:
                    low_part(8 * b + 9, n_work(b, 7, "Q"), 0, 1, 1)
                scale_output(b, 6, 0, n_tail(b, last, "inv", 0))
                o_low(b, 6)
                invert_sums(n_tail(b, last, "sum", 0))
                scale_output(b, 7, 1, n_tail(b, last, "inv", 1))
                o_low(b, 7)
                dve.wait_ge(h_loaded, 16 * (b + 1))
                for i in range(TT):
                    x, n = n_tail(b, last, "O", i)
                    dve.wait_ge(work_full[x], n)
                    v.scalar_tensor_tensor(h2[:, i, :], work[x][:, 0, 0:D], S_OUT, h2[:, i, :], ALU.mult, ALU.add).then_inc(work_free[x], 1)
                x, n = n_tail(b, last, "O", TT - 1)
                dve.wait_ge(work_free[x], n)
                row_stats(B + b, lambda j: h2[:, j, :])
                dve.wait_ge(work_full[0], slot_base(0, b, 0))
                normalise(xn2, lambda j: h2[:, j, :], xn2_ready)
                dve.wait_ge(xn2_ready, TT * (b + 1))
                v.tensor_reduce(xmax[:, bass.ds(b, 1)], xn2[:, :, :], op=ALU.max, axis=AX.XY, apply_absolute_value=True).then_inc(x2_max, 1)

            low_parts(0, n_start("Q", 0), n_start("K", 0), 0, 0)
            for i in range(10):
                maximum(n_start("max", i), i)
            to_unit(n_start("max", 9))
            low_part(1, n_start("Q", 1), 0, 1, 1)
            with dve.Fori(0, B - 1) as b:
                slots(dve_slot, b, False)
                dve_tail(b, False)
            slots(dve_slot, B - 1, True)
            dve_tail(B - 1, True)

            scale_link = Ready(dve, scale_chain)

            def tensor_max(k, parts):
                for n, p in enumerate(parts):
                    ins = v.tensor_reduce(sc[:, 26 + n:27 + n], p, op=ALU.max, axis=AX.X)
                    if n < len(parts) - 1:
                        scale_link(ins, wait=False)
                ins.then_inc(red_ready, 1)
                dve.wait_ge(red_done, k + 1)
                return [sc[:, 18 + 2 * k + n:19 + 2 * k + n] for n in range(len(parts))]

            def quant_scale(top, unit, scale, mult):
                scale_link(v.tensor_scalar(S_TMP, top, unit, 1.0 / QMAX16, ALU.mult, ALU.mult))
                scale_link(v.tensor_scalar(scale, S_TMP, 1e-12, None, ALU.max))
                scale_link(v.reciprocal(S_ALL, scale))
                ins = v.tensor_scalar(mult, S_ALL, unit, None, ALU.mult)
                return ins

            dve.wait_ge(x2_max, B)
            top, = tensor_max(0, [xmax[:, :]])
            scale_link(v.tensor_scalar(S_X, top, 1.0 / QMAX16, 1e-12, ALU.mult, ALU.max))
            v.reciprocal(S_XI, S_X).then_inc(scales_ready, 1)
            dve.wait_ge(scales_ready, 1)
            for x, k in ((0, 4), (1, 3)):
                dve.wait_ge(work_free[x], n_tail(B - 1, True, "L", k)[1])

            def quantise_x(b, par):
                dve.wait_ge(xl_ready, b)
                dve.wait_ge(unit_done, 2 * FT * b)
                v.tensor_scalar(xq[:, :], X32[:, bass.ds(b * (XB // 2), KT * T)], S_XI, None, ALU.mult).then_inc(xq_chain, 1)
                dve.wait_ge(xq_chain, b + 1)
                flat = lambda t: t[par][:, :, :].rearrange("p k t -> p (k t)")
                v.tensor_copy(flat(xh), xq[:, :]).then_inc(xh_ready, 1)
                dve.wait_ge(xh_ready, b + 1)
                v.tensor_tensor(flat(xl), xq[:, :], flat(xh), ALU.subtract).then_inc(xl_ready, 1)

            def unit_maxima(b, ns):
                for n in ns:
                    f, w = divmod(n, 2)
                    dve.wait_ge(unit_copied, 2 * FT * b + n + 1)
                    src, dst = (ubuf[f % 4][:, :], umax) if w == 0 else (G[:, f, bass.ds(b * T, T)], gmax)
                    v.tensor_reduce(dst[:, bass.ds(b * FT + f, 1)], src, op=ALU.max, axis=AX.X, apply_absolute_value=True).then_inc(unit_max, 1)

            quantise_x(0, 0)
            with dve.Fori(0, B // 2 - 1) as bb:
                for par in range(2):
                    unit_maxima(2 * bb + par, range(FT))
                    quantise_x(2 * bb + par + 1, 1 - par)
                    unit_maxima(2 * bb + par, range(FT, 2 * FT))
            unit_maxima(B - 2, range(FT))
            quantise_x(B - 1, 1)
            unit_maxima(B - 2, range(FT, 2 * FT))
            unit_maxima(B - 1, range(2 * FT))

            dve.wait_ge(unit_max, 2 * FT * B)
            u_top, g_top = tensor_max(1, [umax[:, :], gmax[:, :]])
            for top, col, scale, mult in ((u_top, 4, S_U, S_UM), (g_top, 5, S_G, S_GM)):
                scale_link(v.scalar_tensor_tensor(S_RED, pow2[:, col:col + 1], 1.0 / W_SCALE, S_X, ALU.mult, ALU.mult))
                ins = quant_scale(top, S_RED, scale, mult)
                if col == 4:
                    scale_link(ins)
            ins.then_inc(scales_ready, 1)

            dve.sem_inc(p_ready, 2)
            with dve.Fori(0, NG // 2) as c:
                for k in range(2):
                    n = 2 * c + k
                    dve.wait_ge(sg_ready, n + 1)
                    dve.wait_ge(p_ready, n + 1)
                    v.tensor_scalar(sq[k][:, :], sg[k][:, :], 65536.0, None, ALU.mult).then_inc(sq_ready, 1)
                    dve.wait_ge(sq_ready, n + 1)
                    g = Gf[:, bass.ds(n * GC, GC)]
                    v.tensor_tensor(g, gq[k][:, :], sq[k][:, :], ALU.mult).then_inc(p_ready, 1)
                    dve.wait_ge(p_ready, n + 3)
                    v.tensor_reduce(pmax[:, bass.ds(n, 1)], g, op=ALU.max, axis=AX.X, apply_absolute_value=True).then_inc(p_max, 1)
            dve.wait_ge(p_max, NG)
            top, = tensor_max(2, [pmax[:, :]])
            scale_link(v.tensor_scalar(S_RED, S_G, 1.0 / 65536, None, ALU.mult))
            quant_scale(top, S_RED, S_T, S_TM).then_inc(scales_ready, 1)

            dve.sem_inc(t_ready, 2)
            with dve.Fori(0, NG // 2) as c:
                for k in range(2):
                    n = 2 * c + k
                    dve.wait_ge(tq_ready, n + 1)
                    dve.wait_ge(uq_ready, n + 1)
                    g = Gf[:, bass.ds(n * GC, GC)]
                    v.tensor_tensor(g, tq[k][:, :], uq[k][:, :], ALU.mult).then_inc(t_ready, 1)
                    dve.wait_ge(t_ready, n + 3)
                    v.tensor_reduce(omax[:, bass.ds(n, 1)], g, op=ALU.max, axis=AX.X, apply_absolute_value=True).then_inc(t_max, 1)
            dve.wait_ge(t_max, NG)
            top, = tensor_max(3, [omax[:, :]])
            scale_link(v.tensor_scalar(S_RED, S_T, S_U, None, ALU.mult))
            scale_link(quant_scale(top, S_RED, S_O, S_OM))
            v.scalar_tensor_tensor(S_Y, pow2[:, 6:7], 1.0 / W_SCALE, S_O, ALU.mult, ALU.mult).then_inc(scales_ready, 1)
            dve.wait_ge(scales_ready, 4)

            def quantise_o(n, k):
                dve.wait_ge(ol_ready, n)
                dve.wait_ge(y_done, DT * n)
                v.tensor_scalar(oq[:, :, :], G[:, :, bass.ds(n * DT * 128, DT * 128)], S_OM, None, ALU.mult).then_inc(oq_ready, 1)
                dve.wait_ge(oq_ready, n + 1)
                v.tensor_copy(oh[k][:, :, :], oq[:, :, :]).then_inc(oh_ready, 1)
                dve.wait_ge(oh_ready, n + 1)
                v.tensor_tensor(ol[k][:, :, :], oq[:, :, :], oh[k][:, :, :], ALU.subtract).then_inc(ol_ready, 1)

            def results(n, c, k):
                dve.wait_ge(hin_loaded[k], 16 * (c + 1))
                dve.wait_ge(out_stored[k], 16 * c)
                for j in range(DT):
                    dve.wait_ge(y_done, DT * (n + 1) + j + 1)
                    v.scalar_tensor_tensor(yout[k][:, j, :], ps[:, 4 * k + j, 0:D], S_Y, hin[k][:, j, :], ALU.mult, ALU.add).then_inc(y_ready, 1)

            dve.sem_inc(y_ready, DT)
            quantise_o(0, 0)
            with dve.Fori(0, ND // 2 - 1) as c:
                for k in range(2):
                    quantise_o(2 * c + k + 1, 1 - k)
                    results(2 * c + k, c, k)
            quantise_o(ND - 1, 1)
            results(ND - 2, ND // 2 - 1, 0)
            results(ND - 1, ND // 2 - 1, 1)


def kernel(**inputs):
    import numpy as np
    import concourse.bacc as bacc
    from concourse.bass_utils import run_bass_kernel_spmd

    n = {k: np.asarray(v) for k, v in inputs.items()}
    pairs = lambda b: b.reshape(PAIRS, 128).T
    arrays = {
        "x_t": n["x"].reshape(B, T_IMG // 128, 128, KT, 128, DC).transpose(0, 1, 4, 3, 5, 2),
        "txt": n["txt"],
        "tok_ws_t": n["L0_tok_weighted_sum"].T,
        "tok_w_t": n["L0_tok_weight"].T,
        "wq_t": n["L0_attn_W_Q"].reshape(HD, D).T,
        "wk_t": n["L0_attn_W_K"].reshape(HD, D).T,
        "wv_t": n["L0_attn_W_V"].reshape(HD, D).T,
        "wo_t": n["L0_attn_W_O"].transpose(0, 2, 1).reshape(HD, D),
        "bq": pairs(n["L0_attn_b_Q"]),
        "bk": pairs(n["L0_attn_b_K"]),
        "bv": pairs(n["L0_attn_b_V"]),
        "bo": n["L0_attn_b_O"],
        "w_up": n["L0_ffn_w_up"],
        "w_gate": n["L0_ffn_w_gate"],
        "w_down": n["L0_ffn_w_down"],
    }
    arrays = {k: np.ascontiguousarray(v) for k, v in arrays.items()}
    nc = bacc.Bacc("TRN2", target_bir_lowering=False, num_devices=1)
    args = [nc.dram_tensor(k, v.shape, mybir.dt.from_np(v.dtype), kind="ExternalInput").ap() for k, v in arrays.items()]
    out = nc.dram_tensor("out", (B, T, D), F32, kind="ExternalOutput").ap()
    build(nc, *args, out)
    r = run_bass_kernel_spmd(nc, [arrays], core_ids=[0])
    return r.results[0]["out"]
```

```python
import concourse.bass as bass
from concourse import mybir
from contextlib import ExitStack

F32, F16, I16, U16 = mybir.dt.float32, mybir.dt.float16, mybir.dt.int16, mybir.dt.uint16
I32, U32 = mybir.dt.int32, mybir.dt.uint32
ALU = mybir.AluOpType
ACT = mybir.ActivationFunctionType
AX = mybir.AxisListType
RMAX = bass.bass_isa.ReduceOp.max

B = 8
T_IMG, T_TXT = 512, 128
T = T_IMG + T_TXT
TT = T // 128
HT = T // 2
D = 256
KT = D // 128
DC = 4
HEADS, DH = 16, 64
HD = HEADS * DH
PAIRS = HEADS // 2
F = 768
FT = F // 128
BLK = 32
NBLK = FT * D // BLK
LN_EPS = 1e-5
QMAX16, QMAX4 = 32767.0, 7.0
W_SCALE = 8.0
M_UNIT = 32768.0
RING = 4
LEAD = 4
UNITS = B * FT
GC = 1024
NG = FT * B * T // GC
DT = 4
ND = B * TT // DT


class Ready:

    def __init__(self, eng, sem, base=0):
        self.eng, self.sem, self.base, self.n = eng, sem, base, 0

    def __call__(self, ins, wait=True):
        self.n += 1
        ins.then_inc(self.sem, 1)
        if wait:
            self.eng.wait_ge(self.sem, self.base + self.n)


def build(nc, xT, txt, ws, wb, wq, wk, wv, wo, bq, bk, bv, bo, w_up, w_gate, w_down, out):
    ctx = ExitStack()
    with ctx:
        sem = lambda name: ctx.enter_context(nc.semaphore(name))

        start = 16512
        end = 229344
        at = [start]

        def place(name, shape, dt, where=None):
            where = at if where is None else where
            n = mybir.dt.size(dt)
            for k in shape[1:]:
                n *= k
            t = nc.alloc_sbuf_tensor_at(name, shape, dt, offset=where[0])
            where[0] += -(-n // 32) * 32
            assert where[0] <= end, (name, where[0])
            return t

        ident = place("ident", [128, 128], F32)
        ident16 = place("ident16", [128, 128], F16)
        ones = place("ones", [128, 32], F32)
        bo_row = place("bo_row", [128, D], F32)
        b_raw = place("b_raw", [128, 3, PAIRS], F32)
        b_scaled = place("b_scaled", [128, 3, PAIRS], F32)
        b_second = place("b_second", [64, 2, PAIRS], F32)
        amax = place("amax", [128, 8], F32)
        bmax = place("bmax", [128, 3], F32)
        amax_all = place("amax_all", [128, 8], F32)
        pow2 = place("pow2", [128, 8], F32)
        wmul = place("wmul", [128, 8], F32)
        warm = place("warm", [128, 1], F32)
        sc = place("sc", [128, 32], F32)
        blk_max = place("blk_max", [128, 3, NBLK], F32)
        blk_s = place("blk_s", [128, 3, NBLK], F32)
        blk_r = place("blk_r", [128, 3, NBLK], F32)
        bn6 = place("bn6", [128, TT, 6], F32)
        bn2 = place("bn2", [128, TT, 2], F32)
        rs = place("rs", [128, 4, TT], F32)
        nmax = place("nmax", [128, 2 * TT], F32)
        nmax16 = place("nmax16", [128, 2 * TT], F16)
        xmax = place("xmax", [128, B], F32)
        umax = place("umax", [128, B * FT], F32)
        gmax = place("gmax", [128, B * FT], F32)
        pmax = place("pmax", [128, UNITS], F32)
        omax = place("omax", [128, NG], F32)
        ffn_hi = [place(f"{n}_hi", [128, KT * F], F16) for n in ("up", "gate", "down")]
        ffn_lo = [place(f"{n}_lo", [128, KT * F], F16) for n in ("up", "gate", "down")]
        XB = 2 * KT * T
        x_at = at[0]
        X = place("X", [128, B * XB], F16)
        X32 = nc.alloc_sbuf_tensor_at("X32", [128, B * XB // 2], F32, offset=x_at)
        stage_at = at[0]
        w_hi = [place(f"w{n}_hi", [128, KT, HD], F16) for n in "qkv"]
        w_lo = [place(f"w{n}_lo", [128, KT, HD], F16) for n in "qkv"]
        wo_hi = place("wo_hi", [128, PAIRS, D], F16)
        wo_lo = place("wo_lo", [128, PAIRS, D], F16)
        ab_at = at[0]

        a = [ab_at]
        xbuf = [place(f"xbuf{i}", [128, KT, DC, 128], F32, a) for i in range(4)]
        xn = place("xn", [128, TT, D], F32, a)
        w2 = place("w2", [128, KT, DC, D], F32, a)
        w_raw = [place(f"w{n}_raw", [128, KT * HD], F32, a) for n in "qkv"]
        ffn_q = place("ffn_q", [128, KT * F], I16, a)
        late = [x_at + 4 * 2 * XB]
        ffn_raw = [place(f"{n}_raw", [128, KT * F], F32, late) for n in ("up", "gate", "down")]
        late = [x_at + 2 * 2 * XB]
        w_raw.append(place("wo_raw", [128, PAIRS * D], F32, late))
        ws_sb = place("ws_sb", [128, KT, D], F32, a)
        wb_sb = place("wb_sb", [128, DC, D], F32, a)

        h_all = place("h_all", [128, B * TT, D], F32, a)
        h_at = a[0] - B * TT * D * 4

        a = [ab_at]
        v_all = place("v_all", [128, TT, HD], F32, a)
        qA = [place(f"qA{i}", [128, 2, T], F16, a) for i in range(2)]
        qB = [place(f"qB{i}", [128, 2, T], F16, a) for i in range(2)]
        kA = [place(f"kA{i}", [128, 2, T], F16, a) for i in range(2)]
        kB = [place(f"kB{i}", [128, 2, T], F16, a) for i in range(2)]
        v_pair = [place(f"v_pair{i}", [128, TT, 128], F32, a) for i in range(2)]
        probs = place("probs", [128, RING, 2, HT], F32, a)
        psum_p = place("psum_p", [128, 2, T], F32, a)
        assert a[0] <= h_at
        o_raw = [place(f"o_raw{i}", [128, T], F32, a) for i in range(2)]
        sums = place("sums", [128, HT], F32, a)
        inv = place("inv", [128, HT], F32, a)
        inv_all = place("inv_all", [128, 2, HT], F32, a)
        o_norm = place("o_norm", [128, T], F32, a)
        o_hi = place("o_hi", [128, PAIRS, T], F16, a)
        o_lo = place("o_lo", [128, PAIRS, T], F16, a)
        h2 = place("h2", [128, TT, D], F32, a)
        xn2 = place("xn2", [128, TT, D], F32, a)

        a = [stage_at]
        G = place("G", [128, FT, B * T], F32, a)
        Gf = G[:, :, :].rearrange("p f t -> p (f t)")
        ubuf = [place(f"ubuf{i}", [128, T], F32, a) for i in range(3)]
        xq = place("xq", [128, KT * T], I16, a)
        gq = [place(f"gq{i}", [128, T], I16, a) for i in range(2)]
        sg = [place(f"sg{i}", [128, T], F32, a) for i in range(2)]
        sq = [place(f"sq{i}", [128, T], U16, a) for i in range(2)]
        a = [x_at]
        uin = [place(f"uin{i}", [128, GC], F32, a) for i in range(2)]
        uq = [place(f"uq{i}", [128, GC], I16, a) for i in range(2)]
        tq = [place(f"tq{i}", [128, GC], I16, a) for i in range(2)]
        assert a[0] <= stage_at
        a = [x_at]
        oq = place("oq", [128, FT, DT * 128], I16, a)
        oh = [place(f"oh{i}", [128, FT, DT * 128], F16, a) for i in range(2)]
        ol = [place(f"ol{i}", [128, FT, DT * 128], F16, a) for i in range(2)]
        assert a[0] <= stage_at
        a = [stage_at + FT * B * T * 4]
        hin = [place(f"hin{i}", [128, DT, D], F32, a) for i in range(2)]
        yout = [place(f"yout{i}", [128, DT, D], F32, a) for i in range(2)]

        ps = ctx.enter_context(nc.psum_tensor("ps", [128, 8, 512], F32))
        work = [ps[:, 0:2, :], ps[:, 2:4, :]]
        score = [ps[:, 4, 0:HT], ps[:, 5, 0:HT]]
        av = ps[:, 6:8, 0:HT]
        v_bank = [ps[:, 4:6, :], ps[:, 6:8, :]]

        h_dram = nc.dram_tensor("h_scratch", [B, TT, 128, D], F32, kind="Internal").ap()
        u_dram = nc.dram_tensor("u_scratch", [128, FT * B * T], F32, kind="Internal").ap()

        S_SCORE, S_OUT, S_X, S_XI, S_U, S_UM, S_G, S_GM, S_T, S_TM, S_O, S_OM, S_Y, S_TMP, S_RED, S_ALL = (
            sc[:, i:i + 1] for i in range(16))

        ws_loaded, wb_loaded, attn_w_loaded, wo_loaded = sem("ws_loaded"), sem("wb_loaded"), sem("attn_w_loaded"), sem("wo_loaded")
        bias_loaded, ffn_w_loaded, txt_loaded = sem("bias_loaded"), sem("ffn_w_loaded"), sem("txt_loaded")
        x_loaded = [sem(f"x_loaded{i}") for i in range(4)]
        const_ready, ident_ready = sem("const_ready"), sem("ident_ready")
        w2_ready, tok_done, h_copied, xn_ready = sem("w2_ready"), sem("tok_done"), sem("h_copied"), sem("xn_ready")
        xt_done, x_hi_ready, x_lo_ready = sem("xt_done"), sem("x_hi_ready"), sem("x_lo_ready")
        bo_added, h_stored = sem("bo_added"), sem("h_stored")
        amax_ready, amax_reduced, wmul_ready = sem("amax_ready"), sem("amax_reduced"), sem("wmul_ready")
        w_hi_ready, w_lo_ready = sem("w_hi_ready"), sem("w_lo_ready")
        ffn_deq, ffn_t_done, ffn_hi_ready, ffn_lo_ready = sem("ffn_deq"), sem("ffn_t_done"), sem("ffn_hi_ready"), sem("ffn_lo_ready")
        vec_chain = sem("vec_chain")
        norm_chain = sem("norm_chain")
        work_full = [sem("work0_full"), sem("work1_full")]
        work_free = [sem("work0_free"), sem("work1_free")]
        score_ready, prob_ready, av_done, av_saved = sem("score_ready"), sem("prob_ready"), sem("av_done"), sem("av_saved")
        sum_done, q_hi_ready, k_hi_ready = sem("sum_done"), sem("q_hi_ready"), sem("k_hi_ready")
        prep_chain, qk_ready, nmax_ready, row_chain = sem("prep_chain"), sem("qk_ready"), sem("nmax_ready"), sem("row_chain")
        unit_ready, v_staged = sem("unit_ready"), sem("v_staged")
        v_projected, v_copied = sem("v_projected"), sem("v_copied")
        inverted, inv_spread, o_normed = sem("inverted"), sem("inv_spread"), sem("o_normed")
        o_hi_ready, o_lo_ready = sem("o_hi_ready"), sem("o_lo_ready")
        h_loaded, h2_stored, xn2_ready, x2_max = sem("h_loaded"), sem("h2_stored"), sem("xn2_ready"), sem("x2_max")
        red_ready, red_done, scales_ready, scale_chain = sem("red_ready"), sem("red_done"), sem("scales_ready"), sem("scale_chain")
        xh_ready, xl_ready, xq_chain = sem("xh_ready"), sem("xl_ready"), sem("xq_chain")
        unit_done, unit_copied, g_max, u_max, u_stored = sem("unit_done"), sem("unit_copied"), sem("g_max"), sem("u_max"), [sem(f"u_stored{i}") for i in range(3)]
        sq_start = sem("sq_start")
        gq_ready, sg_ready, sq_ready, p_ready, p_max = sem("gq_ready"), sem("sg_ready"), sem("sq_ready"), sem("p_ready"), sem("p_max")
        u_loaded = [sem("u_loaded0"), sem("u_loaded1")]
        uq_ready, tq_ready, t_ready, t_max = sem("uq_ready"), sem("tq_ready"), sem("t_ready"), sem("t_max")
        oq_ready, oh_ready, ol_ready, y_done, y_ready = sem("oq_ready"), sem("oh_ready"), sem("ol_ready"), sem("y_done"), sem("y_ready")
        hin_loaded = [sem("hin_loaded0"), sem("hin_loaded1")]
        out_stored = [sem("out_stored0"), sem("out_stored1")]

        def n_prob(S, u, h):
            return 20 * (S + 1) + 2 * u + h + 1

        def n_av(S, u):
            return 10 * (S + 1) + u + 1

        def n_sum(S, u, h=1):
            half, j = divmod(u, TT)
            return 16 * (S + 1) + half * 8 + (max(j, 1) - 1) * 2 + h + 1

        def back(S, u, n):
            return (S, u - n) if u >= n else (S - 1, u - n + 10)

        START = [("Q", 0, 0), ("K", 0, 1)] + [("max", k, (1 + k) % 2) for k in range(10)] + [("row", 0, 1), ("Q", 1, 0)]
        TAIL = [("inv", 6, 1), ("sum", 0, 0), ("inv", 7, 0), ("O", 0, 1), ("O", 1, 0), ("O", 2, 1), ("O", 3, 0), ("O", 4, 1),
                ("L", 0, 0), ("L", 1, 1), ("L", 2, 0), ("L", 3, 1), ("L", 4, 0)]

        def counted(order, x, upto=None):
            n = 0
            for name, k, y in order:
                n += x == y
                if (name, k) == upto:
                    break
            return n

        def n_sums(s):
            return 0 if isinstance(s, int) and s == 0 else 1

        def has_output(s):
            return not (isinstance(s, int) and s < 2)

        def slot_base(x, b, s, last=False):
            per_slot = 7
            short = (1 - x) * n_sums(s)
            per_batch = 8 * per_slot - (1 - x) + counted(TAIL, x)
            skipped = (0 if s < 7 else (1 - x if s == 7 else 7)) if last else 0
            return counted(START, x) + per_batch * b + per_slot * s - short - skipped

        def n_work(b, s, use, i=0, last=False):
            x0, x1 = slot_base(0, b, s, last), slot_base(1, b, s, last)
            if use == "sum":
                return 0, x0 + 1
            if use == "max":
                return (0, x0 + n_sums(s) + (i + 1) // 2) if i % 2 else (1, x1 + i // 2 + 2)
            if use == "row":
                return 1, x1 + 7
            if use == "Q":
                return 0, x0 + n_sums(s) + 6
            return 1, x1 + 1

        def n_tail(b, last, use, i):
            x = {(name, k): y for name, k, y in TAIL}[use, i]
            return x, slot_base(x, b, 8, last) + counted(TAIL, x, (use, i))

        def n_start(use, i=0):
            x = {(name, k): y for name, k, y in START}[use, i]
            return x, counted(START, x, (use, i))

        SPREAD = 8 * 16
        TAIL_AFTER_SUM = counted(TAIL, 0) - counted(TAIL, 0, ("sum", 0))

        def slots(body, b, last):
            eng = body.eng
            body(b, 0, 0, False)
            body(b, 1, 1, False)
            with eng.Fori(0, 2) as g:
                body(b, 2 + 2 * g, 0, False)
                body(b, 3 + 2 * g, 1, False)
            body(b, 6, 0, last)
            body(b, 7, 1, last)

        block = ctx.enter_context(nc.Block())

        @block.sync
        def _(sp):
            sp.dma_start(ws_sb[:, :, :], ws.rearrange("(k p) o -> p k o", p=128)).then_inc(ws_loaded, 16)
            sp.dma_start(wb_sb[:, :, :], wb.rearrange("d o -> (d o)").unsqueeze(0).to_broadcast([128, DC * D]).rearrange("p (d o) -> p d o", d=DC)
                         ).then_inc(wb_loaded, 16)
            for i in range(4):
                sp.dma_start(xbuf[i][:, :, :, :], xT[0, i]).then_inc(x_loaded[i], 16)
            with sp.Fori(1, B) as b:
                for i in range(4):
                    sp.wait_ge(tok_done, 4 * (b - 1) + i + 1)
                    sp.dma_start(xbuf[i][:, :, :, :], xT[bass.ds(b, 1), i].rearrange("a p k d t -> (a p) k d t")
                                 ).then_inc(x_loaded[i], 16)
            sp.wait_ge(h_stored, 16 * B)
            sp.wait_ge(work_full[0], 1)
            with sp.Fori(0, B) as b:
                sp.wait_ge(h2_stored, 16 * b)
                sp.dma_start(h2[:, :, :], h_dram[bass.ds(b, 1)].rearrange("a j p d -> p (a j) d")).then_inc(h_loaded, 16)
                with sp.Fori(0, PAIRS - 2) as p:
                    sp.wait_ge(inverted, 8 * b + p + 1)
                    for h in range(2):
                        for half in range(2):
                            row = 32 * (2 * h + half)
                            for k in range(2):
                                sp.dma_start(inv_all[64 * h + 32 * k:64 * h + 32 * k + 32, half, :], inv[row:row + 32, :]).then_inc(inv_spread, 16)
                sp.wait_ge(xn2_ready, TT * (b + 1))
                sp.dma_start(h_dram[bass.ds(b, 1)].rearrange("a j p d -> p (a j) d"), h2[:, :, :]).then_inc(h2_stored, 16)
            with sp.Fori(0, B) as b:
                for f in range(FT):
                    sp.wait_ge(unit_copied, 3 + UNITS + FT * b + f + 1)
                    sp.dma_start(u_dram[:, bass.ds(b * T + f * B * T, T)], ubuf[f % 3][:, :]
                                 ).then_inc(u_stored[f % 3], 16)
            for k in range(3):
                sp.wait_ge(u_stored[k], 16 * 2 * B)
            sp.wait_ge(unit_done, 2 * UNITS)
            for k in range(2):
                sp.dma_start(uin[k][:, :], u_dram[:, k * GC:(k + 1) * GC]).then_inc(u_loaded[k], 16)
            with sp.Fori(1, NG // 2) as c:
                for k in range(2):
                    sp.wait_ge(uq_ready, 2 * (c - 1) + k + 1)
                    sp.dma_start(uin[k][:, :], u_dram[:, bass.ds(c * 2 * GC + k * GC, GC)]).then_inc(u_loaded[k], 16)
            hd = h_dram.rearrange("b j p d -> (b j) p d")
            sp.wait_ge(scales_ready, 3)
            sp.wait_ge(h2_stored, 16 * B)
            with sp.Fori(0, ND // 2) as c:
                for k in range(2):
                    sp.wait_ge(y_ready, DT * (2 * c + k))
                    sp.dma_start(hin[k][:, :, :], hd[bass.ds(c * 2 * DT + k * DT, DT)].rearrange("j p d -> p j d")
                                 ).then_inc(hin_loaded[k], 16)

        @block.gpsimd
        def _(pool):
            pool.memset(ident[:, :], 0.0).then_inc(const_ready, 1)
            pool.memset(ident16[:, :], 0.0).then_inc(const_ready, 1)
            pool.wait_ge(const_ready, 2)
            for m in (ident, ident16):
                pool.affine_select(out=m[:, :], in_=m[:, :], compare_op=ALU.not_equal, fill=1.0, base=0,
                                   pattern=[[-1, 128]], channel_multiplier=1).then_inc(ident_ready, 1)
            pool.wait_ge(amax_ready, 1)
            pool.partition_all_reduce(amax_all[:, 0:7], amax[:, 0:7], 128, RMAX).then_inc(amax_reduced, 1)
            bo_b = bo_row[:, :].unsqueeze(1).to_broadcast([128, TT, D])
            pool.wait_ge(bias_loaded, 96)
            with pool.Fori(0, B) as b:
                pool.wait_ge(xn_ready, TT * (b + 1))
                hb = h_all[:, bass.ds(b * TT, TT), :]
                pool.tensor_tensor(hb, hb, bo_b, ALU.add).then_inc(bo_added, 1)
                pool.wait_ge(bo_added, b + 1)
                pool.dma_start(h_dram[bass.ds(b, 1)].rearrange("a j p d -> p (a j) d"), hb).then_inc(h_stored, 16)
            pool.wait_ge(h_stored, 16 * B)
            pool.wait_ge(work_full[0], 1)
            pool.sem_inc(sum_done, 16)

            def pool_slot(b, s, par, last):
                S = 8 * b + s
                for half in range(2):
                    for j in range(1, TT):
                        for h in range(2):
                            u = half * TT + j
                            dst = psum_p[:, h, half * HT:(half + 1) * HT]
                            pool.wait_ge(prob_ready, n_prob(S, u, h))
                            if j == 1:
                                if half == 0 and h == 0:
                                    if isinstance(s, int) and s == 0:
                                        pool.wait_ge(work_full[0], slot_base(0, b, 0) - TAIL_AFTER_SUM)
                                    else:
                                        pool.wait_ge(work_full[0], n_work(b, s, "sum", last=last)[1])
                                src = probs[:, (10 * par + u - 1) % RING, h, :]
                            else:
                                pool.wait_ge(sum_done, n_sum(S, u - 1, h))
                                src = dst
                            pool.tensor_tensor(dst, src, probs[:, (10 * par + u) % RING, h, :], ALU.add).then_inc(sum_done, 1)
            pool_slot.eng = pool
            with pool.Fori(0, B - 1) as b:
                slots(pool_slot, b, False)
            slots(pool_slot, B - 1, True)
            def all_max(k):
                width = 2 if k == 2 else 1
                pool.wait_ge(red_ready, k + 1)
                pool.partition_all_reduce(sc[:, 18 + 2 * k:18 + 2 * k + width], sc[:, 30:30 + width], 128, RMAX).then_inc(red_done, 1)
            all_max(0)
            all_max(1)
            with pool.Fori(0, UNITS // 2) as c:
                for k in range(2):
                    n = 2 * c + k
                    pool.wait_ge(sg_ready, n + 1)
                    pool.wait_ge(p_ready, n + 1)
                    pool.sem_inc(sq_start, 1)
                    pool.tensor_scalar(sq[k][:, :], sg[k][:, :], 65536.0, 1.0, ALU.mult, ALU.mult).then_inc(sq_ready, 1)
            all_max(2)
            all_max(3)

        @block.tensor
        def _(pe):
            mm = nc.tensor.matmul

            def tok(b, i):
                pe.wait_ge(x_loaded[i], 16 * (b + 1))
                pe.wait_ge(h_copied, 4 * b + i + 1)
                for n in range(KT * DC):
                    k, d = divmod(n, DC)
                    last = mm(ps[:, i, 0:D], xbuf[i][:, k, d, :], w2[:, k, d, :], start=n == 0, stop=n == KT * DC - 1)
                last.then_inc(tok_done, 1)

            def xn_transposes(b):
                for i in range(TT):
                    pe.wait_ge(xn_ready, TT * b + i + 1)
                    pe.wait_ge(x_lo_ready, TT * b + (1 if i == 4 else 0))
                    for k in range(KT):
                        last = nc.tensor.transpose(ps[:, 4 + i % 4, k * 128:(k + 1) * 128], xn[:, i, k * 128:(k + 1) * 128], ident[:, :])
                    last.then_inc(xt_done, 1)

            pe.wait_ge(w2_ready, KT)
            with pe.Fori(0, LEAD - 1) as b:
                for i in range(4):
                    tok(b, i)
            pe.wait_ge(ident_ready, 2)
            for w in range(3):
                pe.wait_ge(ffn_deq, w + 1)
                for g in range(2):
                    n = 2 * w + g
                    bank = 4 + 2 * (n % 2)
                    if n >= 2:
                        pe.wait_ge(ffn_lo_ready, 2 * (n - 1))
                    for m in range(6):
                        if w < 2:
                            src = ffn_raw[w][:, m * D + g * 128:m * D + (g + 1) * 128]
                            dst = ps[:, bank + m // 3, (m % 3) * 128:(m % 3 + 1) * 128]
                        else:
                            dt_, f = divmod(m, 3)
                            src = ffn_raw[w][:, dt_ * F + (3 * g + f) * 128:dt_ * F + (3 * g + f + 1) * 128]
                            dst = ps[:, bank + dt_, f * 128:(f + 1) * 128]
                        last = nc.tensor.transpose(dst, src, ident[:, :])
                    last.then_inc(ffn_t_done, 1)
            for i in range(4):
                tok(LEAD - 1, i)
            pe.wait_ge(ffn_lo_ready, 12)
            with pe.Fori(0, B - LEAD) as c:
                for k in range(2):
                    tok(c + LEAD, 2 * k)
                    tok(c + LEAD, 2 * k + 1)
                    xn_transposes(2 * c + k)

            def use(where, fill):
                x, n = where
                pe.wait_ge(work_free[x], n - 1)
                fill(work[x]).then_inc(work_full[x], 1)

            def project(wi, bb, pair):
                def fill(w):
                    n = 0
                    for k in range(KT):
                        for wt, xs in ((w_hi[wi], (0, 1)), (w_lo[wi], (0,))):
                            lhsT = wt[:, k, bass.ds(pair * 128, 128)]
                            for xp in xs:
                                for half in range(2):
                                    last = mm(w[:, half, 0:HT], lhsT, X[:, bass.ds(bb * XB + (xp * KT + k) * T + half * HT, HT)],
                                              start=n < 2, stop=n >= 10)
                                    n += 1
                    return last
                return fill

            def project_v(bb, j):
                if j > 1:
                    pe.wait_ge(v_copied, TT * bb + j - 1)
                n = 0
                for k in range(KT):
                    for xp, wt in ((0, w_hi[2]), (0, w_lo[2]), (1, w_hi[2])):
                        lhsT = X[:, bass.ds(bb * XB + (xp * KT + k) * T + j * 128, 128)]
                        for c in range(2):
                            last = mm(v_bank[j % 2][:, c, :], lhsT, wt[:, k, c * 512:(c + 1) * 512], start=n < 2, stop=n >= 10)
                            n += 1
                last.then_inc(v_projected, 1)

            def max_tile(par, i):
                def fill(w):
                    t, h = divmod(i, 2)
                    for half in range(2):
                        last = mm(w[:, half, 0:HT], qA[par][:, h, t * 128:(t + 1) * 128], kA[par][:, h, half * HT:(half + 1) * HT],
                                  start=True, stop=True)
                    return last
                return fill

            def max_row(w):
                flat = w.rearrange("p a n -> p (a n)")
                for h in range(2):
                    for t in range(TT):
                        last = mm(flat[64 + 32 * h:65 + 32 * h, t * 128:(t + 1) * 128], nmax16[:, 2 * t + h:2 * t + h + 1], ident16[:, :],
                                  start=True, stop=True)
                return last

            def sum_rows(w):
                for i in range(4):
                    h, half = divmod(i, 2)
                    last = mm(w[32 * i:32 * i + 32, 0, 0:HT], ones[:, :], psum_p[:, h, half * HT:(half + 1) * HT], start=True, stop=True)
                return last

            def spread_inv(w):
                for half in range(2):
                    for h in range(2):
                        row = 32 * (2 * h + half)
                        last = mm(w[64 * h:64 * h + 64, half, 0:HT], ident[:, row:row + 1].to_broadcast([128, DH]), inv[:, :], start=True, stop=True)
                return last

            def out_tile(j):
                def fill(w):
                    n = 0
                    for p in range(PAIRS):
                        for ot, wt in ((o_hi, wo_hi), (o_hi, wo_lo), (o_lo, wo_hi)):
                            last = mm(w[:, 0, 0:D], ot[:, p, j * 128:(j + 1) * 128], wt[:, p, :], start=n == 0, stop=n == 3 * PAIRS - 1)
                            n += 1
                    return last
                return fill

            def xn2_tile(j):
                def fill(w):
                    for k in range(KT):
                        last = nc.tensor.transpose(w[:, 0, k * 128:(k + 1) * 128], xn2[:, j, k * 128:(k + 1) * 128], ident[:, :])
                    return last
                return fill

            def attend(S, par, u):
                half, j = divmod(u, TT)
                if u == 0:
                    pe.wait_ge(v_staged, S + 1)
                    pe.wait_ge(av_saved, S)
                pe.wait_ge(prob_ready, n_prob(S, u, 1))
                for h in range(2):
                    last = mm(av[64 * h:64 * h + 64, half, :], v_pair[par][:, j, 64 * h:64 * h + 64],
                              probs[:, (10 * par + u) % RING, h, :], start=j == 0, stop=j == TT - 1)
                last.then_inc(av_done, 1)

            def pe_slot(b, s, par, last):
                S = 8 * b + s
                nxt = not (last and isinstance(s, int) and s == 7)
                ahead = nxt and not (last and isinstance(s, int) and s == 6)
                finish = not (isinstance(s, int) and s == 0)
                other = 1 - par

                def maximum_of(i):
                    if nxt and 0 <= i < 10:
                        use(n_work(b, s, "max", i, last), max_tile(other, i))

                if finish:
                    pe.wait_ge(work_free[1], n_work(b, s - 1, "row", last=last)[1])
                else:
                    pe.wait_ge(v_copied, TT * (b + 1))
                for u in range(10):
                    half, j = divmod(u, TT)
                    for h in range(2):
                        pe.wait_ge(prob_ready, n_prob(*back(S, u, 1), h))
                        mm(score[h], kA[par][:, h, j * 128:(j + 1) * 128], qA[par][:, h, half * HT:(half + 1) * HT], start=True, stop=False)
                        mm(score[h], kB[par][0:65, h, j * 128:(j + 1) * 128], qB[par][0:65, h, half * HT:(half + 1) * HT],
                           start=False, stop=True).then_inc(score_ready, 1)
                    if u == 0 and nxt:
                        use(n_work(b, s, "K", last=last), project(1, b + (s + 1) // 8, (s + 1) % 8))
                    maximum_of(2 * (u - 2) - 1)
                    if u >= 2:
                        attend(S, par, u - 2)
                    elif finish:
                        attend(S - 1, other, 8 + u)
                    if u == 1 and finish:
                        pe.wait_ge(sum_done, 16 * (S + 1))
                        use(n_work(b, s, "sum", last=last), sum_rows)
                    if u == 2 and nxt:
                        pe.wait_ge(qk_ready, S + 2)
                    maximum_of(2 * (u - 2))
                    if u == 8 and nxt:
                        pe.wait_ge(nmax_ready, S + 2)
                        use(n_work(b, s, "row", last=last), max_row)
                if ahead:
                    use(n_work(b, s, "Q", last=last), project(0, b + (s + 2) // 8, (s + 2) % 8))
            pe_slot.eng = pe

            def pe_tail(b, last):
                attend(8 * b + 7, 1, 8)
                attend(8 * b + 7, 1, 9)
                pe.wait_ge(inverted, 8 * b + 7)
                use(n_tail(b, last, "inv", 6), spread_inv)
                if not last:
                    project_v(b + 1, 0)
                pe.wait_ge(sum_done, 16 * (8 * b + 9))
                use(n_tail(b, last, "sum", 0), sum_rows)
                if not last:
                    pe.wait_ge(av_saved, 8 * (b + 1))
                    project_v(b + 1, 1)
                pe.wait_ge(inverted, 8 * b + 8)
                use(n_tail(b, last, "inv", 7), spread_inv)
                if not last:
                    project_v(b + 1, 2)
                pe.wait_ge(o_lo_ready, 8 * (b + 1))
                for i in range(TT):
                    use(n_tail(b, last, "O", i), out_tile(i))
                if not last:
                    project_v(b + 1, 3)
                    project_v(b + 1, 4)
                for i in range(TT):
                    pe.wait_ge(xn2_ready, TT * b + i + 1)
                    use(n_tail(b, last, "L", i), xn2_tile(i))

            pe.wait_ge(x_lo_ready, TT * B)
            pe.wait_ge(x_hi_ready, TT * B)
            pe.wait_ge(w_lo_ready, 4)
            pe.sem_inc(av_done, 10)
            pe.wait_ge(unit_ready, 2)
            use(n_start("Q", 0), project(0, 0, 0))
            use(n_start("K", 0), project(1, 0, 0))
            for j in range(TT):
                project_v(0, j)
            pe.wait_ge(qk_ready, 1)
            for i in range(10):
                use(n_start("max", i), max_tile(0, i))
            pe.wait_ge(nmax_ready, 1)
            use(n_start("row"), max_row)
            use(n_start("Q", 1), project(0, 0, 1))
            pe.wait_ge(work_free[1], n_start("row")[1])
            with pe.Fori(0, B - 1) as b:
                slots(pe_slot, b, False)
                pe_tail(b, False)
            slots(pe_slot, B - 1, True)
            pe_tail(B - 1, True)

            pe.sem_inc(y_done, DT)
            for x, k in ((0, 4), (1, 3)):
                pe.wait_ge(work_free[x], n_tail(B - 1, True, "L", k)[1])
            for w in (1, 0):
                with pe.Fori(0, B) as b:
                    if w:
                        pe.wait_ge(xh_ready, b + 1)
                        pe.wait_ge(xl_ready, b + 1)
                    for f in range(FT):
                        pe.wait_ge(unit_copied, (1 - w) * UNITS + FT * b + f + 1)
                        banks = ps[:, 2 * (f % 3):2 * (f % 3) + 2, :]
                        m = 0
                        for k in range(KT):
                            for wt, xs in ((ffn_hi[w], (0, 1)), (ffn_lo[w], (0,))):
                                for xp in xs:
                                    for half in range(2):
                                        last = mm(banks[:, half, 0:HT], wt[:, k * F + f * 128:k * F + (f + 1) * 128],
                                                  X[:, bass.ds(b * XB + (xp * KT + k) * T + half * HT, HT)], start=m < 2, stop=m >= 10)
                                        m += 1
                        last.then_inc(unit_done, 1)
            pe.wait_ge(unit_copied, 3 + 2 * UNITS)
            with pe.Fori(0, ND // 2) as c:
                for k in range(2):
                    n = 2 * c + k
                    pe.wait_ge(ol_ready, n + 1)
                    for j in range(DT):
                        pe.wait_ge(y_ready, DT * n)
                        m = 0
                        for f in range(FT):
                            for ot, wt in ((oh, ffn_hi[2]), (oh, ffn_lo[2]), (ol, ffn_hi[2])):
                                last = mm(ps[:, 4 * k + j, 0:D], ot[k][:, f, j * 128:(j + 1) * 128], wt[:, f * D:(f + 1) * D],
                                          start=m == 0, stop=m == 3 * FT - 1)
                                m += 1
                        last.then_inc(y_done, 1)

        @block.scalar
        def _(act):
            fn = nc.scalar.activation
            act.sem_inc(h_copied, 4)
            for i, w in enumerate((wq, wk, wv)):
                act.dma_start(w_raw[i][:, :].rearrange("p (k n) -> p k n", k=KT), w.rearrange("(k p) n -> p k n", p=128)).then_inc(attn_w_loaded, 16)
            act.dma_start(w_raw[3][:, :].rearrange("p (k n) -> p k n", k=PAIRS), wo.rearrange("(k p) n -> p k n", p=128)).then_inc(wo_loaded, 16)
            for i, bias in enumerate((bq, bk, bv)):
                act.dma_start(b_raw[:, i, :], bias).then_inc(bias_loaded, 16)
                if i < 2:
                    act.dma_start(b_second[:, i, :], bias[64:128, :]).then_inc(bias_loaded, 16)
            act.dma_start(bo_row[:, :], bo.unsqueeze(0).to_broadcast([128, D])).then_inc(bias_loaded, 16)
            for i, w in enumerate((w_up, w_gate, w_down)):
                act.dma_start(ffn_raw[i][:, :].rearrange("p (k n) -> p k n", k=(FT, FT, KT)[i]), w.rearrange("(k p) n -> p k n", p=128)).then_inc(ffn_w_loaded, 16)
            for b in range(B):
                act.dma_start(h_all[:, b * TT + TT - 1, :], txt[b]).then_inc(txt_loaded, 16)

            def copy_h(b, tiles=range(4)):
                for i in tiles:
                    act.wait_ge(tok_done, 4 * b + i + 1)
                    fn(h_all[:, bass.ds(b * TT + i, 1), :].rearrange("p a d -> p (a d)"), ps[:, i, 0:D], ACT.Copy).then_inc(h_copied, 1)

            def split_x(b):
                for i in range(TT):
                    act.wait_ge(xt_done, TT * b + i + 1)
                    dst = X[:, bass.ds(b * XB, KT * T)].rearrange("p (k t) -> p k t", k=KT)[:, :, i * 128:(i + 1) * 128]
                    fn(dst, ps[:, 4 + i % 4, 0:D].rearrange("p (k t) -> p k t", k=KT), ACT.Copy).then_inc(x_hi_ready, 1)

            with act.Fori(0, LEAD - 2) as b:
                copy_h(b)
            act.wait_ge(wmul_ready, 1)
            for i in range(4):
                dst = w_hi[i][:, :, :].rearrange("p k n -> p (k n)") if i < 3 else wo_hi[:, :, :].rearrange("p k n -> p (k n)")
                fn(dst, w_raw[i][:, :], ACT.Copy, scale=wmul[:, i:i + 1]).then_inc(w_hi_ready, 1)
            copy_h(LEAD - 2)
            for w in range(3):
                for g in range(2):
                    n = 2 * w + g
                    bank = 4 + 2 * (n % 2)
                    act.wait_ge(ffn_t_done, n + 1)
                    for m in range(2):
                        if w < 2:
                            dst = ffn_hi[w][:, g * F + m * 384:g * F + (m + 1) * 384]
                            src = ps[:, bank + m, 0:384]
                        else:
                            dst = ffn_hi[w][:, :].rearrange("p (f n) -> p f n", n=D)[:, 3 * g:3 * g + 3, m * 128:(m + 1) * 128]
                            src = ps[:, bank + m, 0:384].rearrange("p (f n) -> p f n", n=128)
                        fn(dst, src, ACT.Copy, scale=wmul[:, 4 + w:5 + w]).then_inc(ffn_hi_ready, 1)
            copy_h(LEAD - 1)
            act.wait_ge(w_lo_ready, 4)
            with act.Fori(0, B - LEAD) as c:
                for k in range(2):
                    copy_h(c + LEAD, (2 * k, 2 * k + 1))
                    split_x(2 * c + k)

            act.wait_ge(x_lo_ready, TT * B)
            act.sem_inc(prob_ready, 20)

            def hi_part(dst, wi, sem_hi, where, P, pair, par):
                x, n = where
                act.wait_ge(work_full[x], n)
                for h in range(2):
                    fn(dst[par][0:64, h, :].rearrange("p (a n) -> p a n", a=2), work[x][64 * h:64 * h + 64, :, 0:HT], ACT.Identity,
                       bias=b_scaled[64 * h:64 * h + 64, wi, bass.ds(pair, 1)]).then_inc(sem_hi, 1)

            def move_rows(where, par):
                x, n = where
                act.wait_ge(work_full[x], n)
                for h in range(2):
                    flat = work[x].rearrange("p a n -> p (a n)")
                    ins = fn(qB[par][64:65, h, :], flat[64 + 32 * h:65 + 32 * h, 0:T], ACT.Copy)
                    ins.then_inc(work_free[x] if h else row_chain, 1)

            def copy_v(bb, j):
                act.wait_ge(v_projected, TT * bb + j + 1)
                fn(v_all[:, j, :], v_bank[j % 2].rearrange("p a n -> p (a n)"), ACT.Copy).then_inc(v_copied, 1)

            def o_high(b, pair, where=None):
                if where:
                    act.wait_ge(work_free[where[0]], where[1])
                else:
                    act.wait_ge(o_normed, (PAIRS - 2) * b + pair + 1)
                act.wait_ge(work_full[1], slot_base(1, b, 0) - 2)
                fn(o_hi[:, bass.ds(pair, 1), :].rearrange("p a t -> p (a t)"), o_norm[:, :], ACT.Identity,
                   bias=b_scaled[:, 2, bass.ds(pair, 1)]).then_inc(o_hi_ready, 1)

            def copy_sums(S, where):
                x, n = where
                act.wait_ge(inverted, S)
                act.wait_ge(work_full[x], n)
                fn(sums[:, :], work[x][:, 0, 0:HT], ACT.Copy).then_inc(work_free[x], 1)

            def save_output(S, par):
                act.wait_ge(av_done, n_av(S, 9))
                fn(o_raw[par][:, :].rearrange("p (a n) -> p a n", a=2), av, ACT.Copy).then_inc(av_saved, 1)

            def stage_v(S, pair, par):
                act.wait_ge(av_done, 10 * S)
                act.wait_ge(v_copied, TT * (S // 8 + 1))
                fn(v_pair[par][:, :, :], v_all[:, :, bass.ds(pair * 128, 128)], ACT.Copy).then_inc(v_staged, 1)

            def act_slot(b, s, par, last):
                S = 8 * b + s
                nxt = not (last and isinstance(s, int) and s == 7)
                ahead = nxt and not (last and isinstance(s, int) and s == 6)
                finish = not (isinstance(s, int) and s == 0)
                other = 1 - par
                for u in range(10):
                    act.wait_ge(av_done, n_av(*back(S, u, RING)))
                    act.wait_ge(sum_done, n_sum(*back(S, u, RING)))
                    for h in range(2):
                        act.wait_ge(score_ready, 20 * S + 2 * u + h + 1)
                        fn(probs[:, (10 * par + u) % RING, h, :], score[h], ACT.Exp, scale=S_SCORE).then_inc(prob_ready, 1)
                    if u == 0 and nxt:
                        hi_part(kA, 1, k_hi_ready, n_work(b, s, "K", last=last), S + 1, (s + 1) % 8, other)
                    if u == 1 and finish:
                        save_output(S - 1, other)
                        copy_sums(S - 1, n_work(b, s, "sum", last=last))
                    if u == 5 and not (isinstance(s, int) and s == 7):
                        stage_v(S + 1, s + 1, other)
                    if u == 6 and has_output(s):
                        o_high(b, s - 2)
                    if u == 8 and nxt:
                        move_rows(n_work(b, s, "row", last=last), other)
                if ahead:
                    hi_part(qA, 0, q_hi_ready, n_work(b, s, "Q", last=last), S + 2, (s + 2) % 8, par)
            act_slot.eng = act

            def act_tail(b, last):
                save_output(8 * b + 7, 1)
                o_high(b, 6, n_tail(b, last, "inv", 6))
                if not last:
                    act.wait_ge(v_staged, 8 * (b + 1))
                    copy_v(b + 1, 0)
                copy_sums(8 * b + 7, n_tail(b, last, "sum", 0))
                if not last:
                    copy_v(b + 1, 1)
                o_high(b, 7, n_tail(b, last, "inv", 7))
                if not last:
                    for j in range(2, TT):
                        copy_v(b + 1, j)
                    stage_v(8 * (b + 1), 0, 0)
                for i in range(TT):
                    x, n = n_tail(b, last, "L", i)
                    act.wait_ge(work_full[x], n)
                    dst = X32[:, bass.ds(b * (XB // 2), KT * T)].rearrange("p (k t) -> p k t", k=KT)[:, :, i * 128:(i + 1) * 128]
                    fn(dst, work[x][:, 0, 0:D].rearrange("p (k t) -> p k t", k=KT), ACT.Copy).then_inc(work_free[x], 1)

            hi_part(qA, 0, q_hi_ready, n_start("Q", 0), 0, 0, 0)
            hi_part(kA, 1, k_hi_ready, n_start("K", 0), 0, 0, 0)
            for j in range(TT):
                copy_v(0, j)
            stage_v(0, 0, 0)
            move_rows(n_start("row"), 0)
            hi_part(qA, 0, q_hi_ready, n_start("Q", 1), 1, 1, 1)
            act.wait_ge(h_stored, 16 * B)
            with act.Fori(0, B - 1) as b:
                slots(act_slot, b, False)
                act_tail(b, False)
            slots(act_slot, B - 1, True)
            act_tail(B - 1, True)

            def copy_unit(n, f, dst):
                act.wait_ge(unit_done, n + 1)
                fn(dst.rearrange("p (a n) -> p a n", a=2), ps[:, 2 * (f % 3):2 * (f % 3) + 2, 0:HT], ACT.Copy).then_inc(unit_copied, 1)

            act.wait_ge(h2_stored, 16 * B)
            act.sem_inc(unit_copied, 3)
            with act.Fori(0, B) as b:
                for f in range(FT):
                    copy_unit(FT * b + f, f, G[:, f, bass.ds(b * T, T)])
            fn(warm[:, :], ones[:, 0:1], ACT.Sigmoid)
            with act.Fori(0, B) as b:
                for f in range(FT):
                    n = FT * b + f
                    act.wait_ge(u_stored[f % 3], 16 * (2 * b + f // 3))
                    act.wait_ge(u_max, n + 1)
                    copy_unit(UNITS + n, f, ubuf[f % 3][:, :])
                    if f == 0:
                        act.wait_ge(scales_ready, 2)
                    act.wait_ge(p_ready, n + 1)
                    fn(gq[f % 2][:, :], G[:, f, bass.ds(b * T, T)], ACT.Copy, scale=S_GM).then_inc(gq_ready, 1)
                    act.wait_ge(gq_ready, n + 1)
                    fn(sg[f % 2][:, :], gq[f % 2][:, :], ACT.Sigmoid, scale=S_G).then_inc(sg_ready, 1)
            act.wait_ge(scales_ready, 3)
            with act.Fori(0, NG // 2) as c:
                for k in range(2):
                    n = 2 * c + k
                    act.wait_ge(t_ready, n + 1)
                    fn(tq[k][:, :], Gf[:, bass.ds(n * GC, GC)], ACT.Copy, scale=S_TM).then_inc(tq_ready, 1)
                    act.wait_ge(u_loaded[k], 16 * (c + 1))
                    fn(uq[k][:, :], uin[k][:, :], ACT.Copy, scale=S_UM).then_inc(uq_ready, 1)
            od = out.rearrange("b (j p) d -> (b j) p d", p=128)
            with act.Fori(0, ND // 2) as c:
                for k in range(2):
                    act.wait_ge(y_ready, DT * (2 * c + k + 2))
                    act.dma_start(od[bass.ds(c * 2 * DT + k * DT, DT)].rearrange("j p d -> p j d"), yout[k][:, :, :]).then_inc(out_stored[k], 16)
            for k in range(2):
                act.wait_ge(out_stored[k], 16 * (ND // 2))

        @block.vector
        def _(dve):
            v = nc.vector
            step = Ready(dve, vec_chain)

            dve.wait_ge(ws_loaded, 16)
            dve.wait_ge(wb_loaded, 16)
            for k in range(KT):
                v.tensor_tensor(w2[:, k, :, :], ws_sb[:, k, :].unsqueeze(1).to_broadcast([128, DC, D]), wb_sb[:, :, :], ALU.mult).then_inc(w2_ready, 1)
            step(v.memset(ones[:, :], 1.0), wait=False)
            dve.wait_ge(attn_w_loaded, 48)
            for i in range(3):
                step(v.tensor_reduce(amax[:, i:i + 1], w_raw[i][:, :], op=ALU.max, axis=AX.X, apply_absolute_value=True), wait=False)
            dve.wait_ge(wo_loaded, 16)
            step(v.tensor_reduce(amax[:, 3:4], w_raw[3][:, :], op=ALU.max, axis=AX.X, apply_absolute_value=True), wait=False)
            dve.wait_ge(bias_loaded, 96)
            step(v.tensor_reduce(bmax[:, :], b_raw[:, :, :], op=ALU.max, axis=AX.X, apply_absolute_value=True), wait=False)
            dve.wait_ge(ffn_w_loaded, 48)
            for i in range(3):
                step(v.tensor_reduce(blk_max[:, i, :], ffn_raw[i][:, :].rearrange("p (n c) -> p n c", c=BLK), op=ALU.max, axis=AX.X,
                                     apply_absolute_value=True), wait=i == 2)
            step(v.tensor_reduce(amax[:, 4:7], blk_max[:, :, :], op=ALU.max, axis=AX.X))
            v.scalar_tensor_tensor(amax[:, 0:3], bmax[:, :], 1.0 / 16, amax[:, 0:3], ALU.mult, ALU.max).then_inc(amax_ready, 1)
            dve.wait_ge(amax_reduced, 1)
            step(v.tensor_scalar(amax_all[:, 0:7], amax_all[:, 0:7], 1e-30, None, ALU.max))
            step(v.tensor_scalar(pow2[:, 0:7].bitcast(U32), amax_all[:, 0:7].bitcast(U32), 0x7F800000, None, ALU.bitwise_and))
            step(v.reciprocal(wmul[:, 0:7], pow2[:, 0:7]))
            v.tensor_scalar(wmul[:, 0:7], wmul[:, 0:7], W_SCALE, None, ALU.mult).then_inc(wmul_ready, 1)
            dve.wait_ge(wmul_ready, 1)
            for i in range(3):
                step(v.tensor_scalar(b_scaled[:, i, :], b_raw[:, i, :], wmul[:, i:i + 1], None, ALU.mult), wait=False)
            for i in range(2):
                step(v.tensor_scalar(b_second[:, i, :], b_second[:, i, :], wmul[0:64, i:i + 1], None, ALU.mult), wait=False)
            step(v.scalar_tensor_tensor(S_SCORE, pow2[:, 0:1], 1.0 / (W_SCALE * W_SCALE * DH ** 0.5), pow2[:, 1:2], ALU.mult, ALU.mult), wait=False)
            step(v.scalar_tensor_tensor(S_OUT, pow2[:, 2:3], 1.0 / (W_SCALE * W_SCALE), pow2[:, 3:4], ALU.mult, ALU.mult))
            step(v.tensor_scalar(blk_s[:, :, :], blk_max[:, :, :], 1.0 / QMAX4, 1e-12, ALU.mult, ALU.max))
            step(v.reciprocal(blk_r[:, :, :], blk_s[:, :, :]))
            for i in range(3):
                w3 = ffn_raw[i][:, :].rearrange("p (n c) -> p n c", c=BLK)
                q3 = ffn_q[:, :].rearrange("p (n c) -> p n c", c=BLK)
                step(v.tensor_tensor(w3, w3, blk_r[:, i, :].unsqueeze(2).to_broadcast([128, NBLK, BLK]), ALU.mult))
                step(v.tensor_scalar(ffn_q[:, :], ffn_raw[i][:, :], QMAX4, -QMAX4 - 1, ALU.min, ALU.max))
                v.tensor_tensor(w3, q3, blk_s[:, i, :].unsqueeze(2).to_broadcast([128, NBLK, BLK]), ALU.mult).then_inc(ffn_deq, 1)
                dve.wait_ge(ffn_deq, i + 1)
            for i in range(4):
                dve.wait_ge(w_hi_ready, i + 1)
                hi = w_hi[i][:, :, :].rearrange("p k n -> p (k n)") if i < 3 else wo_hi[:, :, :].rearrange("p k n -> p (k n)")
                lo = w_lo[i][:, :, :].rearrange("p k n -> p (k n)") if i < 3 else wo_lo[:, :, :].rearrange("p k n -> p (k n)")
                v.scalar_tensor_tensor(lo, w_raw[i][:, :], wmul[:, i:i + 1], hi, ALU.mult, ALU.subtract).then_inc(w_lo_ready, 1)
            for w in range(3):
                for g in range(2):
                    n = 2 * w + g
                    bank = 4 + 2 * (n % 2)
                    for m in range(2):
                        dve.wait_ge(ffn_hi_ready, 2 * n + m + 1)
                        if w < 2:
                            view = lambda t: t[:, g * F + m * 384:g * F + (m + 1) * 384]
                            src = ps[:, bank + m, 0:384]
                        else:
                            view = lambda t: t[:, :].rearrange("p (f n) -> p f n", n=D)[:, 3 * g:3 * g + 3, m * 128:(m + 1) * 128]
                            src = ps[:, bank + m, 0:384].rearrange("p (f n) -> p f n", n=128)
                        v.scalar_tensor_tensor(view(ffn_lo[w]), src, wmul[:, 4 + w:5 + w], view(ffn_hi[w]), ALU.mult, ALU.subtract).then_inc(ffn_lo_ready, 1)

            NORM = 2 + 3 + 4 + 3 + 3

            def row_stats(n, last_moments, between=lambda: None):
                link = Ready(dve, norm_chain, NORM * n)
                link(last_moments, wait=False)
                between()
                dve.wait_ge(norm_chain, NORM * n + 1)
                v.memset(rs[:, 2, :], 0.0)
                for j in range(TT):
                    ins = v.bn_aggr(bn2[:, j, :], bn6[:, j, :])
                link(ins)
                y, vh, t, u = (rs[:, i, :] for i in range(4))
                var = bn2[:, :, 1]
                link(v.tensor_scalar(u, var, LN_EPS, None, ALU.add))
                link(v.tensor_scalar(t.bitcast(U32), u.bitcast(U32), 1, None, ALU.logical_shift_right))
                v.tensor_scalar(vh, u, 0.5, None, ALU.mult)
                link(v.tensor_scalar(y.bitcast(I32), t.bitcast(I32), -1.0, 1597463007.0, ALU.mult, ALU.add))
                link(v.tensor_tensor(t, y, y, ALU.mult))
                link(v.tensor_tensor(t, t, vh, ALU.mult))
                link(v.tensor_scalar(t, t, -1.0, 1.5, ALU.mult, ALU.add))
                link(v.tensor_tensor(y, y, t, ALU.mult))
                for _ in range(2):
                    link(v.tensor_tensor(t, y, y, ALU.mult))
                    link(v.tensor_tensor(t, t, vh, ALU.mult))
                    link(v.scalar_tensor_tensor(y, t, 1.5, y, ALU.subtract, ALU.mult))
                assert link.n == NORM

            def normalise(dst, src, ready):
                for j in range(TT):
                    v.tensor_scalar(dst[:, j, :], src(j), bn2[:, j, 0:1], rs[:, 0, j:j + 1], ALU.subtract, ALU.mult).then_inc(ready, 1)

            h_tile = lambda b, j: h_all[:, bass.ds(b * TT + j, 1), :].rearrange("p a d -> p (a d)")

            def stats1(b, between=lambda: None):
                dve.wait_ge(h_copied, 4 * (b + 2))
                dve.wait_ge(xn_ready, TT * b)
                for j in range(TT):
                    ins = v.bn_stats(bn6[:, j, :], h_tile(b, j))
                row_stats(b, ins, between)

            def normalise1(b):
                dve.wait_ge(xt_done, TT * b)
                normalise(xn, lambda j: h_tile(b, j), xn_ready)

            def low_x(b):
                part = lambda hl, j: X[:, bass.ds(b * XB + hl * KT * T, KT * T)].rearrange("p (k t) -> p k t", k=KT)[:, :, j * 128:(j + 1) * 128]
                for j in range(TT):
                    dve.wait_ge(x_hi_ready, TT * b + j + 1)
                    v.tensor_tensor(part(1, j), ps[:, 4 + j % 4, 0:D].rearrange("p (k t) -> p k t", k=KT), part(0, j), ALU.subtract).then_inc(x_lo_ready, 1)

            dve.wait_ge(txt_loaded, 16 * B)
            stats1(0)
            with dve.Fori(0, B - 2) as b:
                normalise1(b)
                stats1(b + 1, between=lambda: low_x(b))
            normalise1(B - 2)
            low_x(B - 2)
            stats1(B - 1)
            normalise1(B - 1)
            low_x(B - 1)

            dve.wait_ge(x_lo_ready, TT * B)
            dve.wait_ge(xn_ready, TT * B)
            for par in range(2):
                v.memset(kB[par][64:65, :, :], M_UNIT).then_inc(unit_ready, 1)

            def low_part(Pq, where, wi, par, pair):
                x, n = where
                hi, sem_hi = ((qA, q_hi_ready), (kA, k_hi_ready))[wi]
                dst, rows = ((qA, slice(64, 128)), (kB, slice(0, 64)))[wi]
                for h in range(2):
                    bias = b_second if h else b_scaled
                    dve.wait_ge(sem_hi, 2 * Pq + h + 1)
                    ins = v.scalar_tensor_tensor(dst[par][rows, h, :].rearrange("p (a n) -> p a n", a=2), work[x][64 * h:64 * h + 64, :, 0:HT],
                                                 bias[0:64, wi, bass.ds(pair, 1)],
                                                 hi[par][0:64, h, :].rearrange("p (a n) -> p a n", a=2), ALU.add, ALU.subtract)
                    ins.then_inc(work_free[x] if h else prep_chain, 1)
                if wi == 0:
                    v.tensor_copy(qB[par][0:64, :, :], qA[par][0:64, :, :]).then_inc(prep_chain, 1)
                else:
                    v.tensor_copy(kA[par][64:128, :, :], kA[par][0:64, :, :]).then_inc(qk_ready, 1)

            def maximum(where, i):
                x, n = where
                dve.wait_ge(work_full[x], n)
                v.tensor_reduce(nmax[:, i:i + 1], work[x][:, :, 0:HT], op=ALU.max, axis=AX.XY, negate=True).then_inc(work_free[x], 1)

            def to_unit(last_where):
                x, n = last_where
                dve.wait_ge(work_free[x], n)
                v.tensor_scalar(nmax16[:, :], nmax[:, :], 1.0 / M_UNIT, None, ALU.mult).then_inc(nmax_ready, 1)

            spreads_before = lambda pair: min(pair, PAIRS - 2) if isinstance(pair, int) else pair

            def invert_sums(b, pair, where):
                x, n = where
                dve.wait_ge(work_free[x], n)
                dve.wait_ge(inv_spread, SPREAD * ((PAIRS - 2) * b + spreads_before(pair)))
                v.reciprocal(inv[:, :], sums[:, :]).then_inc(inverted, 1)

            def scale_output(b, pair, par, where=None):
                dve.wait_ge(av_saved, 8 * b + pair + 1)
                dve.wait_ge(o_lo_ready, 8 * b + pair)
                two = lambda t: t.rearrange("p (a n) -> p a n", a=2)
                if where:
                    x, n = where
                    dve.wait_ge(work_full[x], n)
                    v.tensor_tensor(two(o_norm[:, :]), two(o_raw[par][:, :]), work[x][:, :, 0:HT], ALU.mult).then_inc(work_free[x], 1)
                else:
                    dve.wait_ge(inv_spread, SPREAD * ((PAIRS - 2) * b + pair + 1))
                    v.tensor_tensor(two(o_norm[:, :]), two(o_raw[par][:, :]), inv_all[:, :, :], ALU.mult).then_inc(o_normed, 1)

            def o_low(b, pair):
                dve.wait_ge(o_hi_ready, 8 * b + pair + 1)
                one = lambda t: t[:, bass.ds(pair, 1), :].rearrange("p a t -> p (a t)")
                v.scalar_tensor_tensor(one(o_lo), o_norm[:, :], b_scaled[:, 2, bass.ds(pair, 1)], one(o_hi), ALU.add, ALU.subtract).then_inc(o_lo_ready, 1)

            def dve_slot(b, s, par, last):
                S = 8 * b + s
                nxt = not (last and isinstance(s, int) and s == 7)
                zero = isinstance(s, int) and s == 0
                other = 1 - par
                if nxt and not zero:
                    low_part(S + 1, n_work(b, s - 1, "Q"), 0, other, (s + 1) % 8)
                if nxt:
                    low_part(S + 1, n_work(b, s, "K", last=last), 1, other, (s + 1) % 8)
                if not nxt:
                    scale_output(b, s - 2, par)
                if nxt:
                    for i in range(10):
                        maximum(n_work(b, s, "max", i, last), i)
                        if i == 3 and has_output(s):
                            scale_output(b, s - 2, par)
                    to_unit(n_work(b, s, "max", 9, last))
                if has_output(s):
                    o_low(b, s - 2)
                if not zero:
                    invert_sums(b, s - 1, n_work(b, s, "sum", last=last))
            dve_slot.eng = dve

            def dve_tail(b, last):
                if not last:
                    low_part(8 * b + 9, n_work(b, 7, "Q"), 0, 1, 1)
                scale_output(b, 6, 0, n_tail(b, last, "inv", 6))
                o_low(b, 6)
                invert_sums(b, 7, n_tail(b, last, "sum", 0))
                scale_output(b, 7, 1, n_tail(b, last, "inv", 7))
                o_low(b, 7)
                dve.wait_ge(h_loaded, 16 * (b + 1))
                def moments(i):
                    x, n = n_tail(b, last, "O", i)
                    dve.wait_ge(work_free[x], n)
                    return v.bn_stats(bn6[:, i, :], h2[:, i, :])

                for i in range(TT):
                    x, n = n_tail(b, last, "O", i)
                    dve.wait_ge(work_full[x], n)
                    v.scalar_tensor_tensor(h2[:, i, :], work[x][:, 0, 0:D], S_OUT, h2[:, i, :], ALU.mult, ALU.add).then_inc(work_free[x], 1)
                    if i:
                        moments(i - 1)
                row_stats(B + b, moments(TT - 1))
                dve.wait_ge(work_full[0], slot_base(0, b, 0))
                normalise(xn2, lambda j: h2[:, j, :], xn2_ready)
                dve.wait_ge(xn2_ready, TT * (b + 1))
                v.tensor_reduce(xmax[:, bass.ds(b, 1)], xn2[:, :, :], op=ALU.max, axis=AX.XY, apply_absolute_value=True).then_inc(x2_max, 1)

            low_part(0, n_start("Q", 0), 0, 0, 0)
            low_part(0, n_start("K", 0), 1, 0, 0)
            for i in range(10):
                maximum(n_start("max", i), i)
            to_unit(n_start("max", 9))
            low_part(1, n_start("Q", 1), 0, 1, 1)
            dve.wait_ge(h_stored, 16 * B)
            with dve.Fori(0, B - 1) as b:
                slots(dve_slot, b, False)
                dve_tail(b, False)
            slots(dve_slot, B - 1, True)
            dve_tail(B - 1, True)

            scale_link = Ready(dve, scale_chain)

            def tensor_max(k, parts):
                for n, p in enumerate(parts):
                    ins = v.tensor_reduce(sc[:, 30 + n:31 + n], p, op=ALU.max, axis=AX.X)
                    if n < len(parts) - 1:
                        scale_link(ins, wait=False)
                ins.then_inc(red_ready, 1)
                dve.wait_ge(red_done, k + 1)
                return [sc[:, 18 + 2 * k + n:19 + 2 * k + n] for n in range(len(parts))]

            def quant_scale(top, unit, scale, mult):
                scale_link(v.tensor_scalar(S_TMP, top, unit, 1.0 / QMAX16, ALU.mult, ALU.mult))
                scale_link(v.tensor_scalar(scale, S_TMP, 1e-12, None, ALU.max))
                scale_link(v.reciprocal(S_ALL, scale))
                ins = v.tensor_scalar(mult, S_ALL, unit, None, ALU.mult)
                return ins

            dve.wait_ge(x2_max, B)
            top, = tensor_max(0, [xmax[:, :]])
            scale_link(v.tensor_scalar(S_X, top, 1.0 / QMAX16, 1e-12, ALU.mult, ALU.max))
            v.reciprocal(S_XI, S_X).then_inc(scales_ready, 1)
            dve.wait_ge(scales_ready, 1)
            for x, k in ((0, 4), (1, 3)):
                dve.wait_ge(work_free[x], n_tail(B - 1, True, "L", k)[1])

            def quantise_x(b):
                dve.wait_ge(xl_ready, b)
                v.tensor_scalar(xq[:, :], X32[:, bass.ds(b * (XB // 2), KT * T)], S_XI, None, ALU.mult).then_inc(xq_chain, 1)
                dve.wait_ge(xq_chain, b + 1)
                part = lambda hl: X[:, bass.ds(b * XB + hl * KT * T, KT * T)]
                v.tensor_copy(part(0), xq[:, :]).then_inc(xh_ready, 1)
                dve.wait_ge(xh_ready, b + 1)
                v.tensor_tensor(part(1), xq[:, :], part(0), ALU.subtract).then_inc(xl_ready, 1)

            def gate_maxima(b, fs):
                for f in fs:
                    n = FT * b + f
                    dve.wait_ge(unit_copied, 3 + n + 1)
                    v.tensor_reduce(gmax[:, bass.ds(n, 1)], G[:, f, bass.ds(b * T, T)], op=ALU.max, axis=AX.X,
                                    apply_absolute_value=True).then_inc(g_max, 1)

            dve.wait_ge(h2_stored, 16 * B)
            quantise_x(0)
            with dve.Fori(0, B - 1) as b:
                quantise_x(b + 1)
                gate_maxima(b, range(FT))
            gate_maxima(B - 1, range(FT))

            dve.wait_ge(g_max, UNITS)
            top, = tensor_max(1, [gmax[:, :]])
            scale_link(v.scalar_tensor_tensor(S_RED, pow2[:, 5:6], 1.0 / W_SCALE, S_X, ALU.mult, ALU.mult))
            quant_scale(top, S_RED, S_G, S_GM).then_inc(scales_ready, 1)

            dve.sem_inc(p_ready, 2)
            dve.sem_inc(u_max, 3)
            with dve.Fori(0, B) as b:
                for f in range(FT):
                    n = FT * b + f
                    dve.wait_ge(sg_ready, n + 1)
                    dve.wait_ge(sq_ready, n + 1)
                    g = G[:, f, bass.ds(b * T, T)]
                    v.tensor_tensor(g, gq[f % 2][:, :], sq[f % 2][:, :], ALU.mult).then_inc(p_ready, 1)
                    dve.wait_ge(unit_copied, 3 + UNITS + n + 1)
                    v.tensor_reduce(umax[:, bass.ds(n, 1)], ubuf[f % 3][:, :], op=ALU.max, axis=AX.X, apply_absolute_value=True).then_inc(u_max, 1)
                    dve.wait_ge(p_ready, n + 3)
                    v.tensor_reduce(pmax[:, bass.ds(n, 1)], g, op=ALU.max, axis=AX.X, apply_absolute_value=True).then_inc(p_max, 1)
            dve.wait_ge(p_max, UNITS)
            dve.wait_ge(u_max, 3 + UNITS)
            u_top, p_top = tensor_max(2, [umax[:, :], pmax[:, :]])
            scale_link(v.scalar_tensor_tensor(S_RED, pow2[:, 4:5], 1.0 / W_SCALE, S_X, ALU.mult, ALU.mult))
            scale_link(quant_scale(u_top, S_RED, S_U, S_UM))
            scale_link(v.tensor_scalar(S_RED, S_G, 1.0 / 65536, None, ALU.mult))
            quant_scale(p_top, S_RED, S_T, S_TM).then_inc(scales_ready, 1)

            dve.sem_inc(t_ready, 2)
            with dve.Fori(0, NG // 2) as c:
                for k in range(2):
                    n = 2 * c + k
                    dve.wait_ge(tq_ready, n + 1)
                    dve.wait_ge(uq_ready, n + 1)
                    v.tensor_tensor(Gf[:, bass.ds(n * GC, GC)], tq[k][:, :], uq[k][:, :], ALU.mult).then_inc(t_ready, 1)
                for k in range(2):
                    n = 2 * c + k
                    dve.wait_ge(t_ready, n + 3)
                    v.tensor_reduce(omax[:, bass.ds(n, 1)], Gf[:, bass.ds(n * GC, GC)], op=ALU.max, axis=AX.X, apply_absolute_value=True).then_inc(t_max, 1)
            dve.wait_ge(t_max, NG)
            top, = tensor_max(3, [omax[:, :]])
            scale_link(v.tensor_scalar(S_RED, S_T, S_U, None, ALU.mult))
            scale_link(quant_scale(top, S_RED, S_O, S_OM))
            v.scalar_tensor_tensor(S_Y, pow2[:, 6:7], 1.0 / W_SCALE, S_O, ALU.mult, ALU.mult).then_inc(scales_ready, 1)
            dve.wait_ge(scales_ready, 4)

            def quantise_o(n, k):
                dve.wait_ge(ol_ready, n)
                dve.wait_ge(y_done, DT * n)
                v.tensor_scalar(oq[:, :, :], G[:, :, bass.ds(n * DT * 128, DT * 128)], S_OM, None, ALU.mult).then_inc(oq_ready, 1)
                dve.wait_ge(oq_ready, n + 1)
                v.tensor_copy(oh[k][:, :, :], oq[:, :, :]).then_inc(oh_ready, 1)
                dve.wait_ge(oh_ready, n + 1)
                v.tensor_tensor(ol[k][:, :, :], oq[:, :, :], oh[k][:, :, :], ALU.subtract).then_inc(ol_ready, 1)

            def results(n, c, k):
                dve.wait_ge(hin_loaded[k], 16 * (c + 1))
                dve.wait_ge(out_stored[k], 16 * c)
                for j in range(DT):
                    dve.wait_ge(y_done, DT * (n + 1) + j + 1)
                    v.scalar_tensor_tensor(yout[k][:, j, :], ps[:, 4 * k + j, 0:D], S_Y, hin[k][:, j, :], ALU.mult, ALU.add).then_inc(y_ready, 1)

            dve.sem_inc(y_ready, DT)
            quantise_o(0, 0)
            with dve.Fori(0, ND // 2 - 1) as c:
                for k in range(2):
                    quantise_o(2 * c + k + 1, 1 - k)
                    results(2 * c + k, c, k)
            quantise_o(ND - 1, 1)
            results(ND - 2, ND // 2 - 1, 0)
            results(ND - 1, ND // 2 - 1, 1)


def kernel(**inputs):
    import numpy as np
    import concourse.bacc as bacc
    from concourse.bass_utils import run_bass_kernel_spmd

    n = {k: np.asarray(v) for k, v in inputs.items()}
    pairs = lambda b: b.reshape(PAIRS, 128).T
    arrays = {
        "x_t": n["x"].reshape(B, T_IMG // 128, 128, KT, 128, DC).transpose(0, 1, 4, 3, 5, 2),
        "txt": n["txt"],
        "tok_ws_t": n["L0_tok_weighted_sum"].T,
        "tok_w_t": n["L0_tok_weight"].T,
        "wq_t": n["L0_attn_W_Q"].reshape(HD, D).T,
        "wk_t": n["L0_attn_W_K"].reshape(HD, D).T,
        "wv_t": n["L0_attn_W_V"].reshape(HD, D).T,
        "wo_t": n["L0_attn_W_O"].transpose(0, 2, 1).reshape(HD, D),
        "bq": pairs(n["L0_attn_b_Q"]),
        "bk": pairs(n["L0_attn_b_K"]),
        "bv": pairs(n["L0_attn_b_V"]),
        "bo": n["L0_attn_b_O"],
        "w_up": n["L0_ffn_w_up"],
        "w_gate": n["L0_ffn_w_gate"],
        "w_down": n["L0_ffn_w_down"],
    }
    arrays = {k: np.ascontiguousarray(v) for k, v in arrays.items()}
    nc = bacc.Bacc("TRN2", target_bir_lowering=False, num_devices=1)
    args = [nc.dram_tensor(k, v.shape, mybir.dt.from_np(v.dtype), kind="ExternalInput").ap() for k, v in arrays.items()]
    out = nc.dram_tensor("out", (B, T, D), F32, kind="ExternalOutput").ap()
    build(nc, *args, out)
    r = run_bass_kernel_spmd(nc, [arrays], core_ids=[0])
    return r.results[0]["out"]
```
